# Optimizing a Trainium2 kernel written in Bass

```python
import numpy as np
import jax
import jax.numpy as jnp

def _softmax(x, axis=-1):
    return jax.nn.softmax(x, axis=axis)

def _gelu(x):
    return jax.nn.gelu(x, approximate=True)

def _silu(x):
    return jax.nn.silu(x)

def _sigmoid(x):
    return jax.nn.sigmoid(x)

def _layernorm(x, axis=-1, eps=1e-05):
    m = jnp.mean(x, axis=axis, keepdims=True)
    v = jnp.var(x, axis=axis, keepdims=True)
    return (x - m) / jnp.sqrt(v + eps)

def _scatter_add(tgt, idx, src, axis=0):
    return tgt.at[idx].add(src)

def _segment_sum(src, seg, n):
    return jax.ops.segment_sum(src, seg, n)
kernel_name = 'mk_xattn_ffn_d2_seqx_r8_7a8386'

def setup_inputs(seed: int=0):
    np.random.seed(seed)
    _w = jnp.asarray

    def _rec_inputs():
        import jax
        import jax.numpy as jnp
        _rk = jax.random.key(seed)
        x = -0.0002928 + 1 * jax.random.normal(jax.random.fold_in(_rk, 1), (8, 128, 128), jnp.float32)
        _lenS = 128 - jax.random.randint(jax.random.fold_in(_rk, 7), (8,), 0, max(1, 128 // 4) + 1, jnp.int32)
        _lenS2 = 128 - jax.random.randint(jax.random.fold_in(_rk, 8), (8,), 0, max(1, 128 // 4) + 1, jnp.int32)
        _ctx_768P = jax.random.normal(jax.random.fold_in(_rk, 11), (8, 16, 96), jnp.float32)
        _ctx_768c = jax.random.dirichlet(jax.random.fold_in(_rk, 511), 0.3 * jnp.ones((16,), jnp.float32), (8, 128))
        _ctx_768t = jnp.einsum('bsk,bkd->bsd', _ctx_768c, _ctx_768P)
        _ctx_768t = _ctx_768t * jax.lax.rsqrt(jnp.mean(jnp.square(_ctx_768t)) + 1e-12) * 0.953939
        ctx_768 = 2.09791e-05 + 1.00001 * (_ctx_768t + 0.3 * jax.random.normal(jax.random.fold_in(_rk, 611), (8, 128, 96), jnp.float32))
        return (x, ctx_768)
    x, ctx_768 = _rec_inputs()

    def _L0_xattn_setup():
        import jax, jax.numpy as jnp
        import numpy as np
        H = 8
        D = 64
        SCALE = D ** (-0.5)
        key = jax.random.key(seed)
        ks = jax.random.split(key, 7)
        B, Nq, Nkv = (2, 256, 256)
        Cq, Ck, I = (128, 96, H * D)
        return {'x': jax.random.normal(ks[0], (B, Nq, Cq), jnp.float32), 'context': jax.random.normal(ks[1], (B, Nkv, Ck), jnp.float32), 'Wq': jax.random.normal(ks[2], (Cq, I), jnp.float32) * Cq ** (-0.5), 'Wk': jax.random.normal(ks[3], (Ck, I), jnp.float32) * Ck ** (-0.5), 'Wv': jax.random.normal(ks[4], (Ck, I), jnp.float32) * Ck ** (-0.5), 'Wo': jax.random.normal(ks[5], (I, Cq), jnp.float32) * I ** (-0.5), 'bo': jnp.zeros((Cq,), jnp.float32)}
    _L0_xattn_all = _L0_xattn_setup()
    _L0_xattn_in = {k: v for k, v in _L0_xattn_all.items() if k in ('Wq', 'Wk', 'Wv', 'Wo', 'bo')}
    del _L0_xattn_all

    def _L0_ffn_setup():
        import jax, jax.numpy as jnp
        import numpy as np
        E = 8
        TOP_K = 2
        DIM = 128
        HID = 256
        key = jax.random.key(seed)
        k1, k2, k3, k4, k5 = jax.random.split(key, 5)
        s = 0.02
        x = jax.random.normal(k1, (2, 256, DIM), dtype=jnp.float32)
        Wg = jax.random.normal(k2, (DIM, E), dtype=jnp.float32) * s
        W1 = jax.random.normal(k3, (E, DIM, HID), dtype=jnp.float32) * s
        W2 = jax.random.normal(k4, (E, DIM, HID), dtype=jnp.float32) * s
        W3 = jax.random.normal(k5, (E, HID, DIM), dtype=jnp.float32) * s
        return {'x': x, 'Wg': Wg, 'W1': W1, 'W2': W2, 'W3': W3}
    _L0_ffn_all = _L0_ffn_setup()
    _L0_ffn_in = {k: v for k, v in _L0_ffn_all.items() if k in ('Wg', 'W1', 'W2', 'W3')}
    del _L0_ffn_all

    def _L1_xattn_setup():
        import jax, jax.numpy as jnp
        import numpy as np
        N_HEADS = 16
        D_EMBED = 128
        N_CROSS = 96
        D_HEAD = D_EMBED // N_HEADS
        key = jax.random.key(seed)
        ks = jax.random.split(key, 10)
        B, S = (2, 256)
        x = jax.random.normal(ks[0], (B, S, D_EMBED), dtype=jnp.float32)
        context = jax.random.normal(ks[1], (B, S, N_CROSS), dtype=jnp.float32)
        sq = 1.0 / np.sqrt(D_EMBED)
        sc = 1.0 / np.sqrt(N_CROSS)
        Wq = jax.random.normal(ks[2], (D_EMBED, D_EMBED), dtype=jnp.float32) * sq
        bq = jnp.zeros((D_EMBED,), dtype=jnp.float32)
        Wk = jax.random.normal(ks[3], (N_CROSS, D_EMBED), dtype=jnp.float32) * sc
        bk = jnp.zeros((D_EMBED,), dtype=jnp.float32)
        Wv = jax.random.normal(ks[4], (N_CROSS, D_EMBED), dtype=jnp.float32) * sc
        bv = jnp.zeros((D_EMBED,), dtype=jnp.float32)
        Wo = jax.random.normal(ks[5], (D_EMBED, D_EMBED), dtype=jnp.float32) * sq
        bo = jnp.zeros((D_EMBED,), dtype=jnp.float32)
        return {'x': x, 'context': context, 'Wq': Wq, 'bq': bq, 'Wk': Wk, 'bk': bk, 'Wv': Wv, 'bv': bv, 'Wo': Wo, 'bo': bo}
    _L1_xattn_all = _L1_xattn_setup()
    _L1_xattn_in = {k: v for k, v in _L1_xattn_all.items() if k in ('Wq', 'bq', 'Wk', 'bk', 'Wv', 'bv', 'Wo', 'bo')}
    del _L1_xattn_all

    def _L1_ffn_setup():
        import jax, jax.numpy as jnp
        import numpy as np
        import math
        D_IN = 128
        FEATURES = (512, 512, 128)
        BATCH, SEQ = (8, 256)

        def _conn_dense(kernel_bool, x):
            w = jnp.where(kernel_bool, jnp.float32(1.0), jnp.float32(-1.0))
            return x @ w
        key = jax.random.key(seed)
        kx, kk0, kk1, kk2 = jax.random.split(key, 4)
        x = jax.random.normal(kx, (BATCH, SEQ, D_IN), dtype=jnp.float32)
        k0 = jax.random.randint(kk0, (2 * D_IN, FEATURES[0]), 0, 2).astype(jnp.bool_)
        k1 = jax.random.randint(kk1, (FEATURES[0], FEATURES[1]), 0, 2).astype(jnp.bool_)
        k2 = jax.random.randint(kk2, (FEATURES[1], FEATURES[2]), 0, 2).astype(jnp.bool_)
        s0 = jnp.asarray(1.0 / math.sqrt(2 * D_IN), dtype=jnp.float32)
        s1 = jnp.asarray(1.0 / math.sqrt(FEATURES[0]), dtype=jnp.float32)
        s2 = jnp.asarray(1.0 / math.sqrt(FEATURES[1]), dtype=jnp.float32)
        return {'x': x, 'k0': k0, 'k1': k1, 'k2': k2, 's0': s0, 's1': s1, 's2': s2}
    _L1_ffn_all = _L1_ffn_setup()
    _L1_ffn_in = {k: v for k, v in _L1_ffn_all.items() if k in ('k0', 'k1', 'k2', 's0', 's1', 's2')}
    del _L1_ffn_all
    return {'x': x, 'ctx_768': ctx_768, 'L0_xattn_Wq': _L0_xattn_in['Wq'], 'L0_xattn_Wk': _L0_xattn_in['Wk'], 'L0_xattn_Wv': _L0_xattn_in['Wv'], 'L0_xattn_Wo': _L0_xattn_in['Wo'], 'L0_xattn_bo': _L0_xattn_in['bo'], 'L0_ffn_Wg': _L0_ffn_in['Wg'], 'L0_ffn_W1': _L0_ffn_in['W1'], 'L0_ffn_W2': _L0_ffn_in['W2'], 'L0_ffn_W3': _L0_ffn_in['W3'], 'L1_xattn_Wq': _L1_xattn_in['Wq'], 'L1_xattn_bq': _L1_xattn_in['bq'], 'L1_xattn_Wk': _L1_xattn_in['Wk'], 'L1_xattn_bk': _L1_xattn_in['bk'], 'L1_xattn_Wv': _L1_xattn_in['Wv'], 'L1_xattn_bv': _L1_xattn_in['bv'], 'L1_xattn_Wo': _L1_xattn_in['Wo'], 'L1_xattn_bo': _L1_xattn_in['bo'], 'L1_ffn_k0': _L1_ffn_in['k0'], 'L1_ffn_k1': _L1_ffn_in['k1'], 'L1_ffn_k2': _L1_ffn_in['k2'], 'L1_ffn_s0': _L1_ffn_in['s0'], 'L1_ffn_s1': _L1_ffn_in['s1'], 'L1_ffn_s2': _L1_ffn_in['s2']}

def reference(x, ctx_768, L0_xattn_Wq, L0_xattn_Wk, L0_xattn_Wv, L0_xattn_Wo, L0_xattn_bo, L0_ffn_Wg, L0_ffn_W1, L0_ffn_W2, L0_ffn_W3, L1_xattn_Wq, L1_xattn_bq, L1_xattn_Wk, L1_xattn_bk, L1_xattn_Wv, L1_xattn_bv, L1_xattn_Wo, L1_xattn_bo, L1_ffn_k0, L1_ffn_k1, L1_ffn_k2, L1_ffn_s0, L1_ffn_s1, L1_ffn_s2):
    import jax
    import jax.numpy as jnp

    def _L0_xattn_ref(x, context, Wq, Wk, Wv, Wo, bo):
        import jax, jax.numpy as jnp
        import numpy as np
        H = 8
        D = 64
        SCALE = D ** (-0.5)
        B, Nq, _ = x.shape
        Nkv = context.shape[1]
        q = (x @ Wq).reshape(B, Nq, H, D)
        k = (context @ Wk).reshape(B, Nkv, H, D)
        v = (context @ Wv).reshape(B, Nkv, H, D)
        sim = jnp.einsum('bihd,bjhd->bhij', q, k) * SCALE
        attn = jax.nn.softmax(sim, axis=-1)
        out = jnp.einsum('bhij,bjhd->bihd', attn, v).reshape(B, Nq, H * D)
        return out @ Wo + bo

    def _L0_ffn_ref(x, Wg, W1, W2, W3):
        import jax, jax.numpy as jnp
        import numpy as np
        E = 8
        TOP_K = 2
        DIM = 128
        HID = 256
        B, T, C = x.shape
        xf = x.reshape(-1, C)
        logits = xf @ Wg
        top_w, top_i = jax.lax.top_k(logits, TOP_K)
        top_w = jax.nn.softmax(top_w, axis=-1)
        one_hot = jax.nn.one_hot(top_i, E, dtype=xf.dtype)
        combine = jnp.einsum('nk,nke->ne', top_w, one_hot)
        h = jnp.einsum('nc,ech->enh', xf, W1)
        g = jnp.einsum('nc,ech->enh', xf, W2)
        y = jnp.einsum('enh,ehc->enc', jax.nn.silu(h) * g, W3)
        out = jnp.einsum('enc,ne->nc', y, combine)
        return out.reshape(B, T, C)

    def _L1_xattn_ref(x, context, Wq, bq, Wk, bk, Wv, bv, Wo, bo):
        import jax, jax.numpy as jnp
        import numpy as np
        N_HEADS = 16
        D_EMBED = 128
        N_CROSS = 96
        D_HEAD = D_EMBED // N_HEADS
        B, S, _ = x.shape

        def split_heads(t):
            return t.reshape(B, S, N_HEADS, D_HEAD).transpose(0, 2, 1, 3)
        q = split_heads(x @ Wq + bq)
        k = split_heads(context @ Wk + bk)
        v = split_heads(context @ Wv + bv)
        scale = 1.0 / np.sqrt(D_HEAD)
        scores = jnp.einsum('bhqd,bhkd->bhqk', q, k) * scale
        attn = jax.nn.softmax(scores, axis=-1)
        out = jnp.einsum('bhqk,bhkd->bhqd', attn, v)
        out = out.transpose(0, 2, 1, 3).reshape(B, S, D_EMBED)
        return out @ Wo + bo

    def _L1_ffn_ref(x, k0, k1, k2, s0, s1, s2):
        import jax, jax.numpy as jnp
        import numpy as np
        import math
        D_IN = 128
        FEATURES = (512, 512, 128)
        BATCH, SEQ = (8, 256)

        def _conn_dense(kernel_bool, x):
            w = jnp.where(kernel_bool, jnp.float32(1.0), jnp.float32(-1.0))
            return x @ w
        h = jnp.concatenate([x, -x], axis=-1)
        h = s0 * _conn_dense(k0, h)
        h = jax.nn.relu(h) * 2
        h = s1 * _conn_dense(k1, h)
        h = jax.nn.relu(h) * 2
        h = s2 * _conn_dense(k2, h)
        return h
    x = x + _L0_xattn_ref(_layernorm(x, axis=-1), ctx_768, L0_xattn_Wq, L0_xattn_Wk, L0_xattn_Wv, L0_xattn_Wo, L0_xattn_bo)
    x = x + _L0_ffn_ref(_layernorm(x, axis=-1), L0_ffn_Wg, L0_ffn_W1, L0_ffn_W2, L0_ffn_W3)
    x = x + _L1_xattn_ref(_layernorm(x, axis=-1), ctx_768, L1_xattn_Wq, L1_xattn_bq, L1_xattn_Wk, L1_xattn_bk, L1_xattn_Wv, L1_xattn_bv, L1_xattn_Wo, L1_xattn_bo)
    x = x + _L1_ffn_ref(_layernorm(x, axis=-1), L1_ffn_k0, L1_ffn_k1, L1_ffn_k2, L1_ffn_s0, L1_ffn_s1, L1_ffn_s2)
    return x

_drawn_inputs = setup_inputs


def setup_inputs(seed=0):
    import zlib

    import numpy as np

    out = dict(_drawn_inputs(seed))
    spreads = {'L0_xattn_bo': (0.0, 0.1),
     'L1_xattn_bq': (0.0, 1.662),
     'L1_xattn_bk': (0.0, 2.0),
     'L1_xattn_bv': (0.0, 0.366),
     'L1_xattn_bo': (0.0, 0.363)}
    factors = {'L0_ffn_Wg': 8.0, 'L0_ffn_W1': 8.0, 'L0_ffn_W2': 8.0, 'L0_ffn_W3': 8.0}
    for name, (base, spread) in spreads.items():
        noise = np.random.default_rng([zlib.crc32(name.encode()), seed]).standard_normal(out[name].shape)
        drawn = base * np.exp(spread * noise) if base else spread * noise
        out[name] = jnp.asarray(drawn.astype(out[name].dtype))
    for name, factor in factors.items():
        out[name] = (out[name] * factor).astype(out[name].dtype)
    return out
```

```python
from contextlib import ExitStack

import concourse.bass as bass
from concourse import mybir

F32 = mybir.dt.float32
F32R = mybir.dt.float32r
I32 = mybir.dt.int32
U32 = mybir.dt.uint32
U8 = mybir.dt.uint8
ALU = mybir.AluOpType
ACT = mybir.ActivationFunctionType
X = mybir.AxisListType.X

P = 128
NB = 8
NP = NB // 2
TG = 512
NT = NB * P // TG
C = 128
CK = 96
CK1 = CK + 1
H0, D0 = 8, 64
I0 = H0 * D0
NC0 = I0 // P
E = 8
HID = 256
NH = HID // P
H1, D1 = 16, 8
NG = 4
NS = 4
F1, F2 = 512, 512
EPS = 1e-5
RSQRT_SEED = 0x5F3759DF


def f32(ap):
    return ap.bitcast(F32)


def program(nc, a, out):
    with ExitStack() as ctx:
        def sb(name, shape, dt=F32):
            return ctx.enter_context(nc.sbuf_tensor(name, shape, dt))

        def sem(name):
            return ctx.enter_context(nc.semaphore(name))

        x_sb = sb("x_sb", [P, NB, C])
        ctx_sb = sb("ctx_sb", [P, NB, CK])
        ident = sb("ident", [P, P])
        ones = sb("ones", [P, P])
        zero = sb("zero", [P, 1])
        ctxT = sb("ctxT", [CK1, NB * P])
        ctxT_hi = sb("ctxT_hi", [CK1, NB * P], F32R)
        ctxT_lo = sb("ctxT_lo", [CK1, NB * P], F32R)
        stats = sb("stats", [P, NB, 6])
        meanvar = sb("meanvar", [P, NB, 2])
        ve = sb("ve", [P, NB])
        rs = sb("rs", [P, NB])
        nt = sb("nt", [P, NB])
        nu = sb("nu", [P, NB])
        nm = sb("nm", [P, NB])
        xn = sb("xn", [P, NB, C])
        xT_hi = sb("xT_hi", [P, NB * P], F32R)
        xT_lo = sb("xT_lo", [P, NB * P], F32R)

        w_raw = sb("w_raw", [P, 2, I0])
        wq0, wk0, w12 = w_raw[:, 0, :], w_raw[0:CK, 1, :], w_raw
        wq0_hi = sb("wq0_hi", [C, I0], F32R)
        wq0_lo = sb("wq0_lo", [C, I0], F32R)
        wk0_hi = sb("wk0_hi", [CK1, I0], F32R)
        wk0_lo = sb("wk0_lo", [CK1, I0], F32R)
        wv0 = sb("wv0", [CK, I0])
        wo0 = sb("wo0", [P, NC0, C])
        bo0 = sb("bo0", [P, C])
        kT0 = sb("kT0", [P, NC0, NB * P])
        v0 = sb("v0", [P, NB, I0])
        q_ev = sb("q_ev", [P, NC0, 2 * P])
        q_od = sb("q_od", [P, NC0, 2 * P])
        probs = sb("probs", [P, 2, H0, P])
        probsT = sb("probsT", [P, 2, H0, P])
        negmax = sb("negmax", [P, 2, H0])
        sums = sb("sums", [P, 2, H0])
        rsum = sb("rsum", [P, 2, H0])
        o_sb = sb("o_sb", [P, 2, I0])
        oT = sb("oT", [P, 2, I0])

        wg = sb("wg", [C, E])
        lg = sb("lg", [P, NB, E])
        top = sb("top", [P, NB, 8])
        topi = sb("topi", [P, NB, 8], U32)
        topf = sb("topf", [P, NB, 8])
        iota_e = sb("iota_e", [P, NB, E])
        gd = sb("gd", [P, NB])
        ge = sb("ge", [P, NB])
        gs = sb("gs", [P, NB])
        gw = sb("gw", [P, 2, NB])
        pick = sb("pick", [P, 2, NB, E])
        picked = sb("picked", [P, 2, NB, E])
        comb = sb("comb", [P, E, NB])
        w12_hi = sb("w12_hi", [P, 2, 2 * HID], F32R)
        w12_lo = sb("w12_lo", [P, 2, 2 * HID], F32R)
        w3 = sb("w3", [P, 2, NH, C])

        wq1 = sb("wq1", [C, C])
        wq1_hi, wq1_lo = wq0_hi, wq0_lo
        wk1 = sb("wk1", [CK1, C])
        wk1_hi, wk1_lo = wk0_hi, wk0_lo
        wv1 = sb("wv1", [CK1, C])
        wo1 = sb("wo1", [C, C])
        bo1 = sb("bo1", [P, C])
        bq1 = sb("bq1", [2, C])
        bq1_r = sb("bq1_r", [2, C], F32R)
        bq1_p = sb("bq1_p", [2, C])
        bq1_s = sb("bq1_s", [2, NS * C], F32R)
        ones_r = sb("ones_r", [2, 2 * P], F32R)
        block_of = sb("block_of", [P, 4])
        row_i = sb("row_i", [P, 1], I32)
        bit_i = sb("bit_i", [P, 3], I32)
        is_lo = sb("is_lo", [P, 3])
        sign = sb("sign", [P, 3])
        part = sb("part", [P, 2, TG], F32R)
        k_st = sb("k_st", [P, NG, NB * P], F32R)
        k_bd = sb("k_bd", [P, 2, NG, 4, P], F32R)
        q_st = sb("q_st", [P, NG, 2 * P], F32R)
        negmax1 = sb("negmax1", [P, 2, 8])
        rsum1 = sb("rsum1", [P, H1])
        o1 = sb("o1", [P, C])
        o1T = sb("o1T", [P, C])

        k0_i = sb("k0_i", [P, 2, F1 // 4], I32)
        k1_i = sb("k1_i", [P, F1 // P, F2 // 4], I32)
        k2_i = sb("k2_i", [P, F2 // P, C // 4], I32)
        k0_u, k1_u, k2_u = (k[:, :, :].bitcast(U8) for k in (k0_i, k1_i, k2_i))
        d0_w = sb("d0_w", [P, F1], F32R)
        d1_w = sb("d1_w", [P, F1 // P, F2], F32R)
        d2_w = sb("d2_w", [P, F2 // P, C], F32R)
        scale = sb("scale", [P, 3])
        scale2 = sb("scale2", [P, 3])
        h_c = sb("h_c", [P, 2, F1 // P, TG], F32R)

        uT = kT0[:, 0:2, :].rearrange("p t (c n) -> p t c n", c=NH)
        silu = kT0[:, 2, :].rearrange("p (c n) -> p c n", c=NH)
        relu = silu
        xT = kT0[:, 3, :]
        v1 = v0[:, :, 0:H1 * (D1 + 1)].rearrange("p b (h d) -> p b h d", d=D1 + 1)
        sh1 = probs[:, :, :, :].rearrange("p j h k -> p j (h k)")
        sh1T = probsT[:, :, :, :].rearrange("p j h k -> p j (h k)")
        h_a = k_bd[:, :, :, :, :].rearrange("p s g h k -> p s g (h k)")
        h_b = k_st[:, :, :].rearrange("p (s g) (u n) -> p s (g u) n", s=2, u=2)
        h_at = {(0, 0): h_a, (0, 1): h_b, (1, 0): h_c, (1, 1): h_a}
        yT = oT[:, :, :]
        fin = o_sb[:, :, :]

        ps = ctx.enter_context(nc.psum_tensor("ps", [P, 8, 512], F32))
        M0 = 6

        ld_x, ld_ctx, ld_w0, ld_w1, ld_d = (sem(n) for n in ("ld_x", "ld_ctx", "ld_w0", "ld_w1", "ld_d"))
        ld_e = [sem("ld_e0"), sem("ld_e1")]
        stored = sem("stored")
        const_ok, zeros_ok, split_w0, split_w1, masks = (sem(n) for n in (
            "const_ok", "zeros_ok", "split_w0", "split_w1", "masks"))
        pool_step = sem("pool_step")
        ctxT_ps, ctxT_f, ctxT_h, ctxT_ok = (sem(n) for n in ("ctxT_ps", "ctxT_f", "ctxT_h", "ctxT_ok"))
        k0_ps, k0_ok, v0_ps, v0_ok = (sem(n) for n in ("k0_ps", "k0_ok", "v0_ps", "v0_ok"))
        ln_st, ln_mv, ln_nw, ln_rs, ln_xn, ln_ps, ln_hi, ln_lo, ln_f = (sem(n) for n in (
            "ln_st", "ln_mv", "ln_nw", "ln_rs", "ln_xn", "ln_ps", "ln_hi", "ln_lo", "ln_f"))
        xb0, xb1 = sem("xb0"), sem("xb1")
        a_q_ps, a_qe, a_qo, a_s, a_max, a_exp, a_pt_ps, a_pt_v, a_pt_a, a_o, a_rs, a_norm, a_oT_ps, a_oT, a_wo, a_x = (
            sem("a_" + n) for n in ("q_ps", "qe", "qo", "s", "max", "exp", "pt_ps", "pt_v", "pt_a", "o", "rs", "norm",
                                    "oT_ps", "oT", "wo", "x"))
        g_ps, g_lg, g_top, g_idx, g_f, g_d, g_e, g_s, g_w, g_pick, g_sel, g_ok = (
            sem("g_" + n) for n in ("ps", "lg", "top", "idx", "f", "d", "e", "s", "w", "pick", "sel", "ok"))
        b_hi, b_lo, b_h, b_g, b_silu, b_u, b_y, b_acc = (
            sem("b_" + n) for n in ("hi", "lo", "h", "g", "silu", "u", "y", "acc"))
        k1_ps, k1_part, k1_st, k1_bd, v1_ps, v1_ok = (
            sem(n) for n in ("k1_ps", "k1_part", "k1_st", "k1_bd", "v1_ps", "v1_ok"))
        c_q_ps, c_part, c_q, c_s, c_max, c_sub, c_exp, c_pt_ps, c_pt, c_o, c_rs, c_norm, c_oT_ps, c_oT, c_wo, c_x = (
            sem("c_" + n) for n in ("q_ps", "part", "q", "s", "max", "sub", "exp", "pt_ps", "pt", "o", "rs", "norm",
                                    "oT_ps", "oT", "wo", "x"))
        d_w, d_ps, d_relu, d_hi, d_lo, d_y, d_yT_ps, d_x = (
            sem("d_" + n) for n in ("w", "ps", "relu", "hi", "lo", "y", "yT_ps", "x"))

        A = a
        def stacked(ap):
            return ap[:, :].rearrange("c (h p d) -> c h p d", p=NS, d=D1)

        def repeated(ap):
            return ap[:, :].rearrange("c (h d) -> c h d", d=D1).unsqueeze(2).to_broadcast([ap.shape[0], H1, NS, D1])

        def row(ap, n):
            return ap.rearrange("(o c) -> o c", o=1).to_broadcast([n, ap.shape[0]])

        block = ctx.enter_context(nc.Block())

        @block.sync
        def _(sp):
            sp.dma_start(ctx_sb[:, :, :], A["ctx_768"].rearrange("b t c -> t b c")).then_inc(ld_ctx, 16)
            sp.dma_start(x_sb[:, :, :], A["x"].rearrange("b t c -> t b c")).then_inc(ld_x, 16)
            for dst, src in ((wk0, A["L0_xattn_Wk"]), (wq0, A["L0_xattn_Wq"]), (wv0[:, :], A["L0_xattn_Wv"]),
                             (wo0[:, :, :], A["L0_xattn_Wo"].rearrange("(k p) c -> p k c", p=P)),
                             (bo0[:, :], row(A["L0_xattn_bo"], P)), (wg[:, :], A["L0_ffn_Wg"])):
                sp.dma_start(dst, src).then_inc(ld_w0, 16)
            for dst, src in ((wq1[:, :], A["L1_xattn_Wq"]), (wk1[0:CK, :], A["L1_xattn_Wk"]),
                             (wk1[CK:CK1, :], row(A["L1_xattn_bk"], 1)), (wv1[0:CK, :], A["L1_xattn_Wv"]),
                             (wv1[CK:CK1, :], row(A["L1_xattn_bv"], 1)), (bq1[:, :], row(A["L1_xattn_bq"], 2)),
                             (wo1[:, :], A["L1_xattn_Wo"]), (bo1[:, :], row(A["L1_xattn_bo"], P))):
                sp.dma_start(dst, src).then_inc(ld_w1, 16)
            for dst, src in ((k0_i[:, :, :], A["L1_ffn_k0"].rearrange("(k p) c -> p k c", p=P)),
                             (k1_i[:, :, :], A["L1_ffn_k1"].rearrange("(k p) c -> p k c", p=P)),
                             (k2_i[:, :, :], A["L1_ffn_k2"].rearrange("(k p) c -> p k c", p=P)),
                             (scale[:, 0:1], row(A["L1_ffn_s0"], P)), (scale[:, 1:2], row(A["L1_ffn_s1"], P)),
                             (scale[:, 2:3], row(A["L1_ffn_s2"], P))):
                sp.dma_start(dst, src).then_inc(ld_d, 16)

            def load_expert(e, buf):
                sp.dma_start(w12[:, buf, 0:HID], A["L0_ffn_W1"][bass.ds(e, 1)].rearrange("o p h -> p (o h)")).then_inc(ld_e[buf], 16)
                sp.dma_start(w12[:, buf, HID:2 * HID], A["L0_ffn_W2"][bass.ds(e, 1)].rearrange("o p h -> p (o h)")).then_inc(ld_e[buf], 16)
                sp.dma_start(w3[:, buf, :, :], A["L0_ffn_W3"][bass.ds(e, 1)].rearrange("o (k p) c -> p (o k) c", p=P)).then_inc(ld_e[buf], 16)

            sp.wait_ge(split_w0, 2)
            load_expert(0, 0)
            load_expert(1, 1)
            with sp.Fori(1, E // 2) as i:
                for buf in range(2):
                    sp.wait_ge(b_y, i * 4 + (2 * buf - 2))
                    load_expert(i * 2 + buf, buf)
            for t in range(NT):
                sp.wait_ge(d_x, t + 1)
                sp.dma_start(out[t * 4:t * 4 + 4].rearrange("b t c -> t b c"),
                             fin[:, t, :].rearrange("p (b c) -> p b c", c=C)).then_inc(stored, 16)
            sp.wait_ge(stored, 16 * NT)

        @block.gpsimd
        def _(pool):
            step = [0]

            def chain(ins):
                step[0] += 1
                ins.then_inc(pool_step, 1)
                pool.wait_ge(pool_step, step[0])

            pool.memset(ones[:, :], 1.0).then_inc(const_ok, 1)
            chain(pool.memset(ident[:, :], 0.0))
            chain(pool.memset(zero[:, :], 0.0))
            pool.affine_select(out=ident[:, :], in_=ident[:, :], compare_op=ALU.not_equal, fill=1.0, base=0,
                               pattern=[[-1, P]], channel_multiplier=1).then_inc(const_ok, 1)
            pool.memset(q_ev[:, :, :], 0.0).then_inc(zeros_ok, 1)
            pool.memset(q_od[:, :, :], 0.0).then_inc(zeros_ok, 1)
            pool.wait_ge(ld_w0, 16 * 6)
            for w, hi, lo in ((wk0, wk0_hi, wk0_lo), (wq0, wq0_hi, wq0_lo)):
                rows = w.shape[0]
                chain(pool.tensor_copy(hi[0:rows, :], w))
                pool.tensor_tensor(lo[0:rows, :], w, f32(hi[0:rows, :]), ALU.subtract).then_inc(split_w0, 1)
            pool.wait_ge(ld_x, 16)
            for b in range(NB):
                pool.wait_ge(ln_xn, b + 1)
                pool.tensor_tensor(x_sb[:, b, :], x_sb[:, b, :], bo0[:, :], ALU.add).then_inc(xb0, 1)
            chain(pool.iota(iota_e[:, :, :], [[0, NB], [1, E]], base=0, channel_multiplier=0,
                            allow_small_or_imprecise_dtypes=True))
            pool.iota(row_i[:, :], [[0, 1]], base=0, channel_multiplier=1).then_inc(const_ok, 1)
            pool.wait_ge(ld_w1, 16 * 8)
            def split_repeated(w, hi, lo):
                chain(pool.tensor_copy(stacked(hi), repeated(w)))
                pool.tensor_tensor(stacked(lo), repeated(w), stacked(f32(hi)), ALU.subtract).then_inc(split_w1, 1)

            pool.wait_ge(k0_ps, NC0 * NT)
            split_repeated(wk1, wk1_hi, wk1_lo)
            pool.memset(f32(ones_r[:, :]), 1.0).then_inc(split_w1, 1)
            chain(pool.memset(block_of[:, :], 1.0))
            chain(pool.affine_select(out=block_of[:, :], in_=block_of[:, :], compare_op=ALU.is_ge, fill=0.0, base=0,
                                     pattern=[[-32, 4]], channel_multiplier=1))
            chain(pool.affine_select(out=block_of[:, :], in_=block_of[:, :], compare_op=ALU.is_ge, fill=0.0, base=31,
                                     pattern=[[32, 4]], channel_multiplier=-1))
            def split_expert(e, buf):
                pool.wait_ge(ld_e[buf], (e - buf) * 24 + 48)
                if not isinstance(e, int) or e >= 2:
                    pool.wait_ge(b_y, e * 2 - 2)
                pool.tensor_tensor(w12_hi[:, buf, :], w12[:, buf, :], zero[:, :].to_broadcast([P, 2 * HID]),
                                   ALU.add).then_inc(b_hi, 1)
                pool.wait_ge(b_hi, e + 1)
                pool.tensor_tensor(w12_lo[:, buf, :], w12[:, buf, :], f32(w12_hi[:, buf, :]), ALU.subtract).then_inc(b_lo, 1)

            split_expert(0, 0)
            split_expert(1, 1)
            pool.wait_ge(ld_d, 16 * 6)
            pool.tensor_scalar(d1_w[:, :, :], k1_u[:, :, :], 2.0, -1.0, ALU.mult, ALU.add).then_inc(d_w, 1)
            pool.tensor_scalar(d2_w[:, :, :], k2_u[:, :, :], 2.0, -1.0, ALU.mult, ALU.add).then_inc(d_w, 1)
            pool.wait_ge(a_q_ps, 2 * NP)
            split_repeated(wq1, wq1_hi, wq1_lo)
            pool.wait_ge(a_o, NB)
            pool.memset(v1, 1.0).then_inc(zeros_ok, 1)

            def block_diagonal(b, j):
                keys = f32(k_st[:, :, bass.ds(b * P, P)]).unsqueeze(2).to_broadcast([P, NG, 4, P])
                blocks = block_of[:, :].unsqueeze(1).unsqueeze(3).to_broadcast([P, NG, 4, P])
                pool.tensor_tensor(k_bd[:, j, :, :, :], keys, blocks, ALU.mult).then_inc(k1_bd, 1)

            pool.wait_ge(k1_st, NG * NT)
            for j in range(2):
                block_diagonal(j, j)
            with pool.Fori(1, E // 2) as i:
                for buf in range(2):
                    split_expert(i * 2 + buf, buf)
            for b in range(NB):
                pool.wait_ge(ln_xn, 2 * NB + b + 1)
                pool.tensor_tensor(x_sb[:, b, :], x_sb[:, b, :], bo1[:, :], ALU.add).then_inc(xb1, 1)
            with pool.Fori(1, NP) as p:
                for j in range(2):
                    pool.wait_ge(c_s, p * 4 + (2 * j - 2))
                    block_diagonal(p * 2 + j, j)

        @block.tensor
        def _(pe):
            def split3(dst, w_hi, w_lo, x_hi, x_lo, start=True, stop=True):
                pe.matmul(dst, w_hi, x_hi, start=start, stop=False)
                pe.matmul(dst, w_hi, x_lo, start=False, stop=False)
                return pe.matmul(dst, w_lo, x_hi, start=False, stop=stop)

            def ln_transposes(s):
                for b in range(NB):
                    pe.wait_ge(ln_xn, NB * s + b + 1)
                    ins = pe.transpose(ps[:, M0 + b // 4, (b % 4) * P:(b % 4 + 1) * P], xn[:, b, :], ident[:, :])
                    if b % 4 == 3:
                        ins.then_inc(ln_ps, 1)

            pe.wait_ge(const_ok, 2)
            pe.wait_ge(ld_ctx, 16)
            for b in range(NB):
                ins = pe.transpose(ps[0:CK, b // 4, (b % 4) * P:(b % 4 + 1) * P], ctx_sb[:, b, :], ident[:, :])
                if b % 4 == 3:
                    ins.then_inc(ctxT_ps, 1)
            ln_transposes(0)
            pe.wait_ge(split_w0, 2)
            for n in range(NC0 * NT):
                k, t = n // NT, n % NT
                pe.wait_ge(ctxT_ok, t + 1)
                if n >= 2:
                    pe.wait_ge(k0_ok, n - 1)
                sl = slice(t * TG, (t + 1) * TG)
                split3(ps[:, 2 + n % 2, :], wk0_hi[0:CK, k * P:(k + 1) * P], wk0_lo[0:CK, k * P:(k + 1) * P],
                       ctxT_hi[0:CK, sl], ctxT_lo[0:CK, sl]).then_inc(k0_ps, 1)
            for b in range(NB):
                if b >= 2:
                    pe.wait_ge(v0_ok, b - 1)
                pe.matmul(ps[:, 4 + b % 2, :], ctxT[0:CK, b * P:(b + 1) * P], wv0[:, :],
                          start=True, stop=True).then_inc(v0_ps, 1)

            def a_queries(p):
                for m in range(2):
                    for k in (2 * m, 2 * m + 1):
                        ins = split3(ps[:, M0 + m, (k % 2) * 2 * P:(k % 2 + 1) * 2 * P],
                                     wq0_hi[:, k * P:(k + 1) * P], wq0_lo[:, k * P:(k + 1) * P],
                                     xT_hi[:, bass.ds(p * 2 * P, 2 * P)], xT_lo[:, bass.ds(p * 2 * P, 2 * P)])
                    ins.then_inc(a_q_ps, 1)

            def a_scores(p, j):
                for h in range(H0):
                    q = (q_ev if h % 2 == 0 else q_od)[:, h // 2, j * P:(j + 1) * P]
                    ins = pe.matmul(ps[:, 2 * j + h // 4, (h % 4) * P:(h % 4 + 1) * P], q,
                                    kT0[:, h // 2, bass.ds(p * 2 * P + j * P, P)], start=True, stop=True)
                ins.then_inc(a_s, 1)

            def a_probs_turn(p, j):
                pe.wait_ge(a_exp, p * 2 + j + 1)
                for h in range(H0):
                    ins = pe.transpose(ps[:, 4 + h // 4, (h % 4) * P:(h % 4 + 1) * P], probs[:, j, h, :], ident[:, :])
                ins.then_inc(a_pt_ps, 1)

            def a_values(p, j):
                pe.wait_ge(a_pt_v, p * 3 + 2 + j)
                if j == 1:
                    pe.wait_ge(a_pt_a, p + 1)
                for h in range(H0):
                    ins = pe.matmul(ps[:, 2 * j, h * D0:(h + 1) * D0], probsT[:, j, h, :],
                                    v0[:, bass.ds(p * 2 + j, 1), h * D0:(h + 1) * D0].rearrange("p o d -> p (o d)"),
                                    start=True, stop=True)
                ins.then_inc(a_o, 1)

            def a_out_turn(p, j):
                pe.wait_ge(a_norm, p * 2 + j + 1)
                for k in range(NC0):
                    ins = pe.transpose(ps[:, M0 + j, k * P:(k + 1) * P], o_sb[:, j, k * P:(k + 1) * P], ident[:, :])
                ins.then_inc(a_oT_ps, 1)

            def a_out(p, j):
                pe.wait_ge(a_oT, p * 2 + j + 1)
                for k in range(NC0):
                    ins = pe.matmul(ps[:, M0 + j, 0:C], oT[:, j, k * P:(k + 1) * P], wo0[:, k, :],
                                    start=(k == 0), stop=(k == NC0 - 1))
                ins.then_inc(a_wo, 1)

            def a_step(p, last):
                a_probs_turn(p, 0)
                a_values(p, 0)
                if not last:
                    a_queries(p + 1)
                a_probs_turn(p, 1)
                a_values(p, 1)
                if not last:
                    pe.wait_ge(a_qe, p * 2 + 4)
                    pe.wait_ge(a_qo, p * 2 + 4)
                    pe.wait_ge(a_norm, p * 2 + 1)
                    a_scores(p + 1, 0)
                a_out_turn(p, 0)
                a_out_turn(p, 1)
                if not last:
                    a_scores(p + 1, 1)
                a_out(p, 0)
                a_out(p, 1)

            pe.wait_ge(ln_lo, NT)
            pe.wait_ge(ln_hi, NT)
            a_queries(0)
            pe.wait_ge(k0_ok, NC0 * NT)
            pe.wait_ge(a_qe, 2)
            pe.wait_ge(a_qo, 2)
            pe.wait_ge(zeros_ok, 2)
            a_scores(0, 0)
            a_scores(0, 1)
            pe.wait_ge(v0_ok, NB)
            with pe.Fori(0, NP - 1) as p:
                a_step(p, False)
            a_step(NP - 1, True)

            pe.wait_ge(split_w1, 3)
            for n in range(NG * NT):
                g, t = n // NT, n % NT
                if n >= 2:
                    pe.wait_ge(k1_st, n - 1)
                sl = slice(t * TG, (t + 1) * TG)
                split3(ps[:, n % 2, :], wk1_hi[:, g * P:(g + 1) * P], wk1_lo[:, g * P:(g + 1) * P], ctxT_hi[:, sl], ctxT_lo[:, sl]).then_inc(k1_ps, 1)
            for b in range(NB):
                if b >= 2:
                    pe.wait_ge(v1_ok, b - 1)
                pe.matmul(ps[:, 2 + b % 2, 0:C], ctxT[:, b * P:(b + 1) * P], wv1[:, :],
                          start=True, stop=True).then_inc(v1_ps, 1)

            ln_transposes(1)
            pe.wait_ge(ln_f, NT)
            for b in range(NB):
                ins = pe.matmul(ps[:, 4, b * E:(b + 1) * E], xT[:, b * P:(b + 1) * P], wg[:, :], start=True, stop=True)
            ins.then_inc(g_ps, 1)

            def b_hidden(e, buf, t):
                for c in range(NH):
                    v = e * (NT * NH) + t * NH + c
                    if not (isinstance(e, int) and e == 0 and t == 0):
                        pe.wait_ge(b_u, v - 1)
                    sl = slice(t * TG, (t + 1) * TG)
                    for half, bank, s in ((0, c, b_h), (HID, 2 + c, b_g)):
                        w = slice(half + c * P, half + (c + 1) * P)
                        split3(ps[:, bank, :], w12_hi[:, buf, w], w12_lo[:, buf, w],
                               xT_hi[:, sl], xT_lo[:, sl]).then_inc(s, 1)

            def b_down(e, buf, t):
                pe.wait_ge(b_u, e * 4 + t * 2 + 2)
                for k in range(4):
                    for c in range(NH):
                        ins = pe.matmul(ps[:, 4 + t, k * C:(k + 1) * C], uT[:, t, c, k * P:(k + 1) * P],
                                        w3[:, buf, c, :], start=(c == 0), stop=(c == NH - 1))
                ins.then_inc(b_y, 1)

            def b_step(e, last):
                b_hidden(e, 0, 1)
                b_down(e, 0, 0)
                pe.wait_ge(b_lo, e + 2)
                b_hidden(e + 1, 1, 0)
                b_down(e, 0, 1)
                b_hidden(e + 1, 1, 1)
                b_down(e + 1, 1, 0)
                if not last:
                    pe.wait_ge(b_lo, e + 3)
                    b_hidden(e + 2, 0, 0)
                b_down(e + 1, 1, 1)

            pe.wait_ge(ln_lo, 2 * NT)
            pe.wait_ge(b_lo, 1)
            pe.wait_ge(v1_ok, NB)
            b_hidden(0, 0, 0)
            pe.wait_ge(g_lg, 1)
            with pe.Fori(0, E // 2 - 1) as i:
                b_step(i * 2, False)
            b_step(E - 2, True)

            ln_transposes(2)

            def c_queries(p):
                for m in range(2):
                    for g in (2 * m, 2 * m + 1):
                        gs = slice(g * P, (g + 1) * P)
                        dst = ps[:, M0 + m, (g % 2) * 2 * P:(g % 2 + 1) * 2 * P]
                        split3(dst, wq1_hi[:, gs], wq1_lo[:, gs], xT_hi[:, bass.ds(p * 2 * P, 2 * P)], xT_lo[:, bass.ds(p * 2 * P, 2 * P)],
                               stop=False)
                        ins = pe.matmul(dst, bq1_s[:, gs], ones_r[:, :], start=False, stop=True)
                    ins.then_inc(c_q_ps, 1)

            def c_scores(p, j, half):
                for g in range(2):
                    ins = pe.matmul(ps[:, 2 * half + g, :], q_st[:, 2 * half + g, j * P:(j + 1) * P],
                                    k_bd[:, j, 2 * half + g, :, :].rearrange("p h k -> p (h k)"), start=True, stop=True)
                ins.then_inc(c_s, 1)

            def c_values(p, j, half):
                n = p * 4 + (2 * j + half)
                pe.wait_ge(c_exp, n + 1)
                for h in range(8):
                    ins = pe.transpose(ps[:, 4 + h // 4, (h % 4) * P:(h % 4 + 1) * P], sh1[:, half, h * P:(h + 1) * P],
                                       ident[:, :])
                ins.then_inc(c_pt_ps, 1)
                return n

            def c_weighted(p, j, half):
                n = p * 4 + (2 * j + half)
                pe.wait_ge(c_pt, n + 1)
                for h in range(8):
                    hh = 8 * half + h
                    ins = pe.matmul(ps[:, M0 + j, hh * (D1 + 1):(hh + 1) * (D1 + 1)], sh1T[:, half, h * P:(h + 1) * P],
                                    v1[:, bass.ds(p * 2 + j, 1), hh, :].rearrange("p o d -> p (o d)"),
                                    start=True, stop=True)
                ins.then_inc(c_o, 1)

            def c_tail(p, j):
                pe.wait_ge(c_norm, p * 2 + j + 1)
                pe.transpose(ps[:, M0 + j, 256:256 + P], o1[:, :], ident[:, :]).then_inc(c_oT_ps, 1)
                pe.wait_ge(c_oT, p * 2 + j + 1)
                pe.matmul(ps[:, M0 + j, 384:384 + C], o1T[:, :], wo1[:, :], start=True, stop=True).then_inc(c_wo, 1)

            def c_step(p, last):
                c_values(p, 0, 0)
                c_weighted(p, 0, 0)
                c_scores_wait(p, 2)
                pe.wait_ge(k1_bd, p * 2 + 2)
                c_scores(p, 1, 0)
                c_values(p, 0, 1)
                c_weighted(p, 0, 1)
                c_scores_wait(p, 3)
                c_scores(p, 1, 1)
                c_tail(p, 0)
                c_values(p, 1, 0)
                c_weighted(p, 1, 0)
                c_values(p, 1, 1)
                c_weighted(p, 1, 1)
                c_tail(p, 1)
                if not last:
                    pe.wait_ge(c_x, p * 2 + 2)
                    c_queries(p + 1)
                    pe.wait_ge(c_q, p * 2 + 4)
                    pe.wait_ge(k1_bd, p * 2 + 3)
                    c_scores(p + 1, 0, 0)
                    c_scores(p + 1, 0, 1)

            def c_scores_wait(p, u):
                pe.wait_ge(c_sub, p * 4 + (u - 1))

            pe.wait_ge(ln_lo, 3 * NT)
            pe.wait_ge(ln_hi, 3 * NT)
            pe.wait_ge(masks, 10)
            c_queries(0)
            pe.wait_ge(c_q, 2)
            pe.wait_ge(k1_bd, 1)
            pe.wait_ge(b_acc, 2 * E)
            c_scores(0, 0, 0)
            c_scores(0, 0, 1)
            with pe.Fori(0, NP - 1) as p:
                c_step(p, False)
            c_step(NP - 1, True)

            ln_transposes(3)
            pe.wait_ge(d_w, 3)
            n = 0
            for layer in range(3):
                for t in range(NT):
                    sl = slice(t * TG, (t + 1) * TG)
                    for m in range(4 if layer < 2 else 1):
                        ms = slice(m * P, (m + 1) * P)
                        if layer == 0:
                            pe.wait_ge(ln_lo, 3 * NT + t + 1)
                            pe.wait_ge(ln_hi, 3 * NT + t + 1)
                            terms = [(d0_w[:, ms], xx[:, sl]) for xx in (xT_hi, xT_lo)]
                        else:
                            pe.wait_ge(d_lo, 8 * (layer - 1) + 4 * t + 4)
                            w = d1_w if layer == 1 else d2_w
                            h = h_at[layer - 1, t]
                            terms = [(w[:, k, ms], h[:, part, k, :]) for k in range(4) for part in range(2)]
                        if n >= 4:
                            pe.wait_ge(d_relu, n - 3)
                        for i, (w_, x_) in enumerate(terms):
                            ins = pe.matmul(ps[:, n % 4, :], w_, x_, start=(i == 0), stop=(i == len(terms) - 1))
                        ins.then_inc(d_ps, 1)
                        n += 1
            for t in range(NT):
                pe.wait_ge(d_relu, 16 + t + 1)
                for k in range(4):
                    ins = pe.transpose(ps[:, 4 + t, k * P:(k + 1) * P], yT[:, t, k * P:(k + 1) * P], ident[:, :])
                ins.then_inc(d_yT_ps, 1)

        @block.scalar
        def _(act):
            def ln_hi_copy(s, plain):
                for t in range(NT):
                    act.wait_ge(ln_ps, NT * s + t + 1)
                    sl = slice(t * TG, (t + 1) * TG)
                    act.activation(xT_hi[:, sl], ps[:, M0 + t, :], ACT.Copy).then_inc(ln_hi, 1)
                    if plain:
                        act.activation(xT[:, sl], ps[:, M0 + t, :], ACT.Copy).then_inc(ln_f, 1)

            for t in range(NT):
                act.wait_ge(ctxT_ps, t + 1)
                act.activation(ctxT[0:CK, t * TG:(t + 1) * TG], ps[0:CK, t, :], ACT.Copy).then_inc(ctxT_f, 1)
            act.wait_ge(const_ok, 1)
            for t in range(NT):
                for k in range(4):
                    ins = act.activation(ctxT[CK:CK1, t * TG + k * P:t * TG + (k + 1) * P], ones[CK:CK1, :], ACT.Copy)
                ins.then_inc(ctxT_f, 1)
            act.wait_ge(ctxT_f, 2 * NT)
            for t in range(NT):
                sl = slice(t * TG, (t + 1) * TG)
                act.activation(ctxT_hi[:, sl], ctxT[:, sl], ACT.Copy).then_inc(ctxT_h, 1)
            ln_hi_copy(0, False)
            for b in range(NB):
                act.wait_ge(v0_ps, b + 1)
                act.activation(v0[:, b, :], ps[:, 4 + b % 2, :], ACT.Copy).then_inc(v0_ok, 1)

            def a_query_copy(n):
                act.wait_ge(zeros_ok, 2)
                for m in range(2):
                    act.wait_ge(a_q_ps, n + m + 1)
                    act.activation(q_od[64:P, 2 * m:2 * m + 2, :],
                                   ps[64:P, M0 + m, :].rearrange("p (k t) -> p k t", k=2), ACT.Copy,
                                   scale=D0 ** -0.5).then_inc(a_qo, 1)

            def a_exp_heads(p, j):
                act.wait_ge(a_max, p * 2 + j + 1)
                for h in range(H0):
                    ins = act.activation(probs[:, j, h, :], ps[:, 2 * j + h // 4, (h % 4) * P:(h % 4 + 1) * P], ACT.Exp,
                                         bias=negmax[:, j, h:h + 1], scale=1.0, accum_out=sums[:, j, h:h + 1])
                ins.then_inc(a_exp, 1)

            def a_oT_copy(p, j):
                act.wait_ge(a_oT_ps, p * 2 + j + 1)
                act.activation(oT[:, j, :], ps[:, M0 + j, :], ACT.Copy).then_inc(a_oT, 1)

            def a_step(p, last):
                a_exp_heads(p, 1)
                if not last:
                    a_query_copy(p * 2 + 2)
                act.wait_ge(a_pt_ps, p * 2 + 2)
                act.activation(probsT[:, 1, 4:8, :].rearrange("p h k -> p (h k)"), ps[:, 5, :], ACT.Copy).then_inc(a_pt_a, 1)
                a_oT_copy(p, 0)
                a_oT_copy(p, 1)
                if not last:
                    a_exp_heads(p + 1, 0)

            a_query_copy(0)
            a_exp_heads(0, 0)
            with act.Fori(0, NP - 1) as p:
                a_step(p, False)
            a_step(NP - 1, True)

            act.wait_ge(masks, 10)
            for n in range(NG * NT):
                act.wait_ge(k1_ps, n + 1)
                act.activation(part[:, n % 2, :], ps[:, n % 2, :], ACT.Copy, scale=sign[:, 1:2]).then_inc(k1_part, 1)
            for b in range(NB):
                act.wait_ge(v1_ps, b + 1)
                act.wait_ge(zeros_ok, 3)
                act.activation(v1[:, b, :, 0:D1], ps[:, 2 + b % 2, 0:C].rearrange("p (h d) -> p h d", d=D1),
                               ACT.Copy).then_inc(v1_ok, 1)
            ln_hi_copy(1, True)
            act.wait_ge(g_d, 1)
            act.activation(ge[:, :], gd[:, :], ACT.Exp).then_inc(g_e, 1)

            def b_silu_step(e):
                for c in range(4):
                    v = e * 4 + c
                    act.wait_ge(b_h, v + 1)
                    if not (isinstance(e, int) and e == 0 and c < 2):
                        act.wait_ge(b_u, v - 1)
                    act.activation(silu[:, c % 2, :], ps[:, c % 2, :], ACT.Silu).then_inc(b_silu, 1)

            b_silu_step(0)
            with act.Fori(1, E) as e:
                b_silu_step(e)

            ln_hi_copy(2, False)

            def c_query_part(n):
                for m in range(2):
                    act.wait_ge(c_q_ps, n + m + 1)
                    act.activation(part[:, m, :], ps[:, M0 + m, :], ACT.Copy, scale=sign[:, 0:1]).then_inc(c_part, 1)

            def c_unit(p, j, half):
                n = p * 4 + (2 * j + half)
                act.wait_ge(c_sub, n + 1)
                act.activation(sh1[:, half, :], sh1[:, half, :], ACT.Exp, scale=D1 ** -0.5).then_inc(c_exp, 1)

            def c_unit_copy(p, j, half):
                n = p * 4 + (2 * j + half)
                act.wait_ge(c_pt_ps, n + 1)
                act.activation(sh1T[:, half, :], ps[:, 4:6, :].rearrange("p a b -> p (a b)"), ACT.Copy).then_inc(c_pt, 1)

            def c_tail(p, j):
                act.wait_ge(c_oT_ps, p * 2 + j + 1)
                act.activation(o1T[:, :], ps[:, M0 + j, 256:256 + P], ACT.Copy).then_inc(c_oT, 1)

            def c_step(p, last):
                c_unit(p, 0, 1)
                c_unit_copy(p, 0, 0)
                c_unit(p, 1, 0)
                c_unit_copy(p, 0, 1)
                c_tail(p, 0)
                c_unit(p, 1, 1)
                c_unit_copy(p, 1, 0)
                c_unit_copy(p, 1, 1)
                c_tail(p, 1)
                if not last:
                    c_query_part(p * 2 + 2)
                    c_unit(p + 1, 0, 0)

            c_query_part(0)
            c_unit(0, 0, 0)
            with act.Fori(0, NP - 1) as p:
                c_step(p, False)
            c_step(NP - 1, True)

            ln_hi_copy(3, False)
            act.wait_ge(d_w, 3)
            for n in range(16):
                act.wait_ge(d_ps, n + 1)
                if n >= 2:
                    act.wait_ge(d_lo, n - 1)
                act.activation(relu[:, n % 2, :], ps[:, n % 4, :], ACT.Relu, scale=scale2[:, n // 8:n // 8 + 1]).then_inc(d_relu, 1)
            for t in range(NT):
                act.wait_ge(d_ps, 16 + t + 1)
                act.activation(yT[:, t, :], ps[:, t, :], ACT.Copy, scale=scale[:, 2:3]).then_inc(d_relu, 1)

        @block.vector
        def _(dve):
            nwt = [0]

            def ln(s):
                def newton(ins):
                    nwt[0] += 1
                    ins.then_inc(ln_nw, 1)
                    dve.wait_ge(ln_nw, nwt[0])

                for b in range(NB):
                    dve.bn_stats(stats[:, b, :], x_sb[:, b, :]).then_inc(ln_st, 1)
                for b in range(NB):
                    dve.wait_ge(ln_st, NB * s + b + 1)
                    dve.bn_aggr(meanvar[:, b, :], stats[:, b, :]).then_inc(ln_mv, 1)
                dve.wait_ge(ln_mv, NB * (s + 1))
                newton(dve.tensor_scalar(ve[:, :], meanvar[:, :, 1], EPS, None, ALU.add))
                newton(dve.tensor_scalar(nt[:, :].bitcast(I32), ve[:, :].bitcast(I32), 1, None, ALU.logical_shift_right))
                newton(dve.tensor_scalar(rs[:, :].bitcast(I32), nt[:, :].bitcast(I32), -1.0, float(RSQRT_SEED), ALU.mult, ALU.add))
                for _ in range(4):
                    newton(dve.tensor_tensor(nt[:, :], rs[:, :], rs[:, :], ALU.mult))
                    newton(dve.scalar_tensor_tensor(nu[:, :], nt[:, :], -0.5, ve[:, :], ALU.mult, ALU.mult))
                    newton(dve.scalar_tensor_tensor(rs[:, :], nu[:, :], 1.5, rs[:, :], ALU.add, ALU.mult))
                for b in range(NB):
                    dve.tensor_scalar(xn[:, b, :], x_sb[:, b, :], meanvar[:, b, 0:1], rs[:, b:b + 1],
                                      ALU.subtract, ALU.mult).then_inc(ln_xn, 1)
                if s == 0:
                    ctx_lo()
                for t in range(NT):
                    dve.wait_ge(ln_hi, NT * s + t + 1)
                    if s == 1:
                        dve.wait_ge(ln_f, t + 1)
                    sl = slice(t * TG, (t + 1) * TG)
                    dve.tensor_tensor(xT_lo[:, sl], ps[:, M0 + t, :], f32(xT_hi[:, sl]), ALU.subtract).then_inc(ln_lo, 1)

            def ctx_lo():
                for t in range(NT):
                    dve.wait_ge(ctxT_h, t + 1)
                    sl = slice(t * TG, (t + 1) * TG)
                    dve.tensor_tensor(ctxT_lo[:, sl], ctxT[:, sl], f32(ctxT_hi[:, sl]), ALU.subtract).then_inc(ctxT_ok, 1)

            dve.wait_ge(ld_x, 16)
            ln(0)
            for n in range(NC0 * NT):
                k, t = n // NT, n % NT
                dve.wait_ge(k0_ps, n + 1)
                dve.tensor_copy(kT0[:, k, t * TG:(t + 1) * TG], ps[:, 2 + n % 2, :]).then_inc(k0_ok, 1)

            def a_query_copy(n):
                for m in range(2):
                    dve.wait_ge(a_q_ps, n + m + 1)
                    dve.tensor_scalar(q_ev[0:64, 2 * m:2 * m + 2, :],
                                      ps[0:64, M0 + m, :].rearrange("p (k t) -> p k t", k=2), D0 ** -0.5, None,
                                      ALU.mult).then_inc(a_qe, 1)

            def a_rowmax(p, j):
                dve.wait_ge(a_s, p * 2 + j + 1)
                dve.tensor_reduce(negmax[:, j, :], ps[:, 2 * j:2 * j + 2, :].rearrange("p a (h k) -> p (a h) k", k=P),
                                  X, ALU.max, negate=True).then_inc(a_max, 1)

            def a_probsT_copy(p, j):
                dve.wait_ge(a_pt_ps, p * 2 + j + 1)
                for m in range(2 - j):
                    dve.tensor_copy(probsT[:, j, 4 * m:4 * m + 4, :].rearrange("p h k -> p (h k)"),
                                    ps[:, 4 + m, :]).then_inc(a_pt_v, 1)

            def a_normalise(p, j):
                dve.wait_ge(a_exp, p * 2 + j + 1)
                dve.reciprocal(rsum[:, j, :], sums[:, j, :]).then_inc(a_rs, 1)
                dve.wait_ge(a_rs, p * 2 + j + 1)
                dve.wait_ge(a_o, p * 2 + j + 1)
                dve.tensor_tensor(o_sb[:, j, :].rearrange("p (h d) -> p h d", d=D0),
                                  ps[:, 2 * j, :].rearrange("p (h d) -> p h d", d=D0),
                                  rsum[:, j, :].unsqueeze(2).to_broadcast([P, H0, D0]), ALU.mult).then_inc(a_norm, 1)

            def a_residual(p, j):
                dve.wait_ge(a_wo, p * 2 + j + 1)
                xs = x_sb[:, bass.ds(p * 2 + j, 1), :].rearrange("p o c -> p (o c)")
                dve.tensor_tensor(xs, ps[:, M0 + j, 0:C], xs, ALU.add).then_inc(a_x, 1)

            def a_step(p, last):
                a_probsT_copy(p, 0)
                if not last:
                    a_query_copy(p * 2 + 2)
                a_normalise(p, 0)
                a_probsT_copy(p, 1)
                a_normalise(p, 1)
                if not last:
                    a_rowmax(p + 1, 0)
                    a_rowmax(p + 1, 1)
                a_residual(p, 0)
                a_residual(p, 1)

            a_query_copy(0)
            a_rowmax(0, 0)
            a_rowmax(0, 1)
            dve.wait_ge(xb0, NB)
            with dve.Fori(0, NP - 1) as p:
                a_step(p, False)
            a_step(NP - 1, True)

            dve.wait_ge(ld_d, 16 * 6)
            dve.tensor_tensor(d0_w[:, :], k0_u[:, 0, :], k0_u[:, 1, :], ALU.subtract).then_inc(d_w, 1)
            dve.tensor_scalar(scale2[:, :], scale[:, :], 2.0, None, ALU.mult).then_inc(masks, 1)
            dve.wait_ge(masks, 1)
            dve.tensor_scalar(scale2[:, 0:1], scale2[:, 0:1], 2.0, None, ALU.mult).then_inc(masks, 1)
            dve.wait_ge(const_ok, 3)
            dve.tensor_scalar(bit_i[:, 0:1], row_i[:, :], 4, 1, ALU.logical_shift_right, ALU.bitwise_and).then_inc(masks, 1)
            dve.tensor_scalar(bit_i[:, 1:2], row_i[:, :], 3, 1, ALU.logical_shift_right, ALU.bitwise_and).then_inc(masks, 1)
            dve.tensor_scalar(bit_i[:, 2:3], row_i[:, :], 0, 1, ALU.logical_shift_right, ALU.bitwise_and).then_inc(masks, 1)
            dve.wait_ge(masks, 5)
            dve.tensor_copy(is_lo[:, :], bit_i[:, :]).then_inc(masks, 1)
            dve.wait_ge(masks, 6)
            dve.tensor_scalar(sign[:, :], is_lo[:, :], -2.0, 1.0, ALU.mult, ALU.add).then_inc(masks, 1)
            dve.wait_ge(masks, 7)
            dve.wait_ge(ld_w1, 16 * 8)
            dve.tensor_scalar(bq1_r[:, :], bq1[:, :], sign[0:2, 2:3], None, ALU.mult).then_inc(masks, 1)
            dve.wait_ge(masks, 8)
            dve.scalar_tensor_tensor(bq1_p[:, :], bq1[:, :], is_lo[0:2, 2:3], f32(bq1_r[:, :]), ALU.mult, ALU.add).then_inc(masks, 1)
            dve.wait_ge(masks, 9)
            dve.tensor_copy(stacked(bq1_s), repeated(bq1_p)).then_inc(masks, 1)
            for n in range(NG * NT):
                dve.wait_ge(k1_part, n + 1)
                dve.scalar_tensor_tensor(k_st[:, n // NT, (n % NT) * TG:(n % NT + 1) * TG], ps[:, n % 2, :], is_lo[:, 1:2], f32(part[:, n % 2, :]),
                                         ALU.mult, ALU.add).then_inc(k1_st, 1)

            dve.wait_ge(a_x, NB)
            ln(1)
            dve.wait_ge(g_ps, 1)
            dve.tensor_copy(lg[:, :, :].rearrange("p b e -> p (b e)"), ps[:, 4, 0:NB * E]).then_inc(g_lg, 1)
            dve.wait_ge(g_lg, 1)
            for b in range(NB):
                dve.max(top[:, b, :], lg[:, b, :]).then_inc(g_top, 1)
            for b in range(NB):
                dve.wait_ge(g_top, b + 1)
                dve.max_index(topi[:, b, :], top[:, b, :], lg[:, b, :]).then_inc(g_idx, 1)
            dve.wait_ge(g_top, NB)
            dve.tensor_tensor(gd[:, :], top[:, :, 1], top[:, :, 0], ALU.subtract).then_inc(g_d, 1)
            dve.wait_ge(g_idx, NB)
            dve.tensor_copy(topf[:, :, :], topi[:, :, :]).then_inc(g_f, 1)
            dve.wait_ge(g_e, 1)
            dve.tensor_scalar(gs[:, :], ge[:, :], 1.0, None, ALU.add).then_inc(g_s, 1)
            dve.wait_ge(g_s, 1)
            dve.reciprocal(gw[:, 0, :], gs[:, :]).then_inc(g_w, 1)
            dve.wait_ge(g_w, 1)
            dve.tensor_tensor(gw[:, 1, :], gw[:, 0, :], ge[:, :], ALU.mult).then_inc(g_w, 1)
            dve.wait_ge(g_f, 1)
            dve.wait_ge(g_w, 2)
            for k in range(2):
                dve.tensor_tensor(pick[:, k, :, :], iota_e[:, :, :], topf[:, :, k:k + 1].to_broadcast([P, NB, E]),
                                  ALU.is_equal).then_inc(g_pick, 1)
            for k in range(2):
                dve.wait_ge(g_pick, k + 1)
                dve.tensor_tensor(picked[:, k, :, :], pick[:, k, :, :], gw[:, k, :].unsqueeze(2).to_broadcast([P, NB, E]),
                                  ALU.mult).then_inc(g_sel, 1)
            dve.wait_ge(g_sel, 2)
            dve.tensor_tensor(comb[:, :, :].rearrange("p e b -> p b e"), picked[:, 0, :, :], picked[:, 1, :, :],
                              ALU.add).then_inc(g_ok, 1)

            def b_gate(e, t):
                for c in range(NH):
                    v = e * 4 + (2 * t + c)
                    dve.wait_ge(b_silu, v + 1)
                    dve.wait_ge(b_g, v + 1)
                    if not isinstance(e, int) or e > 0:
                        dve.wait_ge(b_y, e * 2 + t - 1)
                    dve.tensor_tensor(uT[:, t, c, :], ps[:, 2 + c, :], silu[:, c, :], ALU.mult).then_inc(b_u, 1)

            def b_add(e, t):
                dve.wait_ge(b_y, e * 2 + t + 1)
                if not isinstance(e, int) or e > 0:
                    dve.wait_ge(b_acc, e * 2 + t - 1)
                for k in range(4):
                    b = 4 * t + k
                    ins = dve.scalar_tensor_tensor(x_sb[:, b, :], ps[:, 4 + t, k * C:(k + 1) * C],
                                                   comb[:, bass.ds(e, 1), b:b + 1].rearrange("p o b -> p (o b)"),
                                                   x_sb[:, b, :], ALU.mult, ALU.add)
                ins.then_inc(b_acc, 1)

            dve.wait_ge(g_ok, 1)
            b_gate(0, 0)
            b_gate(0, 1)
            b_add(0, 0)
            with dve.Fori(1, E) as e:
                b_gate(e, 0)
                b_add(e - 1, 1)
                b_gate(e, 1)
                b_add(e, 0)
            b_add(E - 1, 1)

            dve.wait_ge(b_acc, 2 * E)
            ln(2)

            def c_query_stack(n):
                for m in range(2):
                    dve.wait_ge(c_part, n + m + 1)
                    dve.scalar_tensor_tensor(q_st[:, 2 * m:2 * m + 2, :].rearrange("p g n -> p (g n)"), ps[:, M0 + m, :],
                                             is_lo[:, 0:1], f32(part[:, m, :]), ALU.mult, ALU.add).then_inc(c_q, 1)

            def c_shift(p, j, half):
                n = p * 4 + (2 * j + half)
                dve.wait_ge(c_s, n + 1)
                src = ps[:, 2 * half:2 * half + 2, :].rearrange("p a (h k) -> p (a h) k", k=P)
                dve.tensor_reduce(negmax1[:, half, :], src, X, ALU.max, negate=True).then_inc(c_max, 1)
                dve.wait_ge(c_max, n + 1)
                if not (isinstance(n, int) and n < 2):
                    dve.wait_ge(c_pt_ps, n - 1)
                dve.tensor_tensor(sh1[:, half, :].rearrange("p (h k) -> p h k", k=P), src,
                                  negmax1[:, half, :].unsqueeze(2).to_broadcast([P, 8, P]), ALU.add).then_inc(c_sub, 1)

            def c_normalise(p, j):
                dve.wait_ge(c_o, p * 4 + 2 * j + 2)
                o = ps[:, M0 + j, 0:H1 * (D1 + 1)].rearrange("p (h d) -> p h d", d=D1 + 1)
                dve.reciprocal(rsum1[:, :], o[:, :, D1]).then_inc(c_rs, 1)
                dve.wait_ge(c_rs, p * 2 + j + 1)
                dve.tensor_tensor(o1[:, :].rearrange("p (h d) -> p h d", d=D1), o[:, :, 0:D1],
                                  rsum1[:, :].unsqueeze(2).to_broadcast([P, H1, D1]), ALU.mult).then_inc(c_norm, 1)

            def c_residual(p, j):
                dve.wait_ge(c_wo, p * 2 + j + 1)
                xs = x_sb[:, bass.ds(p * 2 + j, 1), :].rearrange("p o c -> p (o c)")
                dve.tensor_tensor(xs, ps[:, M0 + j, 384:384 + C], xs, ALU.add).then_inc(c_x, 1)

            def c_step(p, last):
                c_shift(p, 1, 0)
                c_normalise(p, 0)
                c_shift(p, 1, 1)
                c_residual(p, 0)
                c_normalise(p, 1)
                c_residual(p, 1)
                if not last:
                    c_query_stack(p * 2 + 2)
                    c_shift(p + 1, 0, 0)
                    c_shift(p + 1, 0, 1)

            c_query_stack(0)
            c_shift(0, 0, 0)
            c_shift(0, 0, 1)
            dve.wait_ge(xb1, NB)
            with dve.Fori(0, NP - 1) as p:
                c_step(p, False)
            c_step(NP - 1, True)

            dve.wait_ge(c_x, NB)
            ln(3)
            for n in range(16):
                t, m = (n % 8) // 4, n % 4
                h = h_at[n // 8, t]
                dve.wait_ge(d_relu, n + 1)
                dve.tensor_copy(h[:, 0, m, :], relu[:, n % 2, :]).then_inc(d_hi, 1)
                dve.wait_ge(d_hi, n + 1)
                dve.tensor_tensor(h[:, 1, m, :], relu[:, n % 2, :], f32(h[:, 0, m, :]), ALU.subtract).then_inc(d_lo, 1)
            for t in range(NT):
                dve.wait_ge(d_yT_ps, t + 1)
                dve.tensor_tensor(fin[:, t, :], ps[:, 4 + t, :],
                                  x_sb[:, 4 * t:4 * t + 4, :].rearrange("p b c -> p (b c)"), ALU.add).then_inc(d_x, 1)


_INS = ['x', 'ctx_768', 'L0_xattn_Wq', 'L0_xattn_Wk', 'L0_xattn_Wv', 'L0_xattn_Wo', 'L0_xattn_bo', 'L0_ffn_Wg',
        'L0_ffn_W1', 'L0_ffn_W2', 'L0_ffn_W3', 'L1_xattn_Wq', 'L1_xattn_bq', 'L1_xattn_Wk', 'L1_xattn_bk',
        'L1_xattn_Wv', 'L1_xattn_bv', 'L1_xattn_Wo', 'L1_xattn_bo', 'L1_ffn_k0', 'L1_ffn_k1', 'L1_ffn_k2',
        'L1_ffn_s0', 'L1_ffn_s1', 'L1_ffn_s2']


def kernel(**inputs):
    import numpy as _np
    import concourse.bacc as _bacc
    from concourse import mybir as _mybir
    from concourse.bass_utils import run_bass_kernel_spmd as _run

    nc = _bacc.Bacc("TRN2", target_bir_lowering=False, num_devices=1)
    arrays, args = {}, {}
    for name in _INS:
        v = _np.ascontiguousarray(inputs[name])
        if v.dtype == _np.bool_:
            v = v.view(_np.int32)
        v = v.reshape(v.shape or (1,))
        arrays[f"in_{name}"] = v
        args[name] = nc.dram_tensor(f"in_{name}", v.shape, _mybir.dt.from_np(v.dtype), kind="ExternalInput").ap()
    shape = inputs['x'].shape
    out = nc.dram_tensor("out_0", shape, _mybir.dt.float32, kind="ExternalOutput").ap()
    program(nc, args, out)
    r = _run(nc, [arrays], core_ids=[0])
    return r.results[0]["out_0"]
```

```python
from contextlib import ExitStack

import concourse.bass as bass
from concourse import mybir

F32 = mybir.dt.float32
F32R = mybir.dt.float32r
I32 = mybir.dt.int32
U32 = mybir.dt.uint32
U8 = mybir.dt.uint8
ALU = mybir.AluOpType
ACT = mybir.ActivationFunctionType
X = mybir.AxisListType.X

P = 128
NB = 8
NP = NB // 2
TG = 512
NT = NB * P // TG
C = 128
CK = 96
CK1 = CK + 1
H0, D0 = 8, 64
I0 = H0 * D0
NC0 = I0 // P
E = 8
HID = 256
NH = HID // P
H1, D1 = 16, 8
NG = 4
NS = 4
F1, F2 = 512, 512
EPS = 1e-5
RSQRT_SEED = 0x5F3759DF


def f32(ap):
    return ap.bitcast(F32)


def program(nc, a, out):
    with ExitStack() as ctx:
        def sb(name, shape, dt=F32):
            return ctx.enter_context(nc.sbuf_tensor(name, shape, dt))

        def sem(name):
            return ctx.enter_context(nc.semaphore(name))

        x_sb = sb("x_sb", [P, NB, C])
        ctx_sb = sb("ctx_sb", [P, NB, CK])
        ident = sb("ident", [P, P])
        ones = sb("ones", [P, P])
        zero = sb("zero", [P, 1])
        ctxT = sb("ctxT", [CK1, NB * P])
        ctxT_hi = sb("ctxT_hi", [CK1, NB * P], F32R)
        ctxT_lo = sb("ctxT_lo", [CK1, NB * P], F32R)
        stats = sb("stats", [P, NB, 6])
        meanvar = sb("meanvar", [P, NB, 2])
        ve = sb("ve", [P, NB])
        rs = sb("rs", [P, NB])
        nt = sb("nt", [P, NB])
        nu = sb("nu", [P, NB])
        nm = sb("nm", [P, NB])
        xn = sb("xn", [P, NB, C])
        xT_hi = sb("xT_hi", [P, NB * P], F32R)
        xT_lo = sb("xT_lo", [P, NB * P], F32R)

        w_raw = sb("w_raw", [P, 2, I0])
        wq0, wk0, w12 = w_raw[:, 0, :], w_raw[0:CK, 1, :], w_raw
        wq0_hi = sb("wq0_hi", [C, I0], F32R)
        wq0_lo = sb("wq0_lo", [C, I0], F32R)
        wk0_hi = sb("wk0_hi", [CK1, I0], F32R)
        wk0_lo = sb("wk0_lo", [CK1, I0], F32R)
        wv0 = sb("wv0", [CK, I0])
        wo0 = sb("wo0", [P, NC0, C])
        bo0 = sb("bo0", [P, C])
        kT0 = sb("kT0", [P, NC0, NB * P])
        v0 = sb("v0", [P, NB, I0])
        q_z = sb("q_z", [P, 2, NC0, 2 * P])
        q_ev, q_od = q_z[:, 0], q_z[:, 1]
        probs = sb("probs", [P, 2, H0, P])
        probsT = sb("probsT", [P, 2, H0, P])
        negmax = sb("negmax", [P, 2, H0])
        sums = sb("sums", [P, 2, H0])
        rsum = sb("rsum", [P, 2, H0])
        o_both = sb("o_both", [P, 2, 2, I0])
        o_sb, oT = o_both[:, 0], o_both[:, 1]

        wg = sb("wg", [C, E])
        lg = sb("lg", [P, NB, E])
        top = sb("top", [P, NB, 8])
        topi = sb("topi", [P, NB, 8], U32)
        topf = sb("topf", [P, NB, 8])
        iota_e = sb("iota_e", [P, NB, E])
        gd = sb("gd", [P, NB])
        ge = sb("ge", [P, NB])
        gs = sb("gs", [P, NB])
        gw = sb("gw", [P, 2, NB])
        pick = sb("pick", [P, 2, NB, E])
        picked = sb("picked", [P, 2, NB, E])
        comb = sb("comb", [P, E, NB])
        w12_hi = sb("w12_hi", [P, 2, 2 * HID], F32R)
        w12_lo = sb("w12_lo", [P, 2, 2 * HID], F32R)
        w3 = sb("w3", [P, 2, NH, C])

        wq1 = sb("wq1", [C, C])
        wq1_hi, wq1_lo = wq0_hi, wq0_lo
        wk1 = sb("wk1", [CK1, C])
        wk1_hi, wk1_lo = wk0_hi, wk0_lo
        wv1 = sb("wv1", [CK1, C])
        wo1 = sb("wo1", [C, C])
        bo1 = sb("bo1", [P, C])
        bq1 = sb("bq1", [2, C])
        bq1_r = sb("bq1_r", [2, C], F32R)
        bq1_p = sb("bq1_p", [2, C])
        bq1_s = sb("bq1_s", [2, NS * C], F32R)
        ones_r = sb("ones_r", [2, TG], F32R)
        block_of = sb("block_of", [P, 4])
        row_i = sb("row_i", [P, 1], I32)
        bit_i = sb("bit_i", [P, 3], I32)
        is_lo = sb("is_lo", [P, 3])
        sign = sb("sign", [P, 3])
        part = sb("part", [P, 2, TG], F32R)
        k_st = sb("k_st", [P, NG, NB * P], F32R)
        k_bd = sb("k_bd", [P, 2, NG, 4, P], F32R)
        q_st = sb("q_st", [P, 2, NG, P], F32R)
        negmax1 = sb("negmax1", [P, 4, 4])
        ov = sb("ov", [P, 2 * P])
        rsum1 = sb("rsum1", [P, H1])
        o1 = sb("o1", [P, C])
        o1T = sb("o1T", [P, C])

        k0_i = sb("k0_i", [P, 2, F1 // 4], I32)
        k1_i = sb("k1_i", [P, F1 // P, F2 // 4], I32)
        k2_i = sb("k2_i", [P, F2 // P, C // 4], I32)
        k0_u, k1_u, k2_u = (k[:, :, :].bitcast(U8) for k in (k0_i, k1_i, k2_i))
        d0_w = sb("d0_w", [P, F1], F32R)
        d1_w = sb("d1_w", [P, F1 // P, F2], F32R)
        d2_w = sb("d2_w", [P, F2 // P, C], F32R)
        scale = sb("scale", [P, 3])
        scale2 = sb("scale2", [P, 3])
        h_c = sb("h_c", [P, 2, F1 // P, TG], F32R)

        uT = kT0[:, 0:2, :].rearrange("p t (c n) -> p t c n", c=NH)
        silu = kT0[:, 2, :].rearrange("p (c n) -> p c n", c=NH)
        relu = silu
        xT = kT0[:, 3, :]
        v1 = v0[:, :, 0:C]
        v_bd = [z.rearrange("p (h c) -> p h c", c=P) for z in
                (q_z[:, :, :, :].rearrange("p a k n -> p (a k n)"), o_both[:, :, :, :].rearrange("p a k n -> p (a k n)"))]
        q_all = h_c[:, :, :, :].rearrange("p s k n -> p (s k n)").rearrange("p (g n) -> p g n", g=NG)
        sh1 = probs[:, :, :, :].rearrange("p j (a h) k -> p (j a) (h k)", a=2)
        sh1T = probsT[:, :, :, :].rearrange("p j (a h) k -> p (j a) (h k)", a=2)
        h_a = k_bd[:, :, :, :, :].rearrange("p s g h k -> p s g (h k)")
        h_b = k_st[:, :, :].rearrange("p (s g) (u n) -> p s (g u) n", s=2, u=2)
        h_at = {(0, 0): h_a, (0, 1): h_b, (1, 0): h_c, (1, 1): h_a}
        yT = oT[:, :, :]
        fin = o_sb[:, :, :]

        ps = ctx.enter_context(nc.psum_tensor("ps", [P, 8, 512], F32))
        M0 = 6

        ld_x, ld_ctx, ld_w0, ld_w1, ld_d = (sem(n) for n in ("ld_x", "ld_ctx", "ld_w0", "ld_w1", "ld_d"))
        ld_e = [sem("ld_e0"), sem("ld_e1")]
        stored = sem("stored")
        const_ok, zeros_ok, split_w0, split_w1, masks = (sem(n) for n in (
            "const_ok", "zeros_ok", "split_w0", "split_w1", "masks"))
        pool_step = sem("pool_step")
        ctxT_ps, ctxT_f, ctxT_h, ctxT_ok = (sem(n) for n in ("ctxT_ps", "ctxT_f", "ctxT_h", "ctxT_ok"))
        k0_ps, k0_ok, v0_ps, v0_ok = (sem(n) for n in ("k0_ps", "k0_ok", "v0_ps", "v0_ok"))
        ln_st, ln_mv, ln_nw, ln_rs, ln_xn, ln_ps, ln_hi, ln_lo, ln_f = (sem(n) for n in (
            "ln_st", "ln_mv", "ln_nw", "ln_rs", "ln_xn", "ln_ps", "ln_hi", "ln_lo", "ln_f"))
        xb0, xb1 = sem("xb0"), sem("xb1")
        a_q_ps, a_qe, a_qo, a_s, a_max, a_exp, a_pt_ps, a_pt_v, a_pt_a, a_o, a_rs, a_norm, a_oT_ps, a_oT, a_wo, a_x = (
            sem("a_" + n) for n in ("q_ps", "qe", "qo", "s", "max", "exp", "pt_ps", "pt_v", "pt_a", "o", "rs", "norm",
                                    "oT_ps", "oT", "wo", "x"))
        g_ps, g_lg, g_top, g_idx, g_f, g_d, g_e, g_s, g_w, g_pick, g_sel, g_ok = (
            sem("g_" + n) for n in ("ps", "lg", "top", "idx", "f", "d", "e", "s", "w", "pick", "sel", "ok"))
        b_hi, b_lo, b_h, b_g, b_silu, b_u, b_y, b_acc = (
            sem("b_" + n) for n in ("hi", "lo", "h", "g", "silu", "u", "y", "acc"))
        k1_ps, k1_part, k1_st, v1_ps, v1_ok = (sem(n) for n in ("k1_ps", "k1_part", "k1_st", "v1_ps", "v1_ok"))
        c_q_ps, c_part, c_q, c_kq, c_v, c_s, c_max, c_sub, c_exp, c_pt_ps, c_pt, c_o, c_ov, c_ovT, c_rs, c_norm, \
            c_oT_ps, c_oT, c_wo, c_x = (
                sem("c_" + n) for n in ("q_ps", "part", "q", "kq", "v", "s", "max", "sub", "exp", "pt_ps", "pt", "o",
                                        "ov", "ovT", "rs", "norm", "oT_ps", "oT", "wo", "x"))
        d_w, d_ps, d_relu, d_hi, d_lo, d_y, d_yT_ps, d_x = (
            sem("d_" + n) for n in ("w", "ps", "relu", "hi", "lo", "y", "yT_ps", "x"))

        A = a
        def stacked(ap):
            return ap[:, :].rearrange("c (h p d) -> c h p d", p=NS, d=D1)

        def repeated(ap):
            return ap[:, :].rearrange("c (h d) -> c h d", d=D1).unsqueeze(2).to_broadcast([ap.shape[0], H1, NS, D1])

        def row(ap, n):
            return ap.rearrange("(o c) -> o c", o=1).to_broadcast([n, ap.shape[0]])

        def diagonal(j, half, column):
            flat = v_bd[j].rearrange("p h c -> p (h c)")
            first = half * 8 * P + column
            return bass.AP(tensor=flat.tensor, offset=flat.offset + first, ap=[flat.ap[0], [P + 8, 8], [1, 8]])

        block = ctx.enter_context(nc.Block())

        @block.sync
        def _(sp):
            sp.dma_start(ctx_sb[:, :, :], A["ctx_768"].rearrange("b t c -> t b c")).then_inc(ld_ctx, 16)
            sp.dma_start(x_sb[:, :, :], A["x"].rearrange("b t c -> t b c")).then_inc(ld_x, 16)
            for dst, src in ((wk0, A["L0_xattn_Wk"]), (wq0, A["L0_xattn_Wq"]), (wv0[:, :], A["L0_xattn_Wv"]),
                             (wo0[:, :, :], A["L0_xattn_Wo"].rearrange("(k p) c -> p k c", p=P)),
                             (bo0[:, :], row(A["L0_xattn_bo"], P)), (wg[:, :], A["L0_ffn_Wg"])):
                sp.dma_start(dst, src).then_inc(ld_w0, 16)
            for dst, src in ((wq1[:, :], A["L1_xattn_Wq"]), (wk1[0:CK, :], A["L1_xattn_Wk"]),
                             (wk1[CK:CK1, :], row(A["L1_xattn_bk"], 1)), (wv1[0:CK, :], A["L1_xattn_Wv"]),
                             (wv1[CK:CK1, :], row(A["L1_xattn_bv"], 1)), (bq1[:, :], row(A["L1_xattn_bq"], 2)),
                             (wo1[:, :], A["L1_xattn_Wo"]), (bo1[:, :], row(A["L1_xattn_bo"], P))):
                sp.dma_start(dst, src).then_inc(ld_w1, 16)
            for dst, src in ((k0_i[:, :, :], A["L1_ffn_k0"].rearrange("(k p) c -> p k c", p=P)),
                             (k1_i[:, :, :], A["L1_ffn_k1"].rearrange("(k p) c -> p k c", p=P)),
                             (k2_i[:, :, :], A["L1_ffn_k2"].rearrange("(k p) c -> p k c", p=P)),
                             (scale[:, 0:1], row(A["L1_ffn_s0"], P)), (scale[:, 1:2], row(A["L1_ffn_s1"], P)),
                             (scale[:, 2:3], row(A["L1_ffn_s2"], P))):
                sp.dma_start(dst, src).then_inc(ld_d, 16)

            def load_expert(e, buf):
                sp.dma_start(w12[:, buf, 0:HID], A["L0_ffn_W1"][bass.ds(e, 1)].rearrange("o p h -> p (o h)")).then_inc(ld_e[buf], 16)
                sp.dma_start(w12[:, buf, HID:2 * HID], A["L0_ffn_W2"][bass.ds(e, 1)].rearrange("o p h -> p (o h)")).then_inc(ld_e[buf], 16)
                sp.dma_start(w3[:, buf, :, :], A["L0_ffn_W3"][bass.ds(e, 1)].rearrange("o (k p) c -> p (o k) c", p=P)).then_inc(ld_e[buf], 16)

            sp.wait_ge(split_w0, 2)
            load_expert(0, 0)
            load_expert(1, 1)
            with sp.Fori(1, E // 2) as i:
                for buf in range(2):
                    sp.wait_ge(b_y, i * 4 + (2 * buf - 2))
                    load_expert(i * 2 + buf, buf)
            for t in range(NT):
                sp.wait_ge(d_x, t + 1)
                sp.dma_start(out[t * 4:t * 4 + 4].rearrange("b t c -> t b c"),
                             fin[:, t, :].rearrange("p (b c) -> p b c", c=C)).then_inc(stored, 16)
            sp.wait_ge(stored, 16 * NT)

        @block.gpsimd
        def _(pool):
            step = [0]

            def chain(ins):
                step[0] += 1
                ins.then_inc(pool_step, 1)
                pool.wait_ge(pool_step, step[0])

            pool.memset(ones[:, :], 1.0).then_inc(const_ok, 1)
            chain(pool.memset(ident[:, :], 0.0))
            chain(pool.memset(zero[:, :], 0.0))
            pool.affine_select(out=ident[:, :], in_=ident[:, :], compare_op=ALU.not_equal, fill=1.0, base=0,
                               pattern=[[-1, P]], channel_multiplier=1).then_inc(const_ok, 1)
            pool.memset(q_z[:, :, :, :], 0.0).then_inc(zeros_ok, 1)
            pool.wait_ge(ld_w0, 16 * 6)
            for w, hi, lo in ((wk0, wk0_hi, wk0_lo), (wq0, wq0_hi, wq0_lo)):
                rows = w.shape[0]
                chain(pool.tensor_copy(hi[0:rows, :], w))
                pool.tensor_tensor(lo[0:rows, :], w, f32(hi[0:rows, :]), ALU.subtract).then_inc(split_w0, 1)
            pool.wait_ge(ld_x, 16)
            for b in range(NB):
                pool.wait_ge(ln_xn, b + 1)
                pool.tensor_tensor(x_sb[:, b, :], x_sb[:, b, :], bo0[:, :], ALU.add).then_inc(xb0, 1)
            chain(pool.iota(iota_e[:, :, :], [[0, NB], [1, E]], base=0, channel_multiplier=0,
                            allow_small_or_imprecise_dtypes=True))
            pool.iota(row_i[:, :], [[0, 1]], base=0, channel_multiplier=1).then_inc(const_ok, 1)
            pool.wait_ge(ld_w1, 16 * 8)
            def split_repeated(w, hi, lo):
                chain(pool.tensor_copy(stacked(hi), repeated(w)))
                pool.tensor_tensor(stacked(lo), repeated(w), stacked(f32(hi)), ALU.subtract).then_inc(split_w1, 1)

            pool.wait_ge(k0_ps, NC0 * NT)
            split_repeated(wk1, wk1_hi, wk1_lo)
            pool.memset(f32(ones_r[:, :]), 1.0).then_inc(split_w1, 1)
            chain(pool.memset(block_of[:, :], 1.0))
            chain(pool.affine_select(out=block_of[:, :], in_=block_of[:, :], compare_op=ALU.is_ge, fill=0.0, base=0,
                                     pattern=[[-32, 4]], channel_multiplier=1))
            chain(pool.affine_select(out=block_of[:, :], in_=block_of[:, :], compare_op=ALU.is_ge, fill=0.0, base=31,
                                     pattern=[[32, 4]], channel_multiplier=-1))
            def split_expert(e, buf):
                pool.wait_ge(ld_e[buf], (e - buf) * 24 + 48)
                if not isinstance(e, int) or e >= 2:
                    pool.wait_ge(b_y, e * 2 - 2)
                pool.tensor_tensor(w12_hi[:, buf, :], w12[:, buf, :], zero[:, :].to_broadcast([P, 2 * HID]),
                                   ALU.add).then_inc(b_hi, 1)
                pool.wait_ge(b_hi, e + 1)
                pool.tensor_tensor(w12_lo[:, buf, :], w12[:, buf, :], f32(w12_hi[:, buf, :]), ALU.subtract).then_inc(b_lo, 1)

            split_expert(0, 0)
            split_expert(1, 1)
            pool.wait_ge(ld_d, 16 * 6)
            pool.tensor_scalar(d1_w[:, :, :], k1_u[:, :, :], 2.0, -1.0, ALU.mult, ALU.add).then_inc(d_w, 1)
            pool.tensor_scalar(d2_w[:, :, :], k2_u[:, :, :], 2.0, -1.0, ALU.mult, ALU.add).then_inc(d_w, 1)
            pool.wait_ge(a_q_ps, 2 * NP)
            split_repeated(wq1, wq1_hi, wq1_lo)
            pool.wait_ge(a_wo, NB)
            for j in range(2):
                pool.memset(v_bd[j], 0.0).then_inc(zeros_ok, 1)
            for j in range(2):
                pool.wait_ge(zeros_ok, 2 + j)
                for half in range(2):
                    pool.memset(diagonal(j, half, 64), 1.0).then_inc(zeros_ok, 1)

            with pool.Fori(1, E // 2) as i:
                for buf in range(2):
                    split_expert(i * 2 + buf, buf)
            for b in range(NB):
                pool.wait_ge(ln_xn, 2 * NB + b + 1)
                pool.tensor_tensor(x_sb[:, b, :], x_sb[:, b, :], bo1[:, :], ALU.add).then_inc(xb1, 1)
            def stage_kq(b, j):
                keys = f32(k_st[:, :, bass.ds(b * P, P)]).unsqueeze(2).to_broadcast([P, NG, 4, P])
                blocks = block_of[:, :].unsqueeze(1).unsqueeze(3).to_broadcast([P, NG, 4, P])
                pool.tensor_tensor(k_bd[:, j, :, :, :], keys, blocks, ALU.mult).then_inc(c_kq, 1)
                pool.tensor_copy(q_st[:, j, :, :], f32(q_all[:, :, bass.ds(b * P, P)])).then_inc(c_kq, 1)

            def stage_v(b, j):
                for half in range(2):
                    src = v1[:, bass.ds(b, 1), 64 * half:64 * half + 64].rearrange("p o (h d) -> p (o h) d", d=D1)
                    pool.tensor_copy(diagonal(j, half, 0), src).then_inc(c_v, 1)

            pool.wait_ge(zeros_ok, 7)
            pool.wait_ge(v1_ok, NB)
            pool.wait_ge(k1_st, NG * NT)
            pool.wait_ge(c_q, NG * NT)
            for j in range(2):
                stage_kq(j, j)
                stage_v(j, j)
            with pool.Fori(1, NP) as p:
                pool.wait_ge(c_s, p * 8 - 4)
                stage_kq(p * 2, 0)
                pool.wait_ge(c_o, p * 8 - 4)
                stage_v(p * 2, 0)
                pool.wait_ge(c_s, p * 8)
                stage_kq(p * 2 + 1, 1)
                pool.wait_ge(c_o, p * 8)
                stage_v(p * 2 + 1, 1)

        @block.tensor
        def _(pe):
            def split3(dst, w_hi, w_lo, x_hi, x_lo, start=True, stop=True):
                pe.matmul(dst, w_hi, x_hi, start=start, stop=False)
                pe.matmul(dst, w_hi, x_lo, start=False, stop=False)
                return pe.matmul(dst, w_lo, x_hi, start=False, stop=stop)

            def ln_transposes(s):
                for b in range(NB):
                    pe.wait_ge(ln_xn, NB * s + b + 1)
                    ins = pe.transpose(ps[:, M0 + b // 4, (b % 4) * P:(b % 4 + 1) * P], xn[:, b, :], ident[:, :])
                    if b % 4 == 3:
                        ins.then_inc(ln_ps, 1)

            pe.wait_ge(const_ok, 2)
            pe.wait_ge(ld_ctx, 16)
            for b in range(NB):
                ins = pe.transpose(ps[0:CK, b // 4, (b % 4) * P:(b % 4 + 1) * P], ctx_sb[:, b, :], ident[:, :])
                if b % 4 == 3:
                    ins.then_inc(ctxT_ps, 1)
            ln_transposes(0)
            pe.wait_ge(split_w0, 2)
            for n in range(NC0 * NT):
                k, t = n // NT, n % NT
                pe.wait_ge(ctxT_ok, t + 1)
                if n >= 2:
                    pe.wait_ge(k0_ok, n - 1)
                sl = slice(t * TG, (t + 1) * TG)
                split3(ps[:, 2 + n % 2, :], wk0_hi[0:CK, k * P:(k + 1) * P], wk0_lo[0:CK, k * P:(k + 1) * P],
                       ctxT_hi[0:CK, sl], ctxT_lo[0:CK, sl]).then_inc(k0_ps, 1)
            for b in range(NB):
                if b >= 2:
                    pe.wait_ge(v0_ok, b - 1)
                pe.matmul(ps[:, 4 + b % 2, :], ctxT[0:CK, b * P:(b + 1) * P], wv0[:, :],
                          start=True, stop=True).then_inc(v0_ps, 1)

            def a_queries(p):
                for m in range(2):
                    for k in (2 * m, 2 * m + 1):
                        ins = split3(ps[:, M0 + m, (k % 2) * 2 * P:(k % 2 + 1) * 2 * P],
                                     wq0_hi[:, k * P:(k + 1) * P], wq0_lo[:, k * P:(k + 1) * P],
                                     xT_hi[:, bass.ds(p * 2 * P, 2 * P)], xT_lo[:, bass.ds(p * 2 * P, 2 * P)])
                    ins.then_inc(a_q_ps, 1)

            def a_scores(p, j):
                for h in range(H0):
                    q = (q_ev if h % 2 == 0 else q_od)[:, h // 2, j * P:(j + 1) * P]
                    ins = pe.matmul(ps[:, 2 * j + h // 4, (h % 4) * P:(h % 4 + 1) * P], q,
                                    kT0[:, h // 2, bass.ds(p * 2 * P + j * P, P)], start=True, stop=True)
                ins.then_inc(a_s, 1)

            def a_probs_turn(p, j):
                pe.wait_ge(a_exp, p * 2 + j + 1)
                for h in range(H0):
                    ins = pe.transpose(ps[:, 4 + h // 4, (h % 4) * P:(h % 4 + 1) * P], probs[:, j, h, :], ident[:, :])
                ins.then_inc(a_pt_ps, 1)

            def a_values(p, j):
                pe.wait_ge(a_pt_v, p * 3 + 2 + j)
                if j == 1:
                    pe.wait_ge(a_pt_a, p + 1)
                for h in range(H0):
                    ins = pe.matmul(ps[:, 2 * j, h * D0:(h + 1) * D0], probsT[:, j, h, :],
                                    v0[:, bass.ds(p * 2 + j, 1), h * D0:(h + 1) * D0].rearrange("p o d -> p (o d)"),
                                    start=True, stop=True)
                ins.then_inc(a_o, 1)

            def a_out_turn(p, j):
                pe.wait_ge(a_norm, p * 2 + j + 1)
                for k in range(NC0):
                    ins = pe.transpose(ps[:, M0 + j, k * P:(k + 1) * P], o_sb[:, j, k * P:(k + 1) * P], ident[:, :])
                ins.then_inc(a_oT_ps, 1)

            def a_out(p, j):
                pe.wait_ge(a_oT, p * 2 + j + 1)
                for k in range(NC0):
                    ins = pe.matmul(ps[:, M0 + j, 0:C], oT[:, j, k * P:(k + 1) * P], wo0[:, k, :],
                                    start=(k == 0), stop=(k == NC0 - 1))
                ins.then_inc(a_wo, 1)

            def a_step(p, last):
                a_probs_turn(p, 0)
                a_values(p, 0)
                if not last:
                    a_queries(p + 1)
                a_probs_turn(p, 1)
                a_values(p, 1)
                if not last:
                    pe.wait_ge(a_qe, p * 2 + 4)
                    pe.wait_ge(a_qo, p * 2 + 4)
                    pe.wait_ge(a_norm, p * 2 + 1)
                    a_scores(p + 1, 0)
                a_out_turn(p, 0)
                a_out_turn(p, 1)
                if not last:
                    a_scores(p + 1, 1)
                a_out(p, 0)
                a_out(p, 1)

            pe.wait_ge(ln_lo, NT)
            pe.wait_ge(ln_hi, NT)
            a_queries(0)
            pe.wait_ge(k0_ok, NC0 * NT)
            pe.wait_ge(a_qe, 2)
            pe.wait_ge(a_qo, 2)
            pe.wait_ge(zeros_ok, 1)
            a_scores(0, 0)
            a_scores(0, 1)
            pe.wait_ge(v0_ok, NB)
            with pe.Fori(0, NP - 1) as p:
                a_step(p, False)
            a_step(NP - 1, True)

            pe.wait_ge(split_w1, 3)
            for n in range(NG * NT):
                g, t = n // NT, n % NT
                if n >= 4:
                    pe.wait_ge(k1_st, n - 3)
                sl = slice(t * TG, (t + 1) * TG)
                split3(ps[:, n % 4, :], wk1_hi[:, g * P:(g + 1) * P], wk1_lo[:, g * P:(g + 1) * P], ctxT_hi[:, sl], ctxT_lo[:, sl]).then_inc(k1_ps, 1)
            for b in range(NB):
                if b >= 2:
                    pe.wait_ge(v1_ok, b - 1)
                pe.matmul(ps[:, 4 + b % 2, 0:C], ctxT[:, b * P:(b + 1) * P], wv1[:, :],
                          start=True, stop=True).then_inc(v1_ps, 1)

            ln_transposes(1)
            pe.wait_ge(ln_f, NT)
            for b in range(NB):
                ins = pe.matmul(ps[:, 4, b * E:(b + 1) * E], xT[:, b * P:(b + 1) * P], wg[:, :], start=True, stop=True)
            ins.then_inc(g_ps, 1)

            def b_hidden(e, buf, t):
                for c in range(NH):
                    v = e * (NT * NH) + t * NH + c
                    if not (isinstance(e, int) and e == 0 and t == 0):
                        pe.wait_ge(b_u, v - 1)
                    sl = slice(t * TG, (t + 1) * TG)
                    for half, bank, s in ((0, c, b_h), (HID, 2 + c, b_g)):
                        w = slice(half + c * P, half + (c + 1) * P)
                        split3(ps[:, bank, :], w12_hi[:, buf, w], w12_lo[:, buf, w],
                               xT_hi[:, sl], xT_lo[:, sl]).then_inc(s, 1)

            def b_down(e, buf, t):
                pe.wait_ge(b_u, e * 4 + t * 2 + 2)
                for k in range(4):
                    for c in range(NH):
                        ins = pe.matmul(ps[:, 4 + t, k * C:(k + 1) * C], uT[:, t, c, k * P:(k + 1) * P],
                                        w3[:, buf, c, :], start=(c == 0), stop=(c == NH - 1))
                ins.then_inc(b_y, 1)

            def b_step(e, last):
                b_hidden(e, 0, 1)
                b_down(e, 0, 0)
                pe.wait_ge(b_lo, e + 2)
                b_hidden(e + 1, 1, 0)
                b_down(e, 0, 1)
                b_hidden(e + 1, 1, 1)
                b_down(e + 1, 1, 0)
                if not last:
                    pe.wait_ge(b_lo, e + 3)
                    b_hidden(e + 2, 0, 0)
                b_down(e + 1, 1, 1)

            pe.wait_ge(ln_lo, 2 * NT)
            pe.wait_ge(b_lo, 1)
            pe.wait_ge(v1_ok, NB)
            b_hidden(0, 0, 0)
            pe.wait_ge(g_lg, 1)
            with pe.Fori(0, E // 2 - 1) as i:
                b_step(i * 2, False)
            b_step(E - 2, True)

            ln_transposes(2)

            def c_scores(p, u):
                n = p * 8 + u
                j, g = u % 8 // 4, u % 4
                if g == 0:
                    pe.wait_ge(c_kq, p * 4 + (u // 4 * 2 + 2))
                if not (isinstance(p, int) and n < 4):
                    pe.wait_ge(c_sub, n - 3)
                pe.matmul(ps[:, g, :], q_st[:, j, g, :], k_bd[:, j, g, :, :].rearrange("p h k -> p (h k)"),
                          start=True, stop=True).then_inc(c_s, 1)

            def c_turn(p, u):
                pe.wait_ge(c_exp, p * 8 + (u + 1))
                for h in range(4):
                    ins = pe.transpose(ps[:, 4 + u % 2, h * P:(h + 1) * P], sh1[:, u % 4, h * P:(h + 1) * P], ident[:, :])
                ins.then_inc(c_pt_ps, 1)

            def c_values(p, u, first):
                j, half = u // 4, u % 4 // 2
                pe.wait_ge(c_pt, p * 8 + (u + 1))
                if u % 4 == 0:
                    pe.wait_ge(c_v, p * 4 + (2 * j + 2))
                    if not (first and isinstance(p, int)):
                        pe.wait_ge(c_x, p * 2 + (j - 1))
                for h in range(4):
                    hh = 4 * (u % 4) + h
                    ins = pe.matmul(ps[:, M0 + j, half * P:(half + 1) * P], v_bd[j][:, hh, :],
                                    sh1T[:, u % 4, h * P:(h + 1) * P], start=(hh % 8 == 0), stop=(hh % 8 == 7))
                ins.then_inc(c_o, 1)

            def c_tail(b, j, stage):
                if stage == 0:
                    pe.wait_ge(c_ov, b + 1)
                    for half in range(2):
                        ins = pe.transpose(ps[:, M0 + j, (2 + half) * P:(3 + half) * P], ov[:, half * P:(half + 1) * P],
                                           ident[:, :])
                    ins.then_inc(c_ovT, 1)
                elif stage == 1:
                    pe.wait_ge(c_norm, b + 1)
                    pe.transpose(ps[:, M0 + j, 0:P], o1[:, :], ident[:, :]).then_inc(c_oT_ps, 1)
                else:
                    pe.wait_ge(c_oT, b + 1)
                    pe.matmul(ps[:, M0 + j, P:P + C], o1T[:, :], wo1[:, :], start=True, stop=True).then_inc(c_wo, 1)

            def c_step(p, first, last):
                for u in range(8):
                    if not (last and u + 3 >= 8):
                        c_scores(p, u + 3)
                    if not (last and u == 7):
                        c_turn(p, u + 1)
                    c_values(p, u, first)
                    if u < 3 and not first:
                        c_tail(p * 2 - 1, 1, u)
                    if 4 <= u < 7:
                        c_tail(p * 2, 0, u - 4)

            pe.wait_ge(masks, 10)
            for n in range(NG * NT):
                g, t = n // NT, n % NT
                pe.wait_ge(ln_lo, 2 * NT + t + 1)
                pe.wait_ge(ln_hi, 2 * NT + t + 1)
                if n >= 4:
                    pe.wait_ge(c_q, n - 3)
                gs, sl = slice(g * P, (g + 1) * P), slice(t * TG, (t + 1) * TG)
                split3(ps[:, n % 4, :], wq1_hi[:, gs], wq1_lo[:, gs], xT_hi[:, sl], xT_lo[:, sl], stop=False)
                pe.matmul(ps[:, n % 4, :], bq1_s[:, gs], ones_r[:, :], start=False, stop=True).then_inc(c_q_ps, 1)
            pe.wait_ge(c_q, NG * NT)
            for u in range(3):
                c_scores(0, u)
            c_turn(0, 0)
            c_step(0, True, False)
            with pe.Fori(1, NP - 1) as p:
                c_step(p, False, False)
            c_step(NP - 1, False, True)
            for stage in range(3):
                c_tail(NB - 1, 1, stage)

            ln_transposes(3)
            pe.wait_ge(d_w, 3)
            n = 0
            for layer in range(3):
                for t in range(NT):
                    sl = slice(t * TG, (t + 1) * TG)
                    for m in range(4 if layer < 2 else 1):
                        ms = slice(m * P, (m + 1) * P)
                        if layer == 0:
                            pe.wait_ge(ln_lo, 3 * NT + t + 1)
                            pe.wait_ge(ln_hi, 3 * NT + t + 1)
                            terms = [(d0_w[:, ms], xx[:, sl]) for xx in (xT_hi, xT_lo)]
                        else:
                            pe.wait_ge(d_lo, 8 * (layer - 1) + 4 * t + 4)
                            w = d1_w if layer == 1 else d2_w
                            h = h_at[layer - 1, t]
                            terms = [(w[:, k, ms], h[:, part, k, :]) for k in range(4) for part in range(2)]
                        if n >= 4:
                            pe.wait_ge(d_relu, n - 3)
                        for i, (w_, x_) in enumerate(terms):
                            ins = pe.matmul(ps[:, n % 4, :], w_, x_, start=(i == 0), stop=(i == len(terms) - 1))
                        ins.then_inc(d_ps, 1)
                        n += 1
            for t in range(NT):
                pe.wait_ge(d_relu, 16 + t + 1)
                for k in range(4):
                    ins = pe.transpose(ps[:, 4 + t, k * P:(k + 1) * P], yT[:, t, k * P:(k + 1) * P], ident[:, :])
                ins.then_inc(d_yT_ps, 1)

        @block.scalar
        def _(act):
            def ln_hi_copy(s, plain):
                for t in range(NT):
                    act.wait_ge(ln_ps, NT * s + t + 1)
                    sl = slice(t * TG, (t + 1) * TG)
                    act.activation(xT_hi[:, sl], ps[:, M0 + t, :], ACT.Copy).then_inc(ln_hi, 1)
                    if plain:
                        act.activation(xT[:, sl], ps[:, M0 + t, :], ACT.Copy).then_inc(ln_f, 1)

            for t in range(NT):
                act.wait_ge(ctxT_ps, t + 1)
                act.activation(ctxT[0:CK, t * TG:(t + 1) * TG], ps[0:CK, t, :], ACT.Copy).then_inc(ctxT_f, 1)
            act.wait_ge(const_ok, 1)
            for t in range(NT):
                for k in range(4):
                    ins = act.activation(ctxT[CK:CK1, t * TG + k * P:t * TG + (k + 1) * P], ones[CK:CK1, :], ACT.Copy)
                ins.then_inc(ctxT_f, 1)
            act.wait_ge(ctxT_f, 2 * NT)
            for t in range(NT):
                sl = slice(t * TG, (t + 1) * TG)
                act.activation(ctxT_hi[:, sl], ctxT[:, sl], ACT.Copy).then_inc(ctxT_h, 1)
            ln_hi_copy(0, False)
            for b in range(NB):
                act.wait_ge(v0_ps, b + 1)
                act.activation(v0[:, b, :], ps[:, 4 + b % 2, :], ACT.Copy).then_inc(v0_ok, 1)

            def a_query_copy(n):
                act.wait_ge(zeros_ok, 1)
                for m in range(2):
                    act.wait_ge(a_q_ps, n + m + 1)
                    act.activation(q_od[64:P, 2 * m:2 * m + 2, :],
                                   ps[64:P, M0 + m, :].rearrange("p (k t) -> p k t", k=2), ACT.Copy,
                                   scale=D0 ** -0.5).then_inc(a_qo, 1)

            def a_exp_heads(p, j):
                act.wait_ge(a_max, p * 2 + j + 1)
                for h in range(H0):
                    ins = act.activation(probs[:, j, h, :], ps[:, 2 * j + h // 4, (h % 4) * P:(h % 4 + 1) * P], ACT.Exp,
                                         bias=negmax[:, j, h:h + 1], scale=1.0, accum_out=sums[:, j, h:h + 1])
                ins.then_inc(a_exp, 1)

            def a_oT_copy(p, j):
                act.wait_ge(a_oT_ps, p * 2 + j + 1)
                act.activation(oT[:, j, :], ps[:, M0 + j, :], ACT.Copy).then_inc(a_oT, 1)

            def a_step(p, last):
                a_exp_heads(p, 1)
                if not last:
                    a_query_copy(p * 2 + 2)
                act.wait_ge(a_pt_ps, p * 2 + 2)
                act.activation(probsT[:, 1, 4:8, :].rearrange("p h k -> p (h k)"), ps[:, 5, :], ACT.Copy).then_inc(a_pt_a, 1)
                a_oT_copy(p, 0)
                a_oT_copy(p, 1)
                if not last:
                    a_exp_heads(p + 1, 0)

            a_query_copy(0)
            a_exp_heads(0, 0)
            with act.Fori(0, NP - 1) as p:
                a_step(p, False)
            a_step(NP - 1, True)

            act.wait_ge(masks, 10)
            for n in range(NG * NT):
                act.wait_ge(k1_ps, n + 1)
                if n >= 2:
                    act.wait_ge(k1_st, n - 1)
                act.activation(part[:, n % 2, :], ps[:, n % 4, :], ACT.Copy, scale=sign[:, 1:2]).then_inc(k1_part, 1)
            for b in range(NB):
                act.wait_ge(v1_ps, b + 1)
                act.activation(v1[:, b, :], ps[:, 4 + b % 2, 0:C], ACT.Copy).then_inc(v1_ok, 1)
            ln_hi_copy(1, True)
            act.wait_ge(g_d, 1)
            act.activation(ge[:, :], gd[:, :], ACT.Exp).then_inc(g_e, 1)

            def b_silu_step(e):
                for c in range(4):
                    v = e * 4 + c
                    act.wait_ge(b_h, v + 1)
                    if not (isinstance(e, int) and e == 0 and c < 2):
                        act.wait_ge(b_u, v - 1)
                    act.activation(silu[:, c % 2, :], ps[:, c % 2, :], ACT.Silu).then_inc(b_silu, 1)

            b_silu_step(0)
            with act.Fori(1, E) as e:
                b_silu_step(e)

            ln_hi_copy(2, False)

            for n in range(NG * NT):
                act.wait_ge(c_q_ps, n + 1)
                if n >= 2:
                    act.wait_ge(c_q, n - 1)
                act.activation(part[:, n % 2, :], ps[:, n % 4, :], ACT.Copy, scale=sign[:, 0:1]).then_inc(c_part, 1)

            def c_exp_unit(p, u):
                act.wait_ge(c_sub, p * 8 + (u + 1))
                act.activation(sh1[:, u % 4, :], sh1[:, u % 4, :], ACT.Exp, scale=D1 ** -0.5).then_inc(c_exp, 1)

            def c_turn_copy(p, u):
                act.wait_ge(c_pt_ps, p * 8 + (u + 1))
                act.activation(sh1T[:, u % 4, :], ps[:, 4 + u % 2, :], ACT.Copy).then_inc(c_pt, 1)

            def c_tail(b, j, stage):
                if stage == 0:
                    act.wait_ge(c_o, b * 4 + 4)
                    act.activation(ov[:, :], ps[:, M0 + j, 0:2 * P], ACT.Copy).then_inc(c_ov, 1)
                elif stage == 2:
                    act.wait_ge(c_oT_ps, b + 1)
                    act.activation(o1T[:, :], ps[:, M0 + j, 0:P], ACT.Copy).then_inc(c_oT, 1)

            def c_step(p, first, last):
                for u in range(8):
                    if u < 3 and not first:
                        c_tail(p * 2 - 1, 1, u)
                    if 4 <= u < 7:
                        c_tail(p * 2, 0, u - 4)
                    if not (last and u + 2 >= 8):
                        c_exp_unit(p, u + 2)
                    if not (last and u == 7):
                        c_turn_copy(p, u + 1)

            c_exp_unit(0, 0)
            c_exp_unit(0, 1)
            c_turn_copy(0, 0)
            c_step(0, True, False)
            with act.Fori(1, NP - 1) as p:
                c_step(p, False, False)
            c_step(NP - 1, False, True)
            for stage in range(3):
                c_tail(NB - 1, 1, stage)

            ln_hi_copy(3, False)
            act.wait_ge(d_w, 3)
            for n in range(16):
                act.wait_ge(d_ps, n + 1)
                if n >= 2:
                    act.wait_ge(d_lo, n - 1)
                act.activation(relu[:, n % 2, :], ps[:, n % 4, :], ACT.Relu, scale=scale2[:, n // 8:n // 8 + 1]).then_inc(d_relu, 1)
            for t in range(NT):
                act.wait_ge(d_ps, 16 + t + 1)
                act.activation(yT[:, t, :], ps[:, t, :], ACT.Copy, scale=scale[:, 2:3]).then_inc(d_relu, 1)

        @block.vector
        def _(dve):
            nwt = [0]

            def ln(s):
                def newton(ins):
                    nwt[0] += 1
                    ins.then_inc(ln_nw, 1)
                    dve.wait_ge(ln_nw, nwt[0])

                for b in range(NB):
                    dve.bn_stats(stats[:, b, :], x_sb[:, b, :]).then_inc(ln_st, 1)
                for b in range(NB):
                    dve.wait_ge(ln_st, NB * s + b + 1)
                    dve.bn_aggr(meanvar[:, b, :], stats[:, b, :]).then_inc(ln_mv, 1)
                dve.wait_ge(ln_mv, NB * (s + 1))
                newton(dve.tensor_scalar(ve[:, :], meanvar[:, :, 1], EPS, None, ALU.add))
                newton(dve.tensor_scalar(nt[:, :].bitcast(I32), ve[:, :].bitcast(I32), 1, None, ALU.logical_shift_right))
                newton(dve.tensor_scalar(rs[:, :].bitcast(I32), nt[:, :].bitcast(I32), -1.0, float(RSQRT_SEED), ALU.mult, ALU.add))
                for _ in range(3):
                    newton(dve.tensor_tensor(nt[:, :], rs[:, :], rs[:, :], ALU.mult))
                    newton(dve.scalar_tensor_tensor(nu[:, :], nt[:, :], -0.5, ve[:, :], ALU.mult, ALU.mult))
                    newton(dve.scalar_tensor_tensor(rs[:, :], nu[:, :], 1.5, rs[:, :], ALU.add, ALU.mult))
                for b in range(NB):
                    dve.tensor_scalar(xn[:, b, :], x_sb[:, b, :], meanvar[:, b, 0:1], rs[:, b:b + 1],
                                      ALU.subtract, ALU.mult).then_inc(ln_xn, 1)
                if s == 0:
                    ctx_lo()
                for t in range(NT):
                    dve.wait_ge(ln_hi, NT * s + t + 1)
                    if s == 1:
                        dve.wait_ge(ln_f, t + 1)
                    sl = slice(t * TG, (t + 1) * TG)
                    dve.tensor_tensor(xT_lo[:, sl], ps[:, M0 + t, :], f32(xT_hi[:, sl]), ALU.subtract).then_inc(ln_lo, 1)

            def ctx_lo():
                for t in range(NT):
                    dve.wait_ge(ctxT_h, t + 1)
                    sl = slice(t * TG, (t + 1) * TG)
                    dve.tensor_tensor(ctxT_lo[:, sl], ctxT[:, sl], f32(ctxT_hi[:, sl]), ALU.subtract).then_inc(ctxT_ok, 1)

            dve.wait_ge(ld_x, 16)
            ln(0)
            for n in range(NC0 * NT):
                k, t = n // NT, n % NT
                dve.wait_ge(k0_ps, n + 1)
                dve.tensor_copy(kT0[:, k, t * TG:(t + 1) * TG], ps[:, 2 + n % 2, :]).then_inc(k0_ok, 1)

            def a_query_copy(n):
                for m in range(2):
                    dve.wait_ge(a_q_ps, n + m + 1)
                    dve.tensor_scalar(q_ev[0:64, 2 * m:2 * m + 2, :],
                                      ps[0:64, M0 + m, :].rearrange("p (k t) -> p k t", k=2), D0 ** -0.5, None,
                                      ALU.mult).then_inc(a_qe, 1)

            def a_rowmax(p, j):
                dve.wait_ge(a_s, p * 2 + j + 1)
                dve.tensor_reduce(negmax[:, j, :], ps[:, 2 * j:2 * j + 2, :].rearrange("p a (h k) -> p (a h) k", k=P),
                                  X, ALU.max, negate=True).then_inc(a_max, 1)

            def a_probsT_copy(p, j):
                dve.wait_ge(a_pt_ps, p * 2 + j + 1)
                for m in range(2 - j):
                    dve.tensor_copy(probsT[:, j, 4 * m:4 * m + 4, :].rearrange("p h k -> p (h k)"),
                                    ps[:, 4 + m, :]).then_inc(a_pt_v, 1)

            def a_normalise(p, j):
                dve.wait_ge(a_exp, p * 2 + j + 1)
                dve.reciprocal(rsum[:, j, :], sums[:, j, :]).then_inc(a_rs, 1)
                dve.wait_ge(a_rs, p * 2 + j + 1)
                dve.wait_ge(a_o, p * 2 + j + 1)
                dve.tensor_tensor(o_sb[:, j, :].rearrange("p (h d) -> p h d", d=D0),
                                  ps[:, 2 * j, :].rearrange("p (h d) -> p h d", d=D0),
                                  rsum[:, j, :].unsqueeze(2).to_broadcast([P, H0, D0]), ALU.mult).then_inc(a_norm, 1)

            def a_residual(p, j):
                dve.wait_ge(a_wo, p * 2 + j + 1)
                xs = x_sb[:, bass.ds(p * 2 + j, 1), :].rearrange("p o c -> p (o c)")
                dve.tensor_tensor(xs, ps[:, M0 + j, 0:C], xs, ALU.add).then_inc(a_x, 1)

            def a_step(p, last):
                a_probsT_copy(p, 0)
                if not last:
                    a_query_copy(p * 2 + 2)
                a_normalise(p, 0)
                a_probsT_copy(p, 1)
                a_normalise(p, 1)
                if not last:
                    a_rowmax(p + 1, 0)
                    a_rowmax(p + 1, 1)
                a_residual(p, 0)
                a_residual(p, 1)

            a_query_copy(0)
            a_rowmax(0, 0)
            a_rowmax(0, 1)
            dve.wait_ge(xb0, NB)
            with dve.Fori(0, NP - 1) as p:
                a_step(p, False)
            a_step(NP - 1, True)

            dve.wait_ge(ld_d, 16 * 6)
            dve.tensor_tensor(d0_w[:, :], k0_u[:, 0, :], k0_u[:, 1, :], ALU.subtract).then_inc(d_w, 1)
            dve.tensor_scalar(scale2[:, :], scale[:, :], 2.0, None, ALU.mult).then_inc(masks, 1)
            dve.wait_ge(masks, 1)
            dve.tensor_scalar(scale2[:, 0:1], scale2[:, 0:1], 2.0, None, ALU.mult).then_inc(masks, 1)
            dve.wait_ge(const_ok, 3)
            dve.tensor_scalar(bit_i[:, 0:1], row_i[:, :], 4, 1, ALU.logical_shift_right, ALU.bitwise_and).then_inc(masks, 1)
            dve.tensor_scalar(bit_i[:, 1:2], row_i[:, :], 3, 1, ALU.logical_shift_right, ALU.bitwise_and).then_inc(masks, 1)
            dve.tensor_scalar(bit_i[:, 2:3], row_i[:, :], 0, 1, ALU.logical_shift_right, ALU.bitwise_and).then_inc(masks, 1)
            dve.wait_ge(masks, 5)
            dve.tensor_copy(is_lo[:, :], bit_i[:, :]).then_inc(masks, 1)
            dve.wait_ge(masks, 6)
            dve.tensor_scalar(sign[:, :], is_lo[:, :], -2.0, 1.0, ALU.mult, ALU.add).then_inc(masks, 1)
            dve.wait_ge(masks, 7)
            dve.wait_ge(ld_w1, 16 * 8)
            dve.tensor_scalar(bq1_r[:, :], bq1[:, :], sign[0:2, 2:3], None, ALU.mult).then_inc(masks, 1)
            dve.wait_ge(masks, 8)
            dve.scalar_tensor_tensor(bq1_p[:, :], bq1[:, :], is_lo[0:2, 2:3], f32(bq1_r[:, :]), ALU.mult, ALU.add).then_inc(masks, 1)
            dve.wait_ge(masks, 9)
            dve.tensor_copy(stacked(bq1_s), repeated(bq1_p)).then_inc(masks, 1)
            for n in range(NG * NT):
                dve.wait_ge(k1_part, n + 1)
                dve.scalar_tensor_tensor(k_st[:, n // NT, (n % NT) * TG:(n % NT + 1) * TG], ps[:, n % 4, :], is_lo[:, 1:2], f32(part[:, n % 2, :]),
                                         ALU.mult, ALU.add).then_inc(k1_st, 1)

            dve.wait_ge(a_x, NB)
            ln(1)
            dve.wait_ge(g_ps, 1)
            dve.tensor_copy(lg[:, :, :].rearrange("p b e -> p (b e)"), ps[:, 4, 0:NB * E]).then_inc(g_lg, 1)
            dve.wait_ge(g_lg, 1)
            for b in range(NB):
                dve.max(top[:, b, :], lg[:, b, :]).then_inc(g_top, 1)
            for b in range(NB):
                dve.wait_ge(g_top, b + 1)
                dve.max_index(topi[:, b, :], top[:, b, :], lg[:, b, :]).then_inc(g_idx, 1)
            dve.wait_ge(g_top, NB)
            dve.tensor_tensor(gd[:, :], top[:, :, 1], top[:, :, 0], ALU.subtract).then_inc(g_d, 1)
            dve.wait_ge(g_idx, NB)
            dve.tensor_copy(topf[:, :, :], topi[:, :, :]).then_inc(g_f, 1)
            dve.wait_ge(g_e, 1)
            dve.tensor_scalar(gs[:, :], ge[:, :], 1.0, None, ALU.add).then_inc(g_s, 1)
            dve.wait_ge(g_s, 1)
            dve.reciprocal(gw[:, 0, :], gs[:, :]).then_inc(g_w, 1)
            dve.wait_ge(g_w, 1)
            dve.tensor_tensor(gw[:, 1, :], gw[:, 0, :], ge[:, :], ALU.mult).then_inc(g_w, 1)
            dve.wait_ge(g_f, 1)
            dve.wait_ge(g_w, 2)
            for k in range(2):
                dve.tensor_tensor(pick[:, k, :, :], iota_e[:, :, :], topf[:, :, k:k + 1].to_broadcast([P, NB, E]),
                                  ALU.is_equal).then_inc(g_pick, 1)
            for k in range(2):
                dve.wait_ge(g_pick, k + 1)
                dve.tensor_tensor(picked[:, k, :, :], pick[:, k, :, :], gw[:, k, :].unsqueeze(2).to_broadcast([P, NB, E]),
                                  ALU.mult).then_inc(g_sel, 1)
            dve.wait_ge(g_sel, 2)
            dve.tensor_tensor(comb[:, :, :].rearrange("p e b -> p b e"), picked[:, 0, :, :], picked[:, 1, :, :],
                              ALU.add).then_inc(g_ok, 1)

            def b_gate(e, t):
                for c in range(NH):
                    v = e * 4 + (2 * t + c)
                    dve.wait_ge(b_silu, v + 1)
                    dve.wait_ge(b_g, v + 1)
                    if not isinstance(e, int) or e > 0:
                        dve.wait_ge(b_y, e * 2 + t - 1)
                    dve.tensor_tensor(uT[:, t, c, :], ps[:, 2 + c, :], silu[:, c, :], ALU.mult).then_inc(b_u, 1)

            def b_add(e, t):
                dve.wait_ge(b_y, e * 2 + t + 1)
                if not isinstance(e, int) or e > 0:
                    dve.wait_ge(b_acc, e * 2 + t - 1)
                for k in range(4):
                    b = 4 * t + k
                    ins = dve.scalar_tensor_tensor(x_sb[:, b, :], ps[:, 4 + t, k * C:(k + 1) * C],
                                                   comb[:, bass.ds(e, 1), b:b + 1].rearrange("p o b -> p (o b)"),
                                                   x_sb[:, b, :], ALU.mult, ALU.add)
                ins.then_inc(b_acc, 1)

            dve.wait_ge(g_ok, 1)
            b_gate(0, 0)
            b_gate(0, 1)
            b_add(0, 0)
            with dve.Fori(1, E) as e:
                b_gate(e, 0)
                b_add(e - 1, 1)
                b_gate(e, 1)
                b_add(e, 0)
            b_add(E - 1, 1)

            dve.wait_ge(b_acc, 2 * E)
            ln(2)

            for n in range(NG * NT):
                dve.wait_ge(c_part, n + 1)
                dve.scalar_tensor_tensor(q_all[:, n // NT, (n % NT) * TG:(n % NT + 1) * TG], ps[:, n % 4, :],
                                         is_lo[:, 0:1], f32(part[:, n % 2, :]), ALU.mult, ALU.add).then_inc(c_q, 1)

            def c_shift(p, u):
                n = p * 8 + u
                dve.wait_ge(c_s, n + 1)
                src = ps[:, u % 4, :].rearrange("p (h k) -> p h k", k=P)
                dve.tensor_reduce(negmax1[:, u % 4, :], src, X, ALU.max, negate=True).then_inc(c_max, 1)
                if not (isinstance(p, int) and n < 4):
                    dve.wait_ge(c_pt_ps, n - 3)
                dve.wait_ge(c_max, n + 1)
                dve.tensor_tensor(sh1[:, u % 4, :].rearrange("p (h k) -> p h k", k=P), src,
                                  negmax1[:, u % 4, :].unsqueeze(2).to_broadcast([P, 4, P]), ALU.add).then_inc(c_sub, 1)

            def c_tail(b, j, stage):
                if stage == 1:
                    dve.wait_ge(c_ovT, b + 1)
                    o = ps[:, M0 + j, 2 * P:4 * P].rearrange("p (a s h d) -> p a s h d", a=2, s=2, d=D1)
                    dve.reciprocal(rsum1[:, :].rearrange("p (a h) -> p a h", a=2), o[:, :, 1, :, 0]).then_inc(c_rs, 1)
                    dve.wait_ge(c_rs, b + 1)
                    dve.tensor_tensor(o1[:, :].rearrange("p (a h d) -> p a h d", a=2, d=D1), o[:, :, 0, :, :],
                                      rsum1[:, :].rearrange("p (a h) -> p a h", a=2).unsqueeze(3)
                                      .to_broadcast([P, 2, 8, D1]), ALU.mult).then_inc(c_norm, 1)
                elif stage == 3:
                    dve.wait_ge(c_wo, b + 1)
                    xs = x_sb[:, bass.ds(b, 1), :].rearrange("p o c -> p (o c)")
                    dve.tensor_tensor(xs, ps[:, M0 + j, P:P + C], xs, ALU.add).then_inc(c_x, 1)

            def c_step(p, first, last):
                for u in range(8):
                    if u < 4 and not first:
                        c_tail(p * 2 - 1, 1, u)
                    if not (last and u + 3 >= 8):
                        c_shift(p, u + 3)
                    if u >= 4:
                        c_tail(p * 2, 0, u - 4)

            for u in range(3):
                c_shift(0, u)
            dve.wait_ge(xb1, NB)
            c_step(0, True, False)
            with dve.Fori(1, NP - 1) as p:
                c_step(p, False, False)
            c_step(NP - 1, False, True)
            for stage in range(4):
                c_tail(NB - 1, 1, stage)

            dve.wait_ge(c_x, NB)
            ln(3)
            for n in range(16):
                t, m = (n % 8) // 4, n % 4
                h = h_at[n // 8, t]
                dve.wait_ge(d_relu, n + 1)
                dve.tensor_copy(h[:, 0, m, :], relu[:, n % 2, :]).then_inc(d_hi, 1)
                dve.wait_ge(d_hi, n + 1)
                dve.tensor_tensor(h[:, 1, m, :], relu[:, n % 2, :], f32(h[:, 0, m, :]), ALU.subtract).then_inc(d_lo, 1)
            for t in range(NT):
                dve.wait_ge(d_yT_ps, t + 1)
                dve.tensor_tensor(fin[:, t, :], ps[:, 4 + t, :],
                                  x_sb[:, 4 * t:4 * t + 4, :].rearrange("p b c -> p (b c)"), ALU.add).then_inc(d_x, 1)


_INS = ['x', 'ctx_768', 'L0_xattn_Wq', 'L0_xattn_Wk', 'L0_xattn_Wv', 'L0_xattn_Wo', 'L0_xattn_bo', 'L0_ffn_Wg',
        'L0_ffn_W1', 'L0_ffn_W2', 'L0_ffn_W3', 'L1_xattn_Wq', 'L1_xattn_bq', 'L1_xattn_Wk', 'L1_xattn_bk',
        'L1_xattn_Wv', 'L1_xattn_bv', 'L1_xattn_Wo', 'L1_xattn_bo', 'L1_ffn_k0', 'L1_ffn_k1', 'L1_ffn_k2',
        'L1_ffn_s0', 'L1_ffn_s1', 'L1_ffn_s2']


def kernel(**inputs):
    import numpy as _np
    import concourse.bacc as _bacc
    from concourse import mybir as _mybir
    from concourse.bass_utils import run_bass_kernel_spmd as _run

    nc = _bacc.Bacc("TRN2", target_bir_lowering=False, num_devices=1)
    arrays, args = {}, {}
    for name in _INS:
        v = _np.ascontiguousarray(inputs[name])
        if v.dtype == _np.bool_:
            v = v.view(_np.int32)
        v = v.reshape(v.shape or (1,))
        arrays[f"in_{name}"] = v
        args[name] = nc.dram_tensor(f"in_{name}", v.shape, _mybir.dt.from_np(v.dtype), kind="ExternalInput").ap()
    shape = inputs['x'].shape
    out = nc.dram_tensor("out_0", shape, _mybir.dt.float32, kind="ExternalOutput").ap()
    program(nc, args, out)
    r = _run(nc, [arrays], core_ids=[0])
    return r.results[0]["out_0"]
```

```python
from contextlib import ExitStack

import concourse.bass as bass
from concourse import mybir

F32 = mybir.dt.float32
F32R = mybir.dt.float32r
I32 = mybir.dt.int32
U32 = mybir.dt.uint32
U8 = mybir.dt.uint8
ALU = mybir.AluOpType
ACT = mybir.ActivationFunctionType
X = mybir.AxisListType.X

P = 128
NB = 8
NP = NB // 2
TG = 512
NT = NB * P // TG
C = 128
CK = 96
CK1 = CK + 1
H0, D0 = 8, 64
I0 = H0 * D0
NC0 = I0 // P
E = 8
HID = 256
NH = HID // P
H1, D1 = 16, 8
NG = 4
NS = 4
F1, F2 = 512, 512
EPS = 1e-5
RSQRT_SEED = 0x5F3759DF


def f32(ap):
    return ap.bitcast(F32)


def program(nc, a, out):
    with ExitStack() as ctx:
        def sb(name, shape, dt=F32):
            return ctx.enter_context(nc.sbuf_tensor(name, shape, dt))

        def sem(name):
            return ctx.enter_context(nc.semaphore(name))

        x_sb = sb("x_sb", [P, NB, C])
        ctx_sb = sb("ctx_sb", [P, NB, CK])
        ident = sb("ident", [P, P])
        ones = sb("ones", [P, P])
        zero = sb("zero", [P, 1])
        warm = sb("warm", [P, 1])
        ctxT = sb("ctxT", [CK1, NB * P])
        ctxT_hi = sb("ctxT_hi", [CK1, NB * P], F32R)
        ctxT_lo = sb("ctxT_lo", [CK1, NB * P], F32R)
        stats = sb("stats", [P, NB, 6])
        meanvar = sb("meanvar", [P, NB, 2])
        ve = sb("ve", [P, NB])
        rs = sb("rs", [P, NB])
        nt = sb("nt", [P, NB])
        nu = sb("nu", [P, NB])
        nm = sb("nm", [P, NB])
        xn = sb("xn", [P, NB, C])
        xT_hi = sb("xT_hi", [P, NB * P], F32R)
        xT_lo = sb("xT_lo", [P, NB * P], F32R)

        w_raw = sb("w_raw", [P, 2, I0])
        wq0, wk0, w12 = w_raw[:, 0, :], w_raw[0:CK, 1, :], w_raw
        wq0_hi = sb("wq0_hi", [C, I0], F32R)
        wq0_lo = sb("wq0_lo", [C, I0], F32R)
        wk0_hi = sb("wk0_hi", [CK1, I0], F32R)
        wk0_lo = sb("wk0_lo", [CK1, I0], F32R)
        wv0 = sb("wv0", [CK, I0])
        wo0 = sb("wo0", [P, NC0, C])
        bo0 = sb("bo0", [P, C])
        kT0 = sb("kT0", [P, NC0, NB * P])
        v0 = sb("v0", [P, NB, I0])
        q_z = sb("q_z", [P, 2, NC0, 2 * P])
        q_ev, q_od = q_z[:, 0], q_z[:, 1]
        probs = sb("probs", [P, 2, H0, P])
        probsT = sb("probsT", [P, 2, H0, P])
        negmax = sb("negmax", [P, 2, H0])
        sums = sb("sums", [P, 2, H0])
        rsum = sb("rsum", [P, 2, H0])
        o_both = sb("o_both", [P, 2, 2, I0])
        v_st, oT = o_both[:, 0], o_both[:, 1]

        wg = sb("wg", [C, E])
        wg_hi = sb("wg_hi", [C, E], F32R)
        wg_lo = sb("wg_lo", [C, E], F32R)
        lg = sb("lg", [P, NB, E])
        top = sb("top", [P, NB, 8])
        topi = sb("topi", [P, NB, 8], U32)
        topf = sb("topf", [P, NB, 8])
        iota_e = sb("iota_e", [P, NB, E])
        gd = sb("gd", [P, NB])
        ge = sb("ge", [P, NB])
        gs = sb("gs", [P, NB])
        gw = sb("gw", [P, 2, NB])
        pick = sb("pick", [P, 2, NB, E])
        picked = sb("picked", [P, 2, NB, E])
        comb = sb("comb", [P, E, NB])
        w12_hi = sb("w12_hi", [P, 2, 2 * HID], F32R)
        w12_lo = sb("w12_lo", [P, 2, 2 * HID], F32R)
        w3 = sb("w3", [P, 2, NH, C])

        wq1 = sb("wq1", [C, C])
        wq1_hi, wq1_lo = wq0_hi, wq0_lo
        wk1 = sb("wk1", [CK1, C])
        wk1_hi, wk1_lo = wk0_hi, wk0_lo
        wv1 = sb("wv1", [CK1, C])
        wo1 = sb("wo1", [C, C])
        bo1 = sb("bo1", [P, C])
        bq1 = sb("bq1", [2, C])
        bq1_r = sb("bq1_r", [2, C], F32R)
        bq1_p = sb("bq1_p", [2, C])
        bq1_s = sb("bq1_s", [2, NS * C], F32R)
        ones_r = sb("ones_r", [2, TG], F32R)
        block_of = sb("block_of", [P, 4])
        row_i = sb("row_i", [P, 1], I32)
        bit_i = sb("bit_i", [P, 3], I32)
        is_lo = sb("is_lo", [P, 3])
        sign = sb("sign", [P, 3])
        part = sb("part", [P, 2, TG], F32R)
        k_st = sb("k_st", [P, NG, NB * P], F32R)
        k_bd = sb("k_bd", [P, 2, NG, 4, P], F32R)
        q_st = sb("q_st", [P, 2, NG, P], F32R)
        negmax1 = sb("negmax1", [P, 4, 4])
        ov = sb("ov", [P, 2 * P])
        rsum1 = sb("rsum1", [P, H1])
        o1 = sb("o1", [P, C])
        o1T = sb("o1T", [P, C])

        k0_i = sb("k0_i", [P, 2, F1 // 4], I32)
        k1_i = sb("k1_i", [P, F1 // P, F2 // 4], I32)
        k2_i = sb("k2_i", [P, F2 // P, C // 4], I32)
        k0_u, k1_u, k2_u = (k[:, :, :].bitcast(U8) for k in (k0_i, k1_i, k2_i))
        d0_w = sb("d0_w", [P, F1], F32R)
        d1_w = sb("d1_w", [P, F1 // P, F2], F32R)
        d2_w = sb("d2_w", [P, F2 // P, C], F32R)
        scale = sb("scale", [P, 3])
        scale2 = sb("scale2", [P, 3])
        h_c = sb("h_c", [P, 2, F1 // P, TG], F32R)

        uT = kT0[:, 0:2, :].rearrange("p t (c n) -> p t c n", c=NH)
        silu = kT0[:, 2, :].rearrange("p (c n) -> p c n", c=NH)
        relu = kT0[:, :, :].rearrange("p t (c n) -> p (t c) n", c=2)
        lgT = kT0[0:E, 3, :]
        v1 = v0[:, :, 0:C]
        v_bd = [z.rearrange("p (h c) -> p h c", c=P) for z in
                (q_z[:, :, :, :].rearrange("p a k n -> p (a k n)"), o_both[:, :, :, :].rearrange("p a k n -> p (a k n)"))]
        q_all = h_c[:, :, :, :].rearrange("p s k n -> p (s k n)").rearrange("p (g n) -> p g n", g=NG)
        sh1 = probs[:, :, :, :].rearrange("p j (a h) k -> p (j a) (h k)", a=2)
        sh1T = probsT[:, :, :, :].rearrange("p j (a h) k -> p (j a) (h k)", a=2)
        h_a = k_bd[:, :, :, :, :].rearrange("p s g h k -> p s g (h k)")
        h_b = k_st[:, :, :].rearrange("p (s g) (u n) -> p s (g u) n", s=2, u=2)
        D_ORDER = ([(0, 0, m) for m in range(4)] + [(1, 0, 0), (1, 0, 1), (1, 0, 2), (0, 1, 0), (0, 1, 1), (0, 1, 2),
                    (0, 1, 3), (1, 0, 3)] + [(1, 1, m) for m in range(4)] + [(2, 0, 0), (2, 1, 0)])
        h_at = {(0, 0): h_a, (0, 1): h_b, (1, 0): h_c, (1, 1): h_a}
        yT = oT[:, :, :]
        fin = v_st[:, :, :]

        ps = ctx.enter_context(nc.psum_tensor("ps", [P, 8, 512], F32))
        D_POOL = (0, 2, 8)
        D_BANK = (1, 2, 3, 0, 4, 5)
        ND = len(D_BANK)

        def lo_count(n):
            return sum((m in D_POOL) == (n in D_POOL) for m in range(n + 1))

        M0 = 6
        NK1 = 2 * NP
        LN_BANK = ((M0, 5), (4, M0 + 1), (3, M0 + 1), (0, M0 + 1))

        ld_x, ld_ctx, ld_v0, ld_w0, ld_w1, ld_d = (sem(n) for n in ("ld_x", "ld_ctx", "ld_v0", "ld_w0", "ld_w1", "ld_d"))
        ld_up = [sem("ld_up0"), sem("ld_up1")]
        ld_down = [sem("ld_down0"), sem("ld_down1")]
        stored = sem("stored")
        const_ok, zeros_ok, split_w0, split_w1, masks = (sem(n) for n in (
            "const_ok", "zeros_ok", "split_w0", "split_w1", "masks"))
        pool_step = sem("pool_step")
        ctxT_ps, ctxT_f, ctxT_h, ctxT_ok = (sem(n) for n in ("ctxT_ps", "ctxT_f", "ctxT_h", "ctxT_ok"))
        k0_ps, k0_ok_a, k0_ok_v, v0_ps, v0_ok = (sem(n) for n in ("k0_ps", "k0_ok_a", "k0_ok_v", "v0_ps", "v0_ok"))
        ln_st, ln_mv, ln_nw, ln_seed, ln_rs, ln_nm, ln_xn, ln_ps, ln_hi, ln_lo = (sem(n) for n in (
            "ln_st", "ln_mv", "ln_nw", "ln_seed", "ln_rs", "ln_nm", "ln_xn", "ln_ps", "ln_hi", "ln_lo"))
        xb0, xb1 = sem("xb0"), sem("xb1")
        a_q_ps, a_qe, a_qo, a_s, a_max, a_exp, a_pt_ps, a_pt_v, a_pt_a, a_v, a_o, a_rs, a_norm, a_oT, a_wo, a_x = (
            sem("a_" + n) for n in ("q_ps", "qe", "qo", "s", "max", "exp", "pt_ps", "pt_v", "pt_a", "v", "o", "rs", "norm",
                                    "oT", "wo", "x"))
        g_T, g_lT, g_ps, g_lg, g_top, g_idx, g_f, g_d, g_e, g_s, g_w, g_pick, g_sel, g_ok = (
            sem("g_" + n) for n in ("T", "lT", "ps", "lg", "top", "idx", "f", "d", "e", "s", "w", "pick", "sel", "ok"))
        b_hi, b_lo, b_h, b_g, b_silu, b_u, b_y, b_acc = (
            sem("b_" + n) for n in ("hi", "lo", "h", "g", "silu", "u", "y", "acc"))
        k1_ps, k1_part, k1_st, v1_ps, v1_ok = (sem(n) for n in ("k1_ps", "k1_part", "k1_st", "v1_ps", "v1_ok"))
        c_q_ps, c_part, c_q, c_k, c_qs, c_v, c_s, c_max, c_sub, c_exp, c_pt_ps, c_pt, c_o, c_ov, c_ovT, c_rs, c_norm, \
            c_oT_ps, c_oT, c_wo, c_x = (
                sem("c_" + n) for n in ("q_ps", "part", "q", "k", "qs", "v", "s", "max", "sub", "exp", "pt_ps", "pt", "o",
                                        "ov", "ovT", "rs", "norm", "oT_ps", "oT", "wo", "x"))
        d_w, d_ps, d_relu_a, d_relu_v, d_yT, d_hi, d_lo, d_lo_p, d_y, d_yT_ps, d_x = (
            sem("d_" + n) for n in ("w", "ps", "relu_a", "relu_v", "yT", "hi", "lo", "lo_p", "y", "yT_ps", "x"))

        A = a
        def stacked(ap):
            return ap[:, :].rearrange("c (h p d) -> c h p d", p=NS, d=D1)

        def repeated(ap):
            return ap[:, :].rearrange("c (h d) -> c h d", d=D1).unsqueeze(2).to_broadcast([ap.shape[0], H1, NS, D1])

        def row(ap, n):
            return ap.rearrange("(o c) -> o c", o=1).to_broadcast([n, ap.shape[0]])

        def diagonal(j, half, column):
            flat = v_bd[j].rearrange("p h c -> p (h c)")
            first = half * 8 * P + column
            return bass.AP(tensor=flat.tensor, offset=flat.offset + first, ap=[flat.ap[0], [P + 8, 8], [1, 8]])

        block = ctx.enter_context(nc.Block())

        @block.sync
        def _(sp):
            sp.dma_start(ctx_sb[:, :, :], A["ctx_768"].rearrange("b t c -> t b c")).then_inc(ld_ctx, 16)
            sp.dma_start(wv0[:, :], A["L0_xattn_Wv"]).then_inc(ld_v0, 16)
            sp.dma_start(x_sb[:, :, :], A["x"].rearrange("b t c -> t b c")).then_inc(ld_x, 16)
            for dst, src in ((wk0, A["L0_xattn_Wk"]), (wq0, A["L0_xattn_Wq"]),
                             (wo0[:, :, :], A["L0_xattn_Wo"].rearrange("(k p) c -> p k c", p=P)),
                             (bo0[:, :], row(A["L0_xattn_bo"], P)), (wg[:, :], A["L0_ffn_Wg"])):
                sp.dma_start(dst, src).then_inc(ld_w0, 16)
            for dst, src in ((wq1[:, :], A["L1_xattn_Wq"]), (wk1[0:CK, :], A["L1_xattn_Wk"]),
                             (wk1[CK:CK1, :], row(A["L1_xattn_bk"], 1)), (wv1[0:CK, :], A["L1_xattn_Wv"]),
                             (wv1[CK:CK1, :], row(A["L1_xattn_bv"], 1)), (bq1[:, :], row(A["L1_xattn_bq"], 2)),
                             (wo1[:, :], A["L1_xattn_Wo"]), (bo1[:, :], row(A["L1_xattn_bo"], P))):
                sp.dma_start(dst, src).then_inc(ld_w1, 16)
            for dst, src in ((k0_i[:, :, :], A["L1_ffn_k0"].rearrange("(k p) c -> p k c", p=P)),
                             (k1_i[:, :, :], A["L1_ffn_k1"].rearrange("(k p) c -> p k c", p=P)),
                             (k2_i[:, :, :], A["L1_ffn_k2"].rearrange("(k p) c -> p k c", p=P)),
                             (scale[:, 0:1], row(A["L1_ffn_s0"], P)), (scale[:, 1:2], row(A["L1_ffn_s1"], P)),
                             (scale[:, 2:3], row(A["L1_ffn_s2"], P))):
                sp.dma_start(dst, src).then_inc(ld_d, 16)

            def load_up(e, buf):
                sp.dma_start(w12[:, buf, 0:HID], A["L0_ffn_W1"][bass.ds(e, 1)].rearrange("o p h -> p (o h)")).then_inc(ld_up[buf], 16)
                sp.dma_start(w12[:, buf, HID:2 * HID], A["L0_ffn_W2"][bass.ds(e, 1)].rearrange("o p h -> p (o h)")).then_inc(ld_up[buf], 16)

            def load_down(e, buf):
                sp.dma_start(w3[:, buf, :, :], A["L0_ffn_W3"][bass.ds(e, 1)].rearrange("o (k p) c -> p (o k) c", p=P)).then_inc(ld_down[buf], 16)

            sp.wait_ge(split_w0, 2)
            for buf in range(2):
                load_up(buf, buf)
                load_down(buf, buf)
            with sp.Fori(1, E // 2) as i:
                for buf in range(2):
                    sp.wait_ge(b_lo, i * 2 + (buf - 1))
                    load_up(i * 2 + buf, buf)
                    sp.wait_ge(b_y, i * 4 + (2 * buf - 2))
                    load_down(i * 2 + buf, buf)
            for t in range(NT):
                sp.wait_ge(d_x, t + 1)
                sp.dma_start(out[t * 4:t * 4 + 4].rearrange("b t c -> t b c"),
                             fin[:, t, :].rearrange("p (b c) -> p b c", c=C)).then_inc(stored, 16)
            sp.wait_ge(stored, 16 * NT)

        @block.gpsimd
        def _(pool):
            step = [0]

            def chain(ins):
                step[0] += 1
                ins.then_inc(pool_step, 1)
                pool.wait_ge(pool_step, step[0])

            def ln_root(s, t):
                pool.wait_ge(ln_seed, s)
                bs = slice(4 * t, 4 * t + 4)
                v, y, h, z = ve[:, bs], rs[:, bs], nt[:, bs], nu[:, bs]
                chain(pool.tensor_tensor(h, y, y, ALU.mult))
                chain(pool.tensor_tensor(h, h, v, ALU.mult))
                chain(pool.tensor_scalar(z, h, -10.0 / 3, None, ALU.add))
                chain(pool.tensor_tensor(z, z, h, ALU.mult))
                chain(pool.tensor_scalar(z, z, 5.0, None, ALU.add))
                chain(pool.tensor_tensor(y, z, y, ALU.mult))
                chain(pool.tensor_tensor(h, y, y, ALU.mult))
                chain(pool.tensor_tensor(h, h, v, ALU.mult))
                chain(pool.tensor_scalar(h, h, -0.5 * 0.375 ** 3, 1.5 * 0.375, ALU.mult, ALU.add))
                pool.tensor_tensor(y, h, y, ALU.mult).then_inc(ln_rs, 1)

            def ln_scale(s, t):
                pool.wait_ge(ln_rs, s)
                for b in range(4 * t, 4 * t + 4):
                    pool.tensor_scalar(xn[:, b, :], x_sb[:, b, :], meanvar[:, b, 0:1], rs[:, b:b + 1],
                                       ALU.subtract, ALU.mult).then_inc(ln_xn, 1)

            pool.memset(ones[:, :], 1.0).then_inc(const_ok, 1)
            chain(pool.memset(ident[:, :], 0.0))
            chain(pool.memset(zero[:, :], 0.0))
            pool.affine_select(out=ident[:, :], in_=ident[:, :], compare_op=ALU.not_equal, fill=1.0, base=0,
                               pattern=[[-1, P]], channel_multiplier=1).then_inc(const_ok, 1)
            pool.wait_ge(const_ok, 2)
            pool.memset(ctxT[CK:CK1, :], 1.0).then_inc(const_ok, 1)
            pool.wait_ge(const_ok, 3)
            pool.memset(q_z[:, :, :, :], 0.0).then_inc(zeros_ok, 1)
            chain(pool.iota(iota_e[:, :, :], [[0, NB], [1, E]], base=0, channel_multiplier=0,
                            allow_small_or_imprecise_dtypes=True))
            pool.iota(row_i[:, :], [[0, 1]], base=0, channel_multiplier=1).then_inc(const_ok, 1)
            pool.wait_ge(ld_w0, 16 * 5)
            for w, hi, lo in ((wk0, wk0_hi, wk0_lo), (wq0, wq0_hi, wq0_lo)):
                rows = w.shape[0]
                chain(pool.tensor_copy(hi[0:rows, :], w))
                pool.tensor_tensor(lo[0:rows, :], w, f32(hi[0:rows, :]), ALU.subtract).then_inc(split_w0, 1)
            pool.wait_ge(ld_x, 16)
            for b in range(NB):
                pool.wait_ge(ln_xn, b + 1)
                pool.tensor_tensor(x_sb[:, b, :], x_sb[:, b, :], bo0[:, :], ALU.add).then_inc(xb0, 1)
            def stage_values(p):
                for j in range(2):
                    if not (isinstance(p, int) and p == 0):
                        pool.wait_ge(a_o, p * 2 + (j - 1))
                    pool.tensor_tensor(v_st[:, j, :], v0[:, bass.ds(p * 2 + j, 1), :].rearrange("p o d -> p (o d)"),
                                       zero[:, :].to_broadcast([P, I0]), ALU.add).then_inc(a_v, 1)

            pool.wait_ge(v0_ok, NB)
            stage_values(0)
            pool.wait_ge(ld_w1, 16 * 8)
            def split_repeated(w, hi, lo):
                chain(pool.tensor_copy(stacked(hi), repeated(w)))
                pool.tensor_tensor(stacked(lo), repeated(w), stacked(f32(hi)), ALU.subtract).then_inc(split_w1, 1)

            pool.wait_ge(k0_ps, NC0 * NT)
            split_repeated(wk1, wk1_hi, wk1_lo)
            pool.memset(f32(ones_r[:, :]), 1.0).then_inc(split_w1, 1)
            chain(pool.memset(block_of[:, :], 1.0))
            chain(pool.affine_select(out=block_of[:, :], in_=block_of[:, :], compare_op=ALU.is_ge, fill=0.0, base=0,
                                     pattern=[[-32, 4]], channel_multiplier=1))
            chain(pool.affine_select(out=block_of[:, :], in_=block_of[:, :], compare_op=ALU.is_ge, fill=0.0, base=31,
                                     pattern=[[32, 4]], channel_multiplier=-1))
            def split_expert(e, buf):
                pool.wait_ge(ld_up[buf], (e - buf) * 16 + 32)
                if not isinstance(e, int) or e >= 2:
                    pool.wait_ge(b_g, e * 4 - 4)
                pool.tensor_tensor(w12_hi[:, buf, :], w12[:, buf, :], zero[:, :].to_broadcast([P, 2 * HID]),
                                   ALU.add).then_inc(b_hi, 1)
                pool.wait_ge(b_hi, e + 1)
                pool.tensor_tensor(w12_lo[:, buf, :], w12[:, buf, :], f32(w12_hi[:, buf, :]), ALU.subtract).then_inc(b_lo, 1)

            split_expert(0, 0)
            split_expert(1, 1)
            pool.wait_ge(ld_d, 16 * 6)
            pool.tensor_scalar(d1_w[:, :, :], k1_u[:, :, :], 2.0, -1.0, ALU.mult, ALU.add).then_inc(d_w, 1)
            pool.tensor_scalar(d2_w[:, :, :], k2_u[:, :, :], 2.0, -1.0, ALU.mult, ALU.add).then_inc(d_w, 1)
            with pool.Fori(1, NP - 1) as p:
                stage_values(p)
            pool.wait_ge(a_q_ps, 2 * NP)
            split_repeated(wq1, wq1_hi, wq1_lo)
            stage_values(NP - 1)
            ln_root(1, 0)
            pool.wait_ge(a_wo, NB)
            for j in range(2):
                pool.memset(v_bd[j], 0.0).then_inc(zeros_ok, 1)
            for j in range(2):
                pool.wait_ge(zeros_ok, 2 + j)
                for half in range(2):
                    pool.memset(diagonal(j, half, 64), 1.0).then_inc(zeros_ok, 1)

            with pool.Fori(1, E // 2) as i:
                for buf in range(2):
                    split_expert(i * 2 + buf, buf)
            def stage_k(b, j):
                keys = f32(k_st[:, :, bass.ds(b * P, P)]).unsqueeze(2).to_broadcast([P, NG, 4, P])
                blocks = block_of[:, :].unsqueeze(1).unsqueeze(3).to_broadcast([P, NG, 4, P])
                pool.tensor_tensor(k_bd[:, j, :, :, :], keys, blocks, ALU.mult).then_inc(c_k, 1)

            def stage_q(b, j):
                pool.tensor_copy(q_st[:, j, :, :], f32(q_all[:, :, bass.ds(b * P, P)])).then_inc(c_qs, 1)

            def stage_v(b, j):
                for half in range(2):
                    src = v1[:, bass.ds(b, 1), 64 * half:64 * half + 64].rearrange("p o (h d) -> p (o h) d", d=D1)
                    pool.tensor_copy(diagonal(j, half, 0), src).then_inc(c_v, 1)

            pool.wait_ge(zeros_ok, 7)
            pool.wait_ge(v1_ok, NT)
            pool.wait_ge(k1_st, 2)
            for j in range(2):
                stage_k(j, j)
                stage_v(j, j)
            for b in range(NB):
                if b == 4:
                    ln_root(2, 1)
                    pool.wait_ge(ln_rs, 2)
                    chain(pool.tensor_tensor(nm[:, 4:NB], meanvar[:, 4:NB, 0], rs[:, 4:NB], ALU.mult))
                    pool.tensor_scalar(nm[:, 4:NB], nm[:, 4:NB], -1.0, None, ALU.mult).then_inc(ln_nm, 1)
                pool.wait_ge(ln_xn, 2 * NB + b + 1)
                pool.tensor_tensor(x_sb[:, b, :], x_sb[:, b, :], bo1[:, :], ALU.add).then_inc(xb1, 1)
            with pool.Fori(1, NP) as p:
                pool.wait_ge(c_s, p * 8 - 4)
                pool.wait_ge(k1_st, NK1)
                stage_k(p * 2, 0)
                pool.wait_ge(c_q, NG * NT)
                stage_q(p * 2, 0)
                pool.wait_ge(c_o, p * 8 - 4)
                stage_v(p * 2, 0)
                pool.wait_ge(c_s, p * 8)
                stage_k(p * 2 + 1, 1)
                stage_q(p * 2 + 1, 1)
                pool.wait_ge(c_o, p * 8)
                stage_v(p * 2 + 1, 1)

            ln_root(3, 0)
            ln_scale(3, 0)
            for n in D_POOL:
                layer, t, m = D_ORDER[n]
                pool.wait_ge(d_hi, n + 1)
                pool.wait_ge(d_relu_a, n // 2 + 1)
                h = h_at[layer, t]
                pool.tensor_tensor(h[:, 1, m, :], relu[:, n % ND, :], f32(h[:, 0, m, :]), ALU.subtract).then_inc(d_lo_p, 1)

        @block.tensor
        def _(pe):
            def keep_clock(n, bank):
                for _ in range(n):
                    pe.matmul(ps[:, bank, 0:P], ones[:, :], ones[:, :], start=True, stop=True)

            def split3(dst, w_hi, w_lo, x_hi, x_lo, start=True, stop=True):
                pe.matmul(dst, w_hi, x_hi, start=start, stop=False)
                pe.matmul(dst, w_hi, x_lo, start=False, stop=False)
                return pe.matmul(dst, w_lo, x_hi, start=False, stop=stop)

            def ln_transposes(s, t):
                for k in range(4):
                    pe.wait_ge(ln_xn, NB * s + 4 * t + k + 1)
                    ins = pe.transpose(ps[:, LN_BANK[s][t], k * P:(k + 1) * P], xn[:, 4 * t + k, :], ident[:, :])
                ins.then_inc(ln_ps, 1)

            pe.wait_ge(const_ok, 1)
            keep_clock(8, 7)
            pe.wait_ge(const_ok, 2)
            pe.wait_ge(ld_ctx, 16)
            for b in range(NB):
                ins = pe.transpose(ps[0:CK, b // 4, (b % 4) * P:(b % 4 + 1) * P], ctx_sb[:, b, :], ident[:, :])
                if b % 4 == 3:
                    ins.then_inc(ctxT_ps, 1)
            pe.wait_ge(ld_v0, 16)
            for b in range(NB):
                pe.wait_ge(ctxT_f, b // 4 + 1)
                if b >= 2:
                    pe.wait_ge(v0_ok, b - 1)
                pe.matmul(ps[:, 4 + b % 2, :], ctxT[0:CK, b * P:(b + 1) * P], wv0[:, :],
                          start=True, stop=True).then_inc(v0_ps, 1)
            def k0_keys(t, k, bank):
                sl = slice(t * TG, (t + 1) * TG)
                split3(ps[:, bank, :], wk0_hi[0:CK, k * P:(k + 1) * P], wk0_lo[0:CK, k * P:(k + 1) * P],
                       ctxT_hi[0:CK, sl], ctxT_lo[0:CK, sl]).then_inc(k0_ps, 1)

            pe.wait_ge(split_w0, 1)
            pe.wait_ge(ctxT_ok, 1)
            for k in range(NC0):
                k0_keys(0, k, k)
                if k == 0:
                    ln_transposes(0, 0)
                if k == 2:
                    pe.wait_ge(v0_ok, NB)
                    ln_transposes(0, 1)
            pe.wait_ge(split_w0, 2)

            def a_queries(p):
                for m in range(2):
                    for k in (2 * m, 2 * m + 1):
                        ins = split3(ps[:, M0 + m, (k % 2) * 2 * P:(k % 2 + 1) * 2 * P],
                                     wq0_hi[:, k * P:(k + 1) * P], wq0_lo[:, k * P:(k + 1) * P],
                                     xT_hi[:, bass.ds(p * 2 * P, 2 * P)], xT_lo[:, bass.ds(p * 2 * P, 2 * P)])
                    ins.then_inc(a_q_ps, 1)

            def a_scores(p, j):
                for h in range(H0):
                    if j == 0 and h % 4 == 0:
                        pe.wait_ge(a_qe, p * 2 + (h // 4 + 1))
                        pe.wait_ge(a_qo, p * 2 + (h // 4 + 1))
                    q = (q_ev if h % 2 == 0 else q_od)[:, h // 2, j * P:(j + 1) * P]
                    ins = pe.matmul(ps[:, 2 * j + h // 4, (h % 4) * P:(h % 4 + 1) * P], q,
                                    kT0[:, h // 2, bass.ds(p * 2 * P + j * P, P)], start=True, stop=True)
                ins.then_inc(a_s, 1)

            def a_probs_turn(p, j):
                pe.wait_ge(a_norm, p * 2 + j + 1)
                if j == 1:
                    pe.wait_ge(a_pt_a, p * 3 + 2)
                elif isinstance(p, int) and p == 0:
                    pe.wait_ge(k0_ok_v, 3)
                    pe.wait_ge(k0_ok_a, 3)
                for h in range(H0):
                    ins = pe.transpose(ps[:, 4 + h // 4, (h % 4) * P:(h % 4 + 1) * P], probs[:, j, h, :], ident[:, :])
                ins.then_inc(a_pt_ps, 1)

            def a_values(p, j):
                pe.wait_ge(a_v, p * 2 + j + 1)
                if isinstance(p, int) and p == NP - 1:
                    pe.wait_ge(v1_ok, 1)
                for h in range(H0):
                    if j == 1 and h == 0:
                        pe.wait_ge(a_pt_v, p + 1)
                    elif h % 4 == 0:
                        pe.wait_ge(a_pt_a, p * 3 + (2 * j + h // 4 + 1 - j))
                    rows = slice(h % 2 * D0, (h % 2 + 1) * D0)
                    ins = pe.matmul(ps[rows, M0 + j, (h // 2) * P:(h // 2 + 1) * P], v_st[:, j, h * D0:(h + 1) * D0],
                                    probsT[:, j, h, :], start=True, stop=True)
                ins.then_inc(a_o, 1)

            def a_out(p, j, last):
                bank = (M0 if last else 4) + j
                pe.wait_ge(a_oT, p * 2 + j + 1)
                for k in range(NC0):
                    ins = pe.matmul(ps[:, bank, 0:C], oT[:, j, k * P:(k + 1) * P], wo0[:, k, :],
                                    start=(k == 0), stop=(k == NC0 - 1))
                ins.then_inc(a_wo, 1)

            def a_step(p, first, last):
                if not last:
                    if first:
                        pe.wait_ge(k0_ok_v, 5)
                    a_queries(p + 1)
                    if not first:
                        pe.wait_ge(a_x, p * 2)
                    a_probs_turn(p, 0)
                    a_scores(p + 1, 0)
                else:
                    for t in range(NT):
                        for b in range(4):
                            bs = (4 * t + b) * P
                            ins = pe.matmul(ps[:, 1 if t else M0, b * C:(b + 1) * C], ctxT[:, bs:bs + P], wv1[:, :],
                                            start=True, stop=True)
                        ins.then_inc(v1_ps, 1)
                        if t == 0:
                            pe.wait_ge(a_x, p * 2)
                            a_probs_turn(p, 0)
                a_probs_turn(p, 1)
                a_values(p, 0)
                if not last:
                    a_scores(p + 1, 1)
                a_values(p, 1)
                if last:
                    ln_transposes(1, 0)
                a_out(p, 0, last)
                a_out(p, 1, last)

            pe.wait_ge(ln_lo, 1)
            pe.wait_ge(ln_hi, 1)
            a_queries(0)
            pe.wait_ge(ctxT_ok, NT)
            k0_keys(1, 0, 4)
            pe.wait_ge(k0_ok_a, 2)
            pe.wait_ge(k0_ok_v, 2)
            pe.wait_ge(zeros_ok, 1)
            a_scores(0, 0)
            pe.wait_ge(ln_lo, NT)
            pe.wait_ge(ln_hi, NT)
            k0_keys(1, 1, 5)
            a_scores(0, 1)
            k0_keys(1, 2, M0)
            k0_keys(1, 3, M0 + 1)
            a_step(0, True, False)
            with pe.Fori(1, NP - 1) as p:
                a_step(p, False, False)
            a_step(NP - 1, False, True)

            def k1_keys(i, m):
                for k in range(2):
                    gs, cols = slice((2 * m + k) * P, (2 * m + k + 1) * P), bass.ds(i * 2 * P, 2 * P)
                    ins = split3(ps[:, M0 + m, k * 2 * P:(k + 1) * 2 * P], wk1_hi[:, gs], wk1_lo[:, gs],
                                 ctxT_hi[:, cols], ctxT_lo[:, cols])
                ins.then_inc(k1_ps, 1)

            pe.wait_ge(masks, 12)

            def gate_logits(t):
                split3(ps[0:E, 5 - t, :], wg_hi[:, :], wg_lo[:, :],
                       xT_hi[:, t * TG:(t + 1) * TG], xT_lo[:, t * TG:(t + 1) * TG]).then_inc(g_T, 1)

            def b_hidden(q, buf, t, chunks=range(NH)):
                for c in chunks:
                    v = q * NH + c
                    if not (isinstance(q, int) and q == 0):
                        pe.wait_ge(b_u, v - 1)
                    sl = slice(t * TG, (t + 1) * TG)
                    for half, bank, s in ((0, c, b_h), (HID, 2 + c, b_g)):
                        w = slice(half + c * P, half + (c + 1) * P)
                        split3(ps[:, bank, :], w12_hi[:, buf, w], w12_lo[:, buf, w],
                               xT_hi[:, sl], xT_lo[:, sl]).then_inc(s, 1)

            def b_down(q, slot, buf, i):
                pe.wait_ge(ld_down[buf], i * 16 + 16)
                pe.wait_ge(b_u, q * NH + NH)
                for k in range(4):
                    for c in range(NH):
                        ins = pe.matmul(ps[:, 4 + slot, k * C:(k + 1) * C], uT[:, slot, c, k * P:(k + 1) * P],
                                        w3[:, buf, c, :], start=(c == 0), stop=(c == NH - 1))
                ins.then_inc(b_y, 1)

            pe.wait_ge(ln_lo, 2 + 1)
            pe.wait_ge(b_lo, 1)
            pe.wait_ge(v1_ok, NT)
            b_hidden(0, 0, 0)
            gate_logits(0)
            ln_transposes(1, 1)
            pe.wait_ge(split_w1, 3)
            k1_keys(0, 0)
            keep_clock(3, 4)
            pe.wait_ge(ln_lo, 2 * NT)
            gate_logits(1)
            b_hidden(1, 0, 1, (0,))
            pe.wait_ge(g_lT, NT)
            for b in range(NB):
                ins = pe.transpose(ps[:, 5, b * E:(b + 1) * E], lgT[:, b * P:(b + 1) * P], ident[0:E, 0:E])
            ins.then_inc(g_ps, 1)
            b_hidden(1, 0, 1, (1,))
            with pe.Fori(0, NP - 1) as i:
                b_down(i * 4, 0, 0, i)
                pe.wait_ge(b_lo, i * 2 + 2)
                b_hidden(i * 4 + 2, 1, 0)
                b_down(i * 4 + 1, 1, 0, i)
                b_hidden(i * 4 + 3, 1, 1)
                k1_keys(i, 1)
                b_down(i * 4 + 2, 0, 1, i)
                pe.wait_ge(b_lo, i * 2 + 3)
                b_hidden(i * 4 + 4, 0, 0)
                b_down(i * 4 + 3, 1, 1, i)
                b_hidden(i * 4 + 5, 0, 1)
                k1_keys(i + 1, 0)
            q = 2 * E - 4
            b_down(q, 0, 0, NP - 1)
            pe.wait_ge(b_lo, E)
            b_hidden(q + 2, 1, 0)
            b_down(q + 1, 1, 0, NP - 1)
            b_down(q + 2, 0, 1, NP - 1)
            b_hidden(q + 3, 1, 1)
            keep_clock(5, M0 + 1)
            b_down(q + 3, 1, 1, NP - 1)
            keep_clock(3, M0 + 1)
            ln_transposes(2, 0)
            k1_keys(NP - 1, 1)
            keep_clock(4, M0)

            def c_queries(n):
                g, t = n % NG, n // NG
                bank = g if t == 0 else M0 + 1
                pe.wait_ge(ln_lo, 2 * NT + t + 1)
                pe.wait_ge(ln_hi, 2 * NT + t + 1)
                if n > NG:
                    pe.wait_ge(c_q, n)
                gs, sl = slice(g * P, (g + 1) * P), slice(t * TG, (t + 1) * TG)
                split3(ps[:, bank, :], wq1_hi[:, gs], wq1_lo[:, gs], xT_hi[:, sl], xT_lo[:, sl], stop=False)
                pe.matmul(ps[:, bank, :], bq1_s[:, gs], ones_r[:, :], start=False, stop=True).then_inc(c_q_ps, 1)

            def c_scores(p, u):
                n = p * 8 + u
                j, g = u % 8 // 4, u % 4
                if g == 0:
                    pe.wait_ge(c_k, p * 2 + (u // 4 + 1))
                if isinstance(n, int) and n < 8:
                    q = q_all[:, g, j * P:(j + 1) * P]
                    if n < 4:
                        pe.wait_ge(c_q, g + 1)
                else:
                    q = q_st[:, j, g, :]
                    if g == 0:
                        pe.wait_ge(c_qs, p * 2 + (u // 4 - 1))
                if not (isinstance(p, int) and n < 4):
                    pe.wait_ge(c_sub, n - 3)
                pe.matmul(ps[:, g, :], q, k_bd[:, j, g, :, :].rearrange("p h k -> p (h k)"),
                          start=True, stop=True).then_inc(c_s, 1)

            def c_turn(p, u):
                pe.wait_ge(c_exp, p * 8 + (u + 1))
                for h in range(4):
                    ins = pe.transpose(ps[:, 4 + u % 2, h * P:(h + 1) * P], sh1[:, u % 4, h * P:(h + 1) * P], ident[:, :])
                ins.then_inc(c_pt_ps, 1)

            def c_values(p, u, first):
                j, half = u // 4, u % 4 // 2
                pe.wait_ge(c_pt, p * 8 + (u + 1))
                if u % 4 == 0:
                    pe.wait_ge(c_v, p * 4 + (2 * j + 2))
                    if not (first and isinstance(p, int)):
                        pe.wait_ge(c_x, p * 2 + (j - 1))
                    elif j == 1:
                        pe.wait_ge(c_q, NG * NT)
                for h in range(4):
                    hh = 4 * (u % 4) + h
                    ins = pe.matmul(ps[:, M0 + j, half * P:(half + 1) * P], v_bd[j][:, hh, :],
                                    sh1T[:, u % 4, h * P:(h + 1) * P], start=(hh % 8 == 0), stop=(hh % 8 == 7))
                ins.then_inc(c_o, 1)

            def c_tail(b, j, stage):
                if stage == 0:
                    pe.wait_ge(c_ov, b + 1)
                    for half in range(2):
                        ins = pe.transpose(ps[:, M0 + j, (2 + half) * P:(3 + half) * P], ov[:, half * P:(half + 1) * P],
                                           ident[:, :])
                    ins.then_inc(c_ovT, 1)
                elif stage == 1:
                    pe.wait_ge(c_norm, b + 1)
                    pe.transpose(ps[:, M0 + j, 0:P], o1[:, :], ident[:, :]).then_inc(c_oT_ps, 1)
                else:
                    pe.wait_ge(c_oT, b + 1)
                    pe.matmul(ps[:, M0 + j, P:P + C], o1T[:, :], wo1[:, :], start=True, stop=True).then_inc(c_wo, 1)

            def d_unit(n):
                layer, t, m = D_ORDER[n]
                sl, ms = slice(t * TG, (t + 1) * TG), slice(m * P, (m + 1) * P)
                if n == 0:
                    pe.wait_ge(d_w, 3)
                if layer == 0:
                    pe.wait_ge(ln_lo, 3 * NT + t + 1)
                    pe.wait_ge(ln_hi, 3 * NT + t + 1)
                    terms = [(d0_w[:, ms], xx[:, sl]) for xx in (xT_hi, xT_lo)]
                else:
                    w = d1_w if layer == 1 else d2_w
                    h = h_at[layer - 1, t]
                    terms = [(w[:, k, ms], h[:, part, k, :]) for k in range(4) for part in range(2)]
                if n >= ND:
                    pe.wait_ge(d_relu_a if n % 2 == 0 else d_relu_v, (n - ND) // 2 + 1)
                for i, (w_, x_) in enumerate(terms):
                    if n == 6 and i == 4:
                        ln_transposes(3, 1)
                    if layer > 0 and i % 2 == 0:
                        made = D_ORDER.index((layer - 1, t, i // 2))
                        pe.wait_ge(d_lo_p if made in D_POOL else d_lo, lo_count(made))
                    ins = pe.matmul(ps[:, D_BANK[n % ND], :], w_, x_, start=(i == 0), stop=(i == len(terms) - 1))
                ins.then_inc(d_ps, 1)

            def c_step(p, first, last):
                for u in range(8):
                    if not (last and u + 3 >= 8):
                        c_scores(p, u + 3)
                    if not (last and u == 7):
                        c_turn(p, u + 1)
                    if first and u < 4:
                        c_queries(NG + u)
                    c_values(p, u, first)
                    if u < 3 and not first:
                        c_tail(p * 2 - 1, 1, u)
                    if 4 <= u < 7:
                        c_tail(p * 2, 0, u - 4)
                    if last and u == 4:
                        ln_transposes(3, 0)
                    if last and u >= 6:
                        d_unit(2 * u - 12)
                        d_unit(2 * u - 11)

            pe.wait_ge(masks, 12)
            for n in range(NG):
                c_queries(n)
            for u in range(3):
                c_scores(0, u)
            pe.wait_ge(k1_st, NK1)
            keep_clock(8, M0 + 1)
            c_turn(0, 0)
            ln_transposes(2, 1)
            c_step(0, True, False)
            with pe.Fori(1, NP - 1) as p:
                c_step(p, False, False)
            c_step(NP - 1, False, True)
            c_tail(NB - 1, 1, 0)
            keep_clock(3, 5)
            c_tail(NB - 1, 1, 1)
            keep_clock(2, 5)
            c_tail(NB - 1, 1, 2)
            keep_clock(4, 5)

            for n in range(4, len(D_ORDER)):
                d_unit(n)
            for t in range(NT):
                pe.wait_ge(d_yT, t + 1)
                for k in range(4):
                    ins = pe.transpose(ps[:, M0 + t, k * P:(k + 1) * P], yT[:, t, k * P:(k + 1) * P], ident[:, :])
                ins.then_inc(d_yT_ps, 1)

        @block.scalar
        def _(act):
            def table(function):
                act.activation(warm[:, :], zero[:, :], function)

            def ln_hi_copy(s, t):
                act.wait_ge(ln_ps, NT * s + t + 1)
                sl = slice(t * TG, (t + 1) * TG)
                act.activation(xT_hi[:, sl], ps[:, LN_BANK[s][t], :], ACT.Copy).then_inc(ln_hi, 1)

            for t in range(NT):
                act.wait_ge(ctxT_ps, t + 1)
                act.activation(ctxT[0:CK, t * TG:(t + 1) * TG], ps[0:CK, t, :], ACT.Copy).then_inc(ctxT_f, 1)
            act.wait_ge(const_ok, 3)
            act.wait_ge(ctxT_f, NT)
            for b in range(NB):
                act.wait_ge(v0_ps, b + 1)
                act.activation(v0[:, b, :], ps[:, 4 + b % 2, :], ACT.Copy).then_inc(v0_ok, 1)
                if b < NT:
                    sl = slice(b * TG, (b + 1) * TG)
                    act.activation(ctxT_hi[:, sl], ctxT[:, sl], ACT.Copy).then_inc(ctxT_h, 1)
            ln_hi_copy(0, 0)
            for k in (0, 2):
                act.wait_ge(k0_ps, k + 1)
                act.activation(kT0[:, k, 0:TG], ps[:, k, :], ACT.Copy).then_inc(k0_ok_a, 1)
            ln_hi_copy(0, 1)

            def a_query_copy(n):
                act.wait_ge(zeros_ok, 1)
                for m in range(2):
                    act.wait_ge(a_q_ps, n + m + 1)
                    act.activation(q_od[64:P, 2 * m:2 * m + 2, :],
                                   ps[64:P, M0 + m, :].rearrange("p (k t) -> p k t", k=2), ACT.Copy,
                                   scale=D0 ** -0.5).then_inc(a_qo, 1)

            def a_exp_heads(p, j):
                act.wait_ge(a_max, p * 2 + j + 1)
                for h in range(H0):
                    ins = act.activation(probs[:, j, h, :], ps[:, 2 * j + h // 4, (h % 4) * P:(h % 4 + 1) * P], ACT.Exp,
                                         bias=negmax[:, j, h:h + 1], scale=1.0, accum_out=sums[:, j, h:h + 1])
                ins.then_inc(a_exp, 1)

            def a_oT_copy(p, j):
                act.wait_ge(a_o, p * 2 + j + 1)
                act.activation(oT[:, j, :], ps[:, M0 + j, :], ACT.Copy).then_inc(a_oT, 1)

            def a_probsT_copy(p, j):
                act.wait_ge(a_pt_ps, p * 2 + j + 1)
                for m in range(j, 2):
                    act.activation(probsT[:, j, 4 * m:4 * m + 4, :].rearrange("p h k -> p (h k)"), ps[:, 4 + m, :],
                                   ACT.Copy).then_inc(a_pt_a, 1)

            def a_step(p, last):
                if not last:
                    a_query_copy(p * 2 + 2)
                a_probsT_copy(p, 0)
                if last:
                    act.wait_ge(a_v, NB)
                    for k in range(NT):
                        act.wait_ge(v1_ps, k + 1)
                        act.activation(v1[:, 4 * k:4 * k + 4, :], ps[:, 1 if k else M0, :].rearrange("p (b c) -> p b c", c=C),
                                       ACT.Copy).then_inc(v1_ok, 1)
                a_probsT_copy(p, 1)
                if not last:
                    a_exp_heads(p + 1, 0)
                a_oT_copy(p, 0)
                a_oT_copy(p, 1)
                if last:
                    ln_hi_copy(1, 0)
                else:
                    a_exp_heads(p + 1, 1)

            a_query_copy(0)
            act.wait_ge(k0_ps, NC0 + 1)
            act.activation(kT0[:, 0, TG:2 * TG], ps[:, 4, :], ACT.Copy).then_inc(k0_ok_a, 1)
            a_exp_heads(0, 0)
            a_exp_heads(0, 1)
            with act.Fori(0, NP - 1) as p:
                a_step(p, False)
            a_step(NP - 1, True)

            table(ACT.Silu)
            def b_silu_step(q):
                for c in range(NH):
                    v = q * NH + c
                    act.wait_ge(b_h, v + 1)
                    if not (isinstance(q, int) and q == 0):
                        act.wait_ge(b_u, v - 1)
                    act.activation(silu[:, c, :], ps[:, c, :], ACT.Silu).then_inc(b_silu, 1)

            def k1_signed(i, m):
                act.wait_ge(k1_ps, i * 2 + (m + 1))
                act.activation(part[:, m, :], ps[:, M0 + m, :], ACT.Copy, scale=sign[:, 1:2]).then_inc(k1_part, 1)

            def gate_copy(t):
                act.wait_ge(g_T, t + 1)
                act.activation(lgT[:, t * TG:(t + 1) * TG], ps[0:E, 5 - t, :], ACT.Copy).then_inc(g_lT, 1)

            b_silu_step(0)
            ln_hi_copy(1, 1)
            gate_copy(0)
            act.wait_ge(masks, 12)
            k1_signed(0, 0)
            gate_copy(1)
            b_silu_step(1)
            act.wait_ge(g_d, 1)
            act.activation(gw[:, 1, :], gd[:, :], ACT.Sigmoid).then_inc(g_w, 1)
            table(ACT.Silu)
            with act.Fori(0, NP - 1) as i:
                b_silu_step(i * 4 + 2)
                b_silu_step(i * 4 + 3)
                k1_signed(i, 1)
                b_silu_step(i * 4 + 4)
                b_silu_step(i * 4 + 5)
                k1_signed(i + 1, 0)
            b_silu_step(2 * E - 2)
            b_silu_step(2 * E - 1)
            table(ACT.Exp)

            def c_query_signed(n):
                act.wait_ge(c_q_ps, n + 1)
                if n >= 2:
                    act.wait_ge(c_q, n - 1)
                else:
                    act.wait_ge(k1_st, NK1 - 1 + n)
                act.activation(part[:, n % 2, :], ps[:, n if n < NG else M0 + 1, :], ACT.Copy,
                               scale=sign[:, 0:1]).then_inc(c_part, 1)

            ln_hi_copy(2, 0)
            k1_signed(NP - 1, 1)
            for n in range(NG):
                c_query_signed(n)
            def c_exp_unit(p, u):
                act.wait_ge(c_sub, p * 8 + (u + 1))
                act.activation(sh1[:, u % 4, :], sh1[:, u % 4, :], ACT.Exp, scale=D1 ** -0.5).then_inc(c_exp, 1)

            def c_turn_copy(p, u):
                act.wait_ge(c_pt_ps, p * 8 + (u + 1))
                act.activation(sh1T[:, u % 4, :], ps[:, 4 + u % 2, :], ACT.Copy).then_inc(c_pt, 1)

            def c_tail(b, j, stage):
                if stage == 0:
                    act.wait_ge(c_o, b * 4 + 4)
                    act.activation(ov[:, :], ps[:, M0 + j, 0:2 * P], ACT.Copy).then_inc(c_ov, 1)
                elif stage == 2:
                    act.wait_ge(c_oT_ps, b + 1)
                    act.activation(o1T[:, :], ps[:, M0 + j, 0:P], ACT.Copy).then_inc(c_oT, 1)

            def c_step(p, first, last):
                for u in range(8):
                    if u < 3 and not first:
                        c_tail(p * 2 - 1, 1, u)
                    if 4 <= u < 7:
                        c_tail(p * 2, 0, u - 4)
                    if not (last and u + 2 >= 8):
                        c_exp_unit(p, u + 2)
                    if not (last and u == 7):
                        c_turn_copy(p, u + 1)
                    if first and u < 4:
                        c_query_signed(NG + u)
                    if last and u == 4:
                        ln_hi_copy(3, 0)

            def d_evacuate(n):
                layer, t, m = D_ORDER[n]
                act.wait_ge(d_ps, n + 1)
                if n == 0:
                    act.wait_ge(masks, 3)
                act.activation(h_at[layer, t][:, 0, m, :], ps[:, D_BANK[n % ND], :], ACT.Relu,
                               scale=scale2[:, layer:layer + 1]).then_inc(d_hi, 1)
                if n % 2 == 0:
                    if n >= ND + 4:
                        m = n - ND
                        act.wait_ge(d_lo_p if m in D_POOL else d_lo, lo_count(m))
                    act.activation(relu[:, n % ND, :], ps[:, D_BANK[n % ND], :], ACT.Relu,
                                   scale=scale2[:, layer:layer + 1]).then_inc(d_relu_a, 1)

            c_exp_unit(0, 0)
            act.wait_ge(ln_nm, 1)
            for b in range(4, NB):
                act.activation(xn[:, b, :], x_sb[:, b, :], ACT.Identity, bias=nm[:, b:b + 1],
                               scale=rs[:, b:b + 1]).then_inc(ln_xn, 1)
            c_turn_copy(0, 0)
            ln_hi_copy(2, 1)
            c_exp_unit(0, 1)
            c_step(0, True, False)
            with act.Fori(1, NP - 1) as p:
                c_step(p, False, False)
            c_step(NP - 1, False, True)
            d_evacuate(0)
            c_tail(NB - 1, 1, 0)
            d_evacuate(1)
            d_evacuate(2)
            c_tail(NB - 1, 1, 2)

            for n in range(3, 16):
                d_evacuate(n)
                if n == 5:
                    ln_hi_copy(3, 1)
            for t in range(NT):
                act.wait_ge(d_ps, 16 + t + 1)
                act.activation(yT[:, t, :], ps[:, D_BANK[(16 + t) % ND], :], ACT.Copy, scale=scale[:, 2:3]).then_inc(d_yT, 1)

        @block.vector
        def _(dve):
            nwt = [0]

            def ln_stats(b):
                dve.bn_stats(stats[:, b:b + 1, :].rearrange("p o s -> p (o s)") if isinstance(b, int) else
                             stats[:, bass.ds(b, 1), :].rearrange("p o s -> p (o s)"),
                             x_sb[:, b, :] if isinstance(b, int) else
                             x_sb[:, bass.ds(b, 1), :].rearrange("p o c -> p (o c)")).then_inc(ln_st, 1)

            def newton(ins):
                nwt[0] += 1
                ins.then_inc(ln_nw, 1)
                dve.wait_ge(ln_nw, nwt[0])

            def ln_moments(s, t):
                for b in range(4 * t, 4 * t + 4):
                    dve.wait_ge(ln_st, NB * s + b + 1)
                    dve.bn_aggr(meanvar[:, b, :], stats[:, b, :]).then_inc(ln_mv, 1)

            def ln_guess(s, t):
                bs = slice(4 * t, 4 * t + 4)
                ln_moments(s, t)
                dve.wait_ge(ln_mv, NB * s + 4 * t + 4)
                newton(dve.tensor_scalar(ve[:, bs], meanvar[:, bs, 1], EPS, None, ALU.add))
                newton(dve.tensor_scalar(nt[:, bs].bitcast(I32), ve[:, bs].bitcast(I32), 1, None, ALU.logical_shift_right))
                ins = dve.tensor_scalar(rs[:, bs].bitcast(I32), nt[:, bs].bitcast(I32), -1.0, float(RSQRT_SEED), ALU.mult, ALU.add)
                return ins

            def ln_seed_pool(s, t):
                ln_guess(s, t).then_inc(ln_seed, 1)

            def ln_root(s, t):
                bs = slice(4 * t, 4 * t + 4)
                newton(ln_guess(s, t))
                newton(dve.tensor_tensor(nt[:, bs], rs[:, bs], rs[:, bs], ALU.mult))
                newton(dve.tensor_tensor(nu[:, bs], nt[:, bs], ve[:, bs], ALU.mult))
                newton(dve.scalar_tensor_tensor(nt[:, bs], nu[:, bs], -10.0 / 3, nu[:, bs], ALU.add, ALU.mult))
                newton(dve.scalar_tensor_tensor(rs[:, bs], nt[:, bs], 5.0, rs[:, bs], ALU.add, ALU.mult))
                newton(dve.tensor_tensor(nt[:, bs], rs[:, bs], rs[:, bs], ALU.mult))
                newton(dve.scalar_tensor_tensor(nu[:, bs], nt[:, bs], -0.5 * 0.375 ** 3, ve[:, bs], ALU.mult, ALU.mult))
                newton(dve.scalar_tensor_tensor(rs[:, bs], nu[:, bs], 1.5 * 0.375, rs[:, bs], ALU.add, ALU.mult))


            def ln_scale(t):
                for b in range(4 * t, 4 * t + 4):
                    dve.tensor_scalar(xn[:, b, :], x_sb[:, b, :], meanvar[:, b, 0:1], rs[:, b:b + 1],
                                      ALU.subtract, ALU.mult).then_inc(ln_xn, 1)

            def ln_low(s, t):
                dve.wait_ge(ln_hi, NT * s + t + 1)
                sl = slice(t * TG, (t + 1) * TG)
                dve.tensor_tensor(xT_lo[:, sl], ps[:, LN_BANK[s][t], :], f32(xT_hi[:, sl]), ALU.subtract).then_inc(ln_lo, 1)

            dve.wait_ge(ld_x, 16)
            for b in range(NB):
                ln_stats(b)
            ln_root(0, 0)
            ln_scale(0)
            for t in range(NT):
                dve.wait_ge(ctxT_h, t + 1)
                sl = slice(t * TG, (t + 1) * TG)
                dve.tensor_tensor(ctxT_lo[:, sl], ctxT[:, sl], f32(ctxT_hi[:, sl]), ALU.subtract).then_inc(ctxT_ok, 1)
            ln_root(0, 1)
            ln_scale(1)
            def k0_copy(t, k, bank):
                dve.wait_ge(k0_ps, NC0 * t + k + 1)
                dve.tensor_copy(kT0[:, k, t * TG:(t + 1) * TG], ps[:, bank, :]).then_inc(k0_ok_v, 1)

            ln_low(0, 0)
            k0_copy(0, 1, 1)
            k0_copy(0, 3, 3)

            def small_weights():
                dve.wait_ge(ld_d, 16 * 6)
                dve.tensor_tensor(d0_w[:, :], k0_u[:, 0, :], k0_u[:, 1, :], ALU.subtract).then_inc(d_w, 1)
                dve.tensor_scalar(scale2[:, :], scale[:, :], 2.0, None, ALU.mult).then_inc(masks, 1)
                dve.wait_ge(masks, 1)
                dve.tensor_scalar(scale2[:, 0:1], scale2[:, 0:1], 2.0, None, ALU.mult).then_inc(masks, 1)
                dve.wait_ge(ld_w0, 16 * 5)
                dve.tensor_copy(wg_hi[:, :], wg[:, :]).then_inc(masks, 1)
                dve.wait_ge(masks, 3)
                dve.tensor_tensor(wg_lo[:, :], wg[:, :], f32(wg_hi[:, :]), ALU.subtract).then_inc(masks, 1)

            def stack_masks():
                dve.wait_ge(const_ok, 4)
                dve.tensor_scalar(bit_i[:, 0:1], row_i[:, :], 4, 1, ALU.logical_shift_right, ALU.bitwise_and).then_inc(masks, 1)
                dve.tensor_scalar(bit_i[:, 1:2], row_i[:, :], 3, 1, ALU.logical_shift_right, ALU.bitwise_and).then_inc(masks, 1)
                dve.tensor_scalar(bit_i[:, 2:3], row_i[:, :], 0, 1, ALU.logical_shift_right, ALU.bitwise_and).then_inc(masks, 1)
                dve.wait_ge(masks, 7)
                dve.tensor_copy(is_lo[:, :], bit_i[:, :]).then_inc(masks, 1)
                dve.wait_ge(masks, 8)
                dve.tensor_scalar(sign[:, :], is_lo[:, :], -2.0, 1.0, ALU.mult, ALU.add).then_inc(masks, 1)
                dve.wait_ge(masks, 9)
                dve.wait_ge(ld_w1, 16 * 8)
                dve.tensor_scalar(bq1_r[:, :], bq1[:, :], sign[0:2, 2:3], None, ALU.mult).then_inc(masks, 1)
                dve.wait_ge(masks, 10)
                dve.scalar_tensor_tensor(bq1_p[:, :], bq1[:, :], is_lo[0:2, 2:3], f32(bq1_r[:, :]), ALU.mult, ALU.add).then_inc(masks, 1)
                dve.wait_ge(masks, 11)
                dve.tensor_copy(stacked(bq1_s), repeated(bq1_p)).then_inc(masks, 1)

            def a_query_copy(n):
                for m in range(2):
                    dve.wait_ge(a_q_ps, n + m + 1)
                    dve.tensor_scalar(q_ev[0:64, 2 * m:2 * m + 2, :],
                                      ps[0:64, M0 + m, :].rearrange("p (k t) -> p k t", k=2), D0 ** -0.5, None,
                                      ALU.mult).then_inc(a_qe, 1)

            def a_rowmax(p, j):
                dve.wait_ge(a_s, p * 2 + j + 1)
                dve.tensor_reduce(negmax[:, j, :], ps[:, 2 * j:2 * j + 2, :].rearrange("p a (h k) -> p (a h) k", k=P),
                                  X, ALU.max, negate=True).then_inc(a_max, 1)

            def a_probsT_copy(p):
                dve.wait_ge(a_pt_ps, p * 2 + 2)
                dve.tensor_copy(probsT[:, 1, 0:4, :].rearrange("p h k -> p (h k)"), ps[:, 4, :]).then_inc(a_pt_v, 1)

            def a_normalise(p, j):
                dve.wait_ge(a_exp, p * 2 + j + 1)
                dve.reciprocal(rsum[:, j, :], sums[:, j, :]).then_inc(a_rs, 1)
                dve.wait_ge(a_rs, p * 2 + j + 1)
                dve.tensor_tensor(probs[:, j, :, :], probs[:, j, :, :],
                                  rsum[:, j, :].unsqueeze(2).to_broadcast([P, H0, P]), ALU.mult).then_inc(a_norm, 1)

            def a_residual(p, j, last):
                dve.wait_ge(a_wo, p * 2 + j + 1)
                xs = x_sb[:, bass.ds(p * 2 + j, 1), :].rearrange("p o c -> p (o c)")
                dve.tensor_tensor(xs, ps[:, (M0 if last else 4) + j, 0:C], xs, ALU.add).then_inc(a_x, 1)

            def a_step(p, first, last):
                if not last:
                    a_query_copy(p * 2 + 2)
                if last:
                    ln_seed_pool(1, 0)
                a_normalise(p, 1)
                if not last:
                    a_rowmax(p + 1, 0)
                    a_probsT_copy(p)
                if first:
                    stack_masks()
                else:
                    for j in range(2):
                        dve.wait_ge(a_x, p * 2 + (j - 1))
                        ln_stats(p * 2 + (j - 2))
                if last:
                    a_probsT_copy(p)
                    dve.wait_ge(ln_rs, 1)
                    ln_scale(0)
                else:
                    a_rowmax(p + 1, 1)
                    a_normalise(p + 1, 0)
                a_residual(p, 0, last)
                if last:
                    ln_low(1, 0)
                a_residual(p, 1, last)

            a_query_copy(0)
            ln_low(0, 1)
            small_weights()
            a_rowmax(0, 0)
            k0_copy(1, 1, 5)
            a_rowmax(0, 1)
            k0_copy(1, 2, M0)
            k0_copy(1, 3, M0 + 1)
            a_normalise(0, 0)
            dve.wait_ge(xb0, NB)
            a_step(0, True, False)
            with dve.Fori(1, NP - 1) as p:
                a_step(p, False, False)
            a_step(NP - 1, False, True)
            for b in (NB - 2, NB - 1):
                dve.wait_ge(a_x, b + 1)
                ln_stats(b)

            ln_root(1, 1)
            ln_scale(1)
            ln_low(1, 1)

            def b_gate(q, slot):
                for c in range(NH):
                    v = q * NH + c
                    dve.wait_ge(b_silu, v + 1)
                    dve.wait_ge(b_g, v + 1)
                    dve.tensor_tensor(uT[:, slot, c, :], ps[:, 2 + c, :], silu[:, c, :], ALU.mult).then_inc(b_u, 1)

            def b_add(q, slot, e, t, before):
                dve.wait_ge(b_y, q + 1)
                dve.wait_ge(b_acc, before)
                for k in range(4):
                    b = 4 * t + k
                    ins = dve.scalar_tensor_tensor(x_sb[:, b, :], ps[:, 4 + slot, k * C:(k + 1) * C],
                                                   comb[:, bass.ds(e, 1), b:b + 1].rearrange("p o b -> p (o b)"),
                                                   x_sb[:, b, :], ALU.mult, ALU.add)
                ins.then_inc(b_acc, 1)

            def k1_stack(i, m):
                dve.wait_ge(k1_part, i * 2 + (m + 1))
                dve.scalar_tensor_tensor(k_st[:, 2 * m:2 * m + 2, bass.ds(i * 2 * P, 2 * P)],
                                         ps[:, M0 + m, :].rearrange("p (g n) -> p g n", g=2), is_lo[:, 1:2],
                                         f32(part[:, m, :]).rearrange("p (g n) -> p g n", g=2),
                                         ALU.mult, ALU.add).then_inc(k1_st, 1)

            b_gate(0, 0)
            k1_stack(0, 0)

            dve.wait_ge(g_ps, 1)
            dve.tensor_copy(lg[:, :, :].rearrange("p b e -> p (b e)"), ps[:, 5, 0:NB * E]).then_inc(g_lg, 1)
            dve.wait_ge(g_lg, 1)
            for b in range(NB):
                dve.max(top[:, b, :], lg[:, b, :]).then_inc(g_top, 1)
            for b in range(NB):
                dve.wait_ge(g_top, b + 1)
                dve.max_index(topi[:, b, :], top[:, b, :], lg[:, b, :]).then_inc(g_idx, 1)
            dve.wait_ge(g_top, NB)
            dve.tensor_tensor(gd[:, :], top[:, :, 1], top[:, :, 0], ALU.subtract).then_inc(g_d, 1)
            dve.wait_ge(g_idx, NB)
            dve.tensor_copy(topf[:, :, :], topi[:, :, :]).then_inc(g_f, 1)
            b_gate(1, 1)
            dve.wait_ge(g_w, 1)
            dve.tensor_scalar(gw[:, 0, :], gw[:, 1, :], -1.0, 1.0, ALU.mult, ALU.add).then_inc(g_w, 1)
            dve.wait_ge(g_f, 1)
            dve.wait_ge(g_w, 2)
            for k in range(2):
                dve.tensor_tensor(pick[:, k, :, :], iota_e[:, :, :], topf[:, :, k:k + 1].to_broadcast([P, NB, E]),
                                  ALU.is_equal).then_inc(g_pick, 1)
            for k in range(2):
                dve.wait_ge(g_pick, k + 1)
                dve.tensor_tensor(picked[:, k, :, :], pick[:, k, :, :], gw[:, k, :].unsqueeze(2).to_broadcast([P, NB, E]),
                                  ALU.mult).then_inc(g_sel, 1)
            dve.wait_ge(g_sel, 2)
            for t in range(NT):
                bs = slice(4 * t, 4 * t + 4)
                dve.tensor_tensor(comb[:, :, bs].rearrange("p e b -> p b e"), picked[:, 0, bs, :], picked[:, 1, bs, :],
                                  ALU.add).then_inc(b_acc, 1)

            with dve.Fori(0, NP - 1) as i:
                q, e = i * 4, i * 2
                b_add(q, 0, e, 0, q + 1)
                b_gate(q + 2, 0)
                b_add(q + 1, 1, e, 1, q + 2)
                b_gate(q + 3, 1)
                k1_stack(i, 1)
                b_add(q + 2, 0, e + 1, 0, q + 3)
                b_gate(q + 4, 0)
                b_add(q + 3, 1, e + 1, 1, q + 4)
                b_gate(q + 5, 1)
                k1_stack(i + 1, 0)
            q = 2 * E - 4
            b_add(q, 0, E - 2, 0, q + 1)
            b_gate(q + 2, 0)
            b_add(q + 1, 1, E - 2, 1, q + 2)
            b_add(q + 2, 0, E - 1, 0, q + 3)
            dve.wait_ge(b_acc, q + 5)
            for b in range(4):
                ln_stats(b)
            b_gate(q + 3, 1)
            ln_root(2, 0)
            ln_scale(0)
            b_add(q + 3, 1, E - 1, 1, q + 4)
            ln_low(2, 0)
            k1_stack(NP - 1, 1)
            dve.wait_ge(b_acc, q + 6)
            for b in range(4, NB):
                ln_stats(b)

            def c_query_stack(n):
                g, t = n % NG, n // NG
                dve.wait_ge(c_part, n + 1)
                dve.scalar_tensor_tensor(q_all[:, g, t * TG:(t + 1) * TG], ps[:, g if t == 0 else M0 + 1, :],
                                         is_lo[:, 0:1], f32(part[:, n % 2, :]), ALU.mult, ALU.add).then_inc(c_q, 1)
            ln_seed_pool(2, 1)

            def c_shift(p, u):
                n = p * 8 + u
                dve.wait_ge(c_s, n + 1)
                src = ps[:, u % 4, :].rearrange("p (h k) -> p h k", k=P)
                dve.tensor_reduce(negmax1[:, u % 4, :], src, X, ALU.max, negate=True).then_inc(c_max, 1)
                if not (isinstance(p, int) and n < 4):
                    dve.wait_ge(c_pt_ps, n - 3)
                dve.wait_ge(c_max, n + 1)
                dve.tensor_tensor(sh1[:, u % 4, :].rearrange("p (h k) -> p h k", k=P), src,
                                  negmax1[:, u % 4, :].unsqueeze(2).to_broadcast([P, 4, P]), ALU.add).then_inc(c_sub, 1)

            def c_tail(b, j, stage):
                if stage == 1:
                    dve.wait_ge(c_ovT, b + 1)
                    o = ps[:, M0 + j, 2 * P:4 * P].rearrange("p (a s h d) -> p a s h d", a=2, s=2, d=D1)
                    dve.reciprocal(rsum1[:, :].rearrange("p (a h) -> p a h", a=2), o[:, :, 1, :, 0]).then_inc(c_rs, 1)
                    dve.wait_ge(c_rs, b + 1)
                    dve.tensor_tensor(o1[:, :].rearrange("p (a h d) -> p a h d", a=2, d=D1), o[:, :, 0, :, :],
                                      rsum1[:, :].rearrange("p (a h) -> p a h", a=2).unsqueeze(3)
                                      .to_broadcast([P, 2, 8, D1]), ALU.mult).then_inc(c_norm, 1)
                elif stage == 3:
                    dve.wait_ge(c_wo, b + 1)
                    xs = x_sb[:, bass.ds(b, 1), :].rearrange("p o c -> p (o c)")
                    dve.tensor_tensor(xs, ps[:, M0 + j, P:P + C], xs, ALU.add).then_inc(c_x, 1)
                    dve.wait_ge(c_x, b + 1)
                    ln_stats(b)

            def c_step(p, first, last):
                for u in range(8):
                    if u < 4 and not first:
                        c_tail(p * 2 - 1, 1, u)
                    if u >= 4:
                        c_tail(p * 2, 0, u - 4)
                    if not (last and u + 3 >= 8):
                        c_shift(p, u + 3)
                    if first and u < 4:
                        c_query_stack(NG + u)
                    if last and u == 0:
                        ln_seed_pool(3, 0)
                    if last and u == 4:
                        ln_low(3, 0)

            for n in range(NG):
                if n == NG - 1:
                    c_shift(0, 0)
                c_query_stack(n)
            c_shift(0, 1)
            c_shift(0, 2)
            ln_low(2, 1)
            dve.wait_ge(xb1, NB)
            c_step(0, True, False)
            with dve.Fori(1, NP - 1) as p:
                c_step(p, False, False)
            c_step(NP - 1, False, True)
            def d_whole(n):
                dve.wait_ge(d_hi, n + 1)
                if n >= ND + 4:
                    dve.wait_ge(d_lo, lo_count(n - ND))
                layer = D_ORDER[n][0]
                dve.tensor_scalar(relu[:, n % ND, :], ps[:, D_BANK[n % ND], :], scale2[:, layer:layer + 1], 0.0,
                                  ALU.mult, ALU.max).then_inc(d_relu_v, 1)

            def d_low(n):
                layer, t, m = D_ORDER[n]
                h = h_at[layer, t]
                dve.wait_ge(d_hi, n + 1)
                dve.wait_ge(d_relu_a if n % 2 == 0 else d_relu_v, n // 2 + 1)
                dve.tensor_tensor(h[:, 1, m, :], relu[:, n % ND, :], f32(h[:, 0, m, :]), ALU.subtract).then_inc(d_lo, 1)

            c_tail(NB - 1, 1, 1)
            d_whole(1)
            d_low(1)
            c_tail(NB - 1, 1, 3)
            d_whole(3)
            d_low(3)
            ln_root(3, 1)
            ln_scale(1)
            for n in range(4, 16):
                if n % 2 == 1:
                    d_whole(n)
                if n == 5:
                    ln_low(3, 1)
                if n not in D_POOL:
                    d_low(n)
            for t in range(NT):
                dve.wait_ge(d_yT_ps, t + 1)
                dve.tensor_tensor(fin[:, t, :], ps[:, M0 + t, :],
                                  x_sb[:, 4 * t:4 * t + 4, :].rearrange("p b c -> p (b c)"), ALU.add).then_inc(d_x, 1)


_INS = ['x', 'ctx_768', 'L0_xattn_Wq', 'L0_xattn_Wk', 'L0_xattn_Wv', 'L0_xattn_Wo', 'L0_xattn_bo', 'L0_ffn_Wg',
        'L0_ffn_W1', 'L0_ffn_W2', 'L0_ffn_W3', 'L1_xattn_Wq', 'L1_xattn_bq', 'L1_xattn_Wk', 'L1_xattn_bk',
        'L1_xattn_Wv', 'L1_xattn_bv', 'L1_xattn_Wo', 'L1_xattn_bo', 'L1_ffn_k0', 'L1_ffn_k1', 'L1_ffn_k2',
        'L1_ffn_s0', 'L1_ffn_s1', 'L1_ffn_s2']


def kernel(**inputs):
    import numpy as _np
    import concourse.bacc as _bacc
    from concourse import mybir as _mybir
    from concourse.bass_utils import run_bass_kernel_spmd as _run

    nc = _bacc.Bacc("TRN2", target_bir_lowering=False, num_devices=1)
    arrays, args = {}, {}
    for name in _INS:
        v = _np.ascontiguousarray(inputs[name])
        if v.dtype == _np.bool_:
            v = v.view(_np.int32)
        v = v.reshape(v.shape or (1,))
        arrays[f"in_{name}"] = v
        args[name] = nc.dram_tensor(f"in_{name}", v.shape, _mybir.dt.from_np(v.dtype), kind="ExternalInput").ap()
    shape = inputs['x'].shape
    out = nc.dram_tensor("out_0", shape, _mybir.dt.float32, kind="ExternalOutput").ap()
    program(nc, args, out)
    r = _run(nc, [arrays], core_ids=[0])
    return r.results[0]["out_0"]
```
